# Optimizing a Trainium2 kernel written in Bass

```python
import numpy as np
import jax
import jax.numpy as jnp

def _softmax(x, axis=-1):
    return jax.nn.softmax(x, axis=axis)

def _gelu(x):
    return jax.nn.gelu(x, approximate=True)

def _silu(x):
    return jax.nn.silu(x)

def _sigmoid(x):
    return jax.nn.sigmoid(x)

def _layernorm(x, axis=-1, eps=1e-05):
    m = jnp.mean(x, axis=axis, keepdims=True)
    v = jnp.var(x, axis=axis, keepdims=True)
    return (x - m) / jnp.sqrt(v + eps)

def _scatter_add(tgt, idx, src, axis=0):
    return tgt.at[idx].add(src)

def _segment_sum(src, seg, n):
    return jax.ops.segment_sum(src, seg, n)
kernel_name = 'mk_decoder_preln_d2_seqx_r4_156be9'

def setup_inputs(seed: int=0):
    np.random.seed(seed)
    _w = jnp.asarray

    def _rec_inputs():
        import jax
        import jax.numpy as jnp
        _rk = jax.random.key(seed)
        x = 7.22e-05 + 1 * jax.random.normal(jax.random.fold_in(_rk, 1), (16, 128, 1024), jnp.float32)
        _lenS = 128 - jax.random.randint(jax.random.fold_in(_rk, 7), (16,), 0, max(1, 128 // 4) + 1, jnp.int32)
        _lenS2 = 128 - jax.random.randint(jax.random.fold_in(_rk, 8), (16,), 0, max(1, 128 // 4) + 1, jnp.int32)
        _ctx_4096P = jax.random.normal(jax.random.fold_in(_rk, 11), (16, 16, 1024), jnp.float32)
        _ctx_4096c = jax.random.dirichlet(jax.random.fold_in(_rk, 511), 0.3 * jnp.ones((16,), jnp.float32), (16, 128))
        _ctx_4096t = jnp.einsum('bsk,bkd->bsd', _ctx_4096c, _ctx_4096P)
        _ctx_4096t = _ctx_4096t * jax.lax.rsqrt(jnp.mean(jnp.square(_ctx_4096t)) + 1e-12) * 0.953939
        ctx_4096 = 4.13588e-05 + 0.999923 * (_ctx_4096t + 0.3 * jax.random.normal(jax.random.fold_in(_rk, 611), (16, 128, 1024), jnp.float32))
        return (x, ctx_4096)
    x, ctx_4096 = _rec_inputs()

    def _L0_attn_setup():
        import jax, jax.numpy as jnp
        import numpy as np
        H = 32
        HKV = 8
        D = 1024
        HD = D // H
        S = 256
        MASK_OUT = 0.9
        MIN_REMAIN = 128
        THETA = 10000.0

        def rope_tables(seq_len, hd):
            inv_freq = 1.0 / THETA ** (jnp.arange(0, hd, 2, dtype=jnp.float32) / hd)
            t = jnp.arange(seq_len, dtype=jnp.float32)
            freqs = jnp.outer(t, inv_freq)
            emb = jnp.concatenate([freqs, freqs], axis=-1)
            return (jnp.cos(emb), jnp.sin(emb))

        def rotate_half(x):
            x1, x2 = jnp.split(x, 2, axis=-1)
            return jnp.concatenate([-x2, x1], axis=-1)

        def apply_rope(x, cos, sin):
            return x * cos + rotate_half(x) * sin
        key = jax.random.key(seed)
        k0, k1, k2, k3, k4 = jax.random.split(key, 5)
        hidden_states = jax.random.normal(k0, (1, S, D), jnp.float32)
        Wq = jax.random.normal(k1, (D, D), jnp.float32) * 0.02
        Wk = jax.random.normal(k2, (HKV * HD, D), jnp.float32) * 0.02
        Wv = jax.random.normal(k3, (HKV * HD, D), jnp.float32) * 0.02
        Wo = jax.random.normal(k4, (D, D), jnp.float32) * 0.02
        return {'hidden_states': hidden_states, 'Wq': Wq, 'Wk': Wk, 'Wv': Wv, 'Wo': Wo}
    _L0_attn_all = _L0_attn_setup()
    _L0_attn_in = {k: v for k, v in _L0_attn_all.items() if k in ('Wq', 'Wk', 'Wv', 'Wo')}
    del _L0_attn_all

    def _L0_xattn_setup():
        import jax, jax.numpy as jnp
        import numpy as np
        HEADS = 8
        WINDOW = 16

        def _pointwise(W, b, t):
            return jnp.einsum('oc,bct->bot', W, t) + b[None, :, None]
        key = jax.random.key(seed)
        ks = jax.random.split(key, 10)
        B, C, T = (4, 128, 1024)
        s = 0.02
        return {'x': jax.random.normal(ks[0], (B, C, T), jnp.float32), 'cond': jax.random.normal(ks[1], (B, C, T), jnp.float32), 'Wq': jax.random.normal(ks[2], (C, C), jnp.float32) * s, 'bq': jnp.zeros((C,), jnp.float32), 'Wk': jax.random.normal(ks[3], (C, C), jnp.float32) * s, 'bk': jnp.zeros((C,), jnp.float32), 'Wv': jax.random.normal(ks[4], (C, C), jnp.float32) * s, 'bv': jnp.zeros((C,), jnp.float32), 'Wo': jax.random.normal(ks[5], (C, C), jnp.float32) * s, 'bo': jnp.zeros((C,), jnp.float32)}
    _L0_xattn_all = _L0_xattn_setup()
    _L0_xattn_in = {k: v for k, v in _L0_xattn_all.items() if k in ('Wq', 'bq', 'Wk', 'bk', 'Wv', 'bv', 'Wo', 'bo')}
    del _L0_xattn_all

    def _L0_ffn_setup():
        import jax, jax.numpy as jnp
        import numpy as np
        BATCH, SEQ, D = (2, 512, 1024)
        K, TOPK, RANK = (64, 16, 16)
        ALPHA = 32.0
        SCALING = ALPHA / RANK
        key = jax.random.key(seed)
        k1, k2, k3, k4 = jax.random.split(key, 4)
        x = jax.random.normal(k1, (BATCH, SEQ, D), dtype=jnp.float32)
        A = jax.random.normal(k2, (K, RANK, D), dtype=jnp.float32) * 0.02
        B = jax.random.normal(k3, (K, D, RANK), dtype=jnp.float32) * 0.02
        Wr = jax.random.normal(k4, (K, D), dtype=jnp.float32) * 0.02
        return {'x': x, 'A': A, 'B': B, 'Wr': Wr}
    _L0_ffn_all = _L0_ffn_setup()
    _L0_ffn_in = {k: v for k, v in _L0_ffn_all.items() if k in ('A', 'B', 'Wr')}
    del _L0_ffn_all

    def _L1_attn_setup():
        import jax, jax.numpy as jnp
        import numpy as np
        K_FACTOR = 0.5
        key = jax.random.key(seed)
        k1, k2, k3, k4 = jax.random.split(key, 4)
        B, S, H, I = (1, 512, 1024, 2752)
        x = jax.random.normal(k1, (B, S, H), dtype=jnp.float32)
        w_gate = jax.random.normal(k2, (I, H), dtype=jnp.float32) * 0.02
        w_up = jax.random.normal(k3, (I, H), dtype=jnp.float32) * 0.02
        w_down = jax.random.normal(k4, (H, I), dtype=jnp.float32) * 0.02
        return {'x': x, 'w_gate': w_gate, 'w_up': w_up, 'w_down': w_down}
    _L1_attn_all = _L1_attn_setup()
    _L1_attn_in = {k: v for k, v in _L1_attn_all.items() if k in ('w_gate', 'w_up', 'w_down')}
    del _L1_attn_all

    def _L1_xattn_setup():
        import jax, jax.numpy as jnp
        import numpy as np
        H = 8
        C = 2

        def _autocorrelation(Q, K, V):
            B, L, D = Q.shape
            d = D // H
            q = Q.reshape(B, L, H, d).transpose(0, 2, 1, 3)
            k = K.reshape(B, L, H, d).transpose(0, 2, 1, 3)
            v = V.reshape(B, L, H, d).transpose(0, 2, 1, 3)
            qf = jnp.fft.fft(q, axis=2)
            kf = jnp.fft.fft(k, axis=2)
            corr = jnp.fft.ifft(qf * jnp.conj(kf), axis=2).real
            topk = int(C * np.log(L))
            w, idx = jax.lax.top_k(corr.transpose(0, 1, 3, 2), topk)
            w = jax.nn.softmax(w, axis=-1)
            pos = jnp.arange(L)[:, None]
            out = jnp.zeros_like(v)
            for i in range(topk):
                g = jnp.minimum(idx[:, :, None, :, i] + pos, L - 1)
                out = out + w[:, :, None, :, i] * jnp.take_along_axis(v, g, axis=2)
            return out.transpose(0, 2, 1, 3).reshape(B, L, D)
        key = jax.random.key(seed)
        k1, k2, k3 = jax.random.split(key, 3)
        B, L, D = (16, 128, 1024)
        Q = jax.random.normal(k1, (B, L, D), dtype=jnp.float32)
        K = jax.random.normal(k2, (B, L, D), dtype=jnp.float32)
        V = jax.random.normal(k3, (B, L, D), dtype=jnp.float32)
        return {'Q': Q, 'K': K, 'V': V}
    _L1_xattn_all = _L1_xattn_setup()
    _L1_xattn_in = {k: v for k, v in _L1_xattn_all.items() if k in ()}
    del _L1_xattn_all

    def _L1_ffn_setup():
        import jax, jax.numpy as jnp
        import numpy as np

        def sparsemax(z):
            E = z.shape[-1]
            z_sorted = -jnp.sort(-z, axis=-1)
            z_cum = jnp.cumsum(z_sorted, axis=-1)
            k = jnp.arange(1, E + 1, dtype=z.dtype)
            support = 1.0 + k * z_sorted > z_cum
            k_z = jnp.sum(support, axis=-1, keepdims=True)
            tau_sum = jnp.take_along_axis(z_cum, k_z.astype(jnp.int32) - 1, axis=-1)
            tau = (tau_sum - 1.0) / k_z.astype(z.dtype)
            return jnp.maximum(z - tau, 0.0)
        key = jax.random.key(seed)
        ks = jax.random.split(key, 6)
        B, S, D_IN, D_OUT, E, R = (8, 512, 1024, 1024, 8, 16)
        x = jax.random.normal(ks[0], (B, S, D_IN), dtype=jnp.float32)
        W_base = jax.random.normal(ks[1], (D_OUT, D_IN), dtype=jnp.float32) * D_IN ** (-0.5)
        b_base = jax.random.normal(ks[2], (D_OUT,), dtype=jnp.float32) * 0.01
        W_router = jax.random.normal(ks[3], (E, D_IN), dtype=jnp.float32) * D_IN ** (-0.5)
        b_router = jnp.zeros((E,), dtype=jnp.float32)
        lora_A = jax.random.normal(ks[4], (E, D_IN, R), dtype=jnp.float32) * D_IN ** (-0.5)
        lora_B = jnp.zeros((E, R, D_OUT), dtype=jnp.float32)
        return {'x': x, 'W_base': W_base, 'b_base': b_base, 'W_router': W_router, 'b_router': b_router, 'lora_A': lora_A, 'lora_B': lora_B}
    _L1_ffn_all = _L1_ffn_setup()
    _L1_ffn_in = {k: v for k, v in _L1_ffn_all.items() if k in ('W_base', 'b_base', 'W_router', 'b_router', 'lora_A', 'lora_B')}
    del _L1_ffn_all
    return {'x': x, 'ctx_4096': ctx_4096, 'L0_attn_Wq': _L0_attn_in['Wq'], 'L0_attn_Wk': _L0_attn_in['Wk'], 'L0_attn_Wv': _L0_attn_in['Wv'], 'L0_attn_Wo': _L0_attn_in['Wo'], 'L0_xattn_Wq': _L0_xattn_in['Wq'], 'L0_xattn_bq': _L0_xattn_in['bq'], 'L0_xattn_Wk': _L0_xattn_in['Wk'], 'L0_xattn_bk': _L0_xattn_in['bk'], 'L0_xattn_Wv': _L0_xattn_in['Wv'], 'L0_xattn_bv': _L0_xattn_in['bv'], 'L0_xattn_Wo': _L0_xattn_in['Wo'], 'L0_xattn_bo': _L0_xattn_in['bo'], 'L0_ffn_A': _L0_ffn_in['A'], 'L0_ffn_B': _L0_ffn_in['B'], 'L0_ffn_Wr': _L0_ffn_in['Wr'], 'L1_attn_w_gate': _L1_attn_in['w_gate'], 'L1_attn_w_up': _L1_attn_in['w_up'], 'L1_attn_w_down': _L1_attn_in['w_down'], 'L1_ffn_W_base': _L1_ffn_in['W_base'], 'L1_ffn_b_base': _L1_ffn_in['b_base'], 'L1_ffn_W_router': _L1_ffn_in['W_router'], 'L1_ffn_b_router': _L1_ffn_in['b_router'], 'L1_ffn_lora_A': _L1_ffn_in['lora_A'], 'L1_ffn_lora_B': _L1_ffn_in['lora_B']}

def reference(x, ctx_4096, L0_attn_Wq, L0_attn_Wk, L0_attn_Wv, L0_attn_Wo, L0_xattn_Wq, L0_xattn_bq, L0_xattn_Wk, L0_xattn_bk, L0_xattn_Wv, L0_xattn_bv, L0_xattn_Wo, L0_xattn_bo, L0_ffn_A, L0_ffn_B, L0_ffn_Wr, L1_attn_w_gate, L1_attn_w_up, L1_attn_w_down, L1_ffn_W_base, L1_ffn_b_base, L1_ffn_W_router, L1_ffn_b_router, L1_ffn_lora_A, L1_ffn_lora_B):
    import jax
    import jax.numpy as jnp

    def _L0_attn_ref(hidden_states, Wq, Wk, Wv, Wo):
        import jax, jax.numpy as jnp
        import numpy as np
        H = 32
        HKV = 8
        D = 1024
        HD = D // H
        S = 256
        MASK_OUT = 0.9
        MIN_REMAIN = 128
        THETA = 10000.0

        def rope_tables(seq_len, hd):
            inv_freq = 1.0 / THETA ** (jnp.arange(0, hd, 2, dtype=jnp.float32) / hd)
            t = jnp.arange(seq_len, dtype=jnp.float32)
            freqs = jnp.outer(t, inv_freq)
            emb = jnp.concatenate([freqs, freqs], axis=-1)
            return (jnp.cos(emb), jnp.sin(emb))

        def rotate_half(x):
            x1, x2 = jnp.split(x, 2, axis=-1)
            return jnp.concatenate([-x2, x1], axis=-1)

        def apply_rope(x, cos, sin):
            return x * cos + rotate_half(x) * sin
        B, Sq, Dm = hidden_states.shape
        dtype = hidden_states.dtype
        neg = jnp.finfo(dtype).min
        q = (hidden_states @ Wq.T).reshape(B, Sq, H, HD).transpose(0, 2, 1, 3)
        k = (hidden_states @ Wk.T).reshape(B, Sq, HKV, HD).transpose(0, 2, 1, 3)
        v = (hidden_states @ Wv.T).reshape(B, Sq, HKV, HD).transpose(0, 2, 1, 3)
        rep = H // HKV
        k = jnp.repeat(k, rep, axis=1)
        v = jnp.repeat(v, rep, axis=1)
        cos, sin = rope_tables(Sq, HD)
        qr = apply_rope(q, cos, sin)
        kr = apply_rope(k, cos, sin)
        draft = jnp.einsum('bhqd,bhkd->bhqk', qr, kr)
        qi = jnp.arange(Sq)
        ki = jnp.arange(Sq)
        causal_future = qi[:, None] < ki[None, :]
        draft = draft + jnp.where(causal_future, neg, jnp.asarray(0.0, dtype))
        num_remain = max(min(Sq, MIN_REMAIN), Sq - int(Sq * MASK_OUT))
        _, draft_indices = jax.lax.top_k(draft, num_remain)
        mask = jnp.full((B, H, Sq, Sq), neg, dtype)
        b_idx = jnp.arange(B)[:, None, None, None]
        h_idx = jnp.arange(H)[None, :, None, None]
        s_idx = jnp.arange(Sq)[None, None, :, None]
        mask = mask.at[b_idx, h_idx, s_idx, draft_indices].set(0.0)
        mask = jnp.where(causal_future[None, None, :, :], neg, mask)
        scores = jnp.einsum('bhqd,bhkd->bhqk', qr, kr) / np.sqrt(HD).astype(np.float32) + mask
        attn = jax.nn.softmax(scores, axis=-1)
        out = jnp.einsum('bhqk,bhkd->bhqd', attn, v)
        out = out.transpose(0, 2, 1, 3).reshape(B, Sq, Dm)
        return out @ Wo.T

    def _L0_xattn_ref(x, cond, Wq, bq, Wk, bk, Wv, bv, Wo, bo):
        import jax, jax.numpy as jnp
        import numpy as np
        HEADS = 8
        WINDOW = 16

        def _pointwise(W, b, t):
            return jnp.einsum('oc,bct->bot', W, t) + b[None, :, None]
        B, C, T = x.shape
        H, W = (HEADS, WINDOW)
        hd = C // H
        scale = hd ** (-0.5)
        pad_left = W // 2
        pad_right = W - pad_left - 1
        q = _pointwise(Wq, bq, x)
        k = _pointwise(Wk, bk, cond)
        v = _pointwise(Wv, bv, cond)
        k = jnp.pad(k, ((0, 0), (0, 0), (pad_left, pad_right)))
        v = jnp.pad(v, ((0, 0), (0, 0), (pad_left, pad_right)))
        idx = jnp.arange(T)[:, None] + jnp.arange(W)[None, :]
        k_win = k[:, :, idx].reshape(B, H, hd, T, W)
        v_win = v[:, :, idx].reshape(B, H, hd, T, W)
        qh = q.reshape(B, H, hd, T)
        dots = jnp.einsum('bhdt,bhdtw->bhtw', qh, k_win) * scale
        attn = jax.nn.softmax(dots, axis=-1)
        out = jnp.einsum('bhtw,bhdtw->bhdt', attn, v_win)
        out = out.reshape(B, C, T)
        return _pointwise(Wo, bo, out)

    def _L0_ffn_ref(x, A, B, Wr):
        import jax, jax.numpy as jnp
        import numpy as np
        BATCH, SEQ, D = (2, 512, 1024)
        K, TOPK, RANK = (64, 16, 16)
        ALPHA = 32.0
        SCALING = ALPHA / RANK
        prefix = x.shape[:-1]
        xf = x.reshape(-1, x.shape[-1])
        N = xf.shape[0]
        scores = xf @ Wr.T
        top_vals, top_idx = jax.lax.top_k(scores, TOPK)
        gates = jax.nn.softmax(top_vals, axis=-1)
        G = jnp.zeros((N, K), xf.dtype).at[jnp.arange(N)[:, None], top_idx].set(gates)
        h = jnp.einsum('nd,krd->nkr', xf, A)
        out = jnp.einsum('nkr,kdr->nd', h * G[:, :, None], B)
        return (out * SCALING).reshape(*prefix, -1)

    def _L1_attn_ref(x, w_gate, w_up, w_down):
        import jax, jax.numpy as jnp
        import numpy as np
        K_FACTOR = 0.5
        s = jax.nn.silu(jnp.einsum('bsh,ih->bsi', x, w_gate))
        B, S, I = s.shape
        k = int(K_FACTOR * I)
        _, idx = jax.lax.top_k(-jnp.abs(s), k)
        flat = s.reshape(B * S, I)
        rows = jnp.arange(B * S)[:, None]
        flat = flat.at[rows, idx.reshape(B * S, k)].set(0.0)
        s = flat.reshape(B, S, I)
        s = s * jnp.einsum('bsh,ih->bsi', x, w_up)
        return jnp.einsum('bsi,hi->bsh', s, w_down)

    def _L1_xattn_ref(Q, K, V):
        import jax, jax.numpy as jnp
        import numpy as np
        H = 8
        C = 2

        def _autocorrelation(Q, K, V):
            B, L, D = Q.shape
            d = D // H
            q = Q.reshape(B, L, H, d).transpose(0, 2, 1, 3)
            k = K.reshape(B, L, H, d).transpose(0, 2, 1, 3)
            v = V.reshape(B, L, H, d).transpose(0, 2, 1, 3)
            qf = jnp.fft.fft(q, axis=2)
            kf = jnp.fft.fft(k, axis=2)
            corr = jnp.fft.ifft(qf * jnp.conj(kf), axis=2).real
            topk = int(C * np.log(L))
            w, idx = jax.lax.top_k(corr.transpose(0, 1, 3, 2), topk)
            w = jax.nn.softmax(w, axis=-1)
            pos = jnp.arange(L)[:, None]
            out = jnp.zeros_like(v)
            for i in range(topk):
                g = jnp.minimum(idx[:, :, None, :, i] + pos, L - 1)
                out = out + w[:, :, None, :, i] * jnp.take_along_axis(v, g, axis=2)
            return out.transpose(0, 2, 1, 3).reshape(B, L, D)
        return _autocorrelation(Q, K, V)

    def _L1_ffn_ref(x, W_base, b_base, W_router, b_router, lora_A, lora_B):
        import jax, jax.numpy as jnp
        import numpy as np

        def sparsemax(z):
            E = z.shape[-1]
            z_sorted = -jnp.sort(-z, axis=-1)
            z_cum = jnp.cumsum(z_sorted, axis=-1)
            k = jnp.arange(1, E + 1, dtype=z.dtype)
            support = 1.0 + k * z_sorted > z_cum
            k_z = jnp.sum(support, axis=-1, keepdims=True)
            tau_sum = jnp.take_along_axis(z_cum, k_z.astype(jnp.int32) - 1, axis=-1)
            tau = (tau_sum - 1.0) / k_z.astype(z.dtype)
            return jnp.maximum(z - tau, 0.0)
        base_out = jnp.einsum('bsd,od->bso', x, W_base) + b_base
        logits = jnp.einsum('bsd,ed->bse', x, W_router) + b_router
        weights = sparsemax(logits)
        h = jnp.einsum('bsd,edr->bser', x, lora_A)
        expert_out = jnp.einsum('bser,bse,ero->bso', h, weights, lora_B)
        return base_out + expert_out
    x = x + _L0_attn_ref(_layernorm(x, axis=-1), L0_attn_Wq, L0_attn_Wk, L0_attn_Wv, L0_attn_Wo)
    x = x + _L0_xattn_ref(_layernorm(x, axis=-1), ctx_4096, L0_xattn_Wq, L0_xattn_bq, L0_xattn_Wk, L0_xattn_bk, L0_xattn_Wv, L0_xattn_bv, L0_xattn_Wo, L0_xattn_bo)
    x = x + _L0_ffn_ref(_layernorm(x, axis=-1), L0_ffn_A, L0_ffn_B, L0_ffn_Wr)
    x = x + _L1_attn_ref(_layernorm(x, axis=-1), L1_attn_w_gate, L1_attn_w_up, L1_attn_w_down)
    x = x + _L1_xattn_ref(_layernorm(x, axis=-1), ctx_4096, ctx_4096)
    x = x + _L1_ffn_ref(_layernorm(x, axis=-1), L1_ffn_W_base, L1_ffn_b_base, L1_ffn_W_router, L1_ffn_b_router, L1_ffn_lora_A, L1_ffn_lora_B)
    return x

_drawn_inputs = setup_inputs


def setup_inputs(seed=0):
    import zlib

    import numpy as np

    out = dict(_drawn_inputs(seed))
    spreads = {'L0_xattn_bq': (0.0, 0.8),
     'L0_xattn_bk': (0.0, 0.8),
     'L0_xattn_bv': (0.0, 0.622),
     'L0_xattn_bo': (0.0, 0.1),
     'L1_ffn_b_router': (0.0, 0.301),
     'L1_ffn_lora_B': (0.0, 0.1)}
    factors = {'L0_xattn_Wq': 8.0, 'L0_xattn_Wk': 8.0, 'L1_ffn_b_base': 8.0}
    for name, (base, spread) in spreads.items():
        noise = np.random.default_rng([zlib.crc32(name.encode()), seed]).standard_normal(out[name].shape)
        drawn = base * np.exp(spread * noise) if base else spread * noise
        out[name] = jnp.asarray(drawn.astype(out[name].dtype))
    for name, factor in factors.items():
        out[name] = (out[name] * factor).astype(out[name].dtype)
    return out
```

```python
from contextlib import ExitStack

import concourse.bass as bass
from concourse import mybir

ALU = mybir.AluOpType
ACT = mybir.ActivationFunctionType
F32 = mybir.dt.float32
BF16 = mybir.dt.bfloat16
U16 = mybir.dt.uint16
U32 = mybir.dt.uint32
AX = mybir.AxisListType

P = 128
BATCHES = 16
D = 1024
DC = D // P
PAIRS = BATCHES // 2
BANK = 512
EPS = 1e-5
MASKED = -1e30


class Slot:

    def __init__(self, sem, name, uses=1, unit=1):
        self.full = sem(name + "_full")
        self.free = sem(name + "_free")
        self.uses = uses
        self.unit = unit

    def turn(self, it, k=0):
        return (it * self.uses + (k + 1)) * self.unit


class Plan:

    def __init__(self, banks):
        self.uses = [0] * banks
        self.table = {}

    def add(self, key, *banks):
        self.table[key] = [(b, self.take(b)) for b in banks]

    def take(self, b):
        self.uses[b] += 1
        return self.uses[b] - 1

    def of(self, *key):
        return self.table[key]


def makers(ctx, nc, prefix):
    ctx.sems = []

    def sb(name, shape, dt=F32):
        return ctx.enter_context(nc.sbuf_tensor(prefix + name, shape, dt))

    def sem(name):
        s = ctx.enter_context(nc.semaphore(prefix + name))
        ctx.sems.append(s)
        return s

    def slots(name, uses=1, unit=1, n=2):
        return [Slot(sem, f"{name}{i}", uses, unit) for i in range(n)]

    return sb, sem, slots


def open_slots(engine, slots):
    for s in slots:
        engine.nop().then_inc(s.free, s.unit)


def norm_stats(nc, v, x, st, var_ready):
    nc.vector.bn_stats(st[:, 0:6], x[:, 0:BANK])
    nc.vector.bn_stats(st[:, 6:12], x[:, BANK:D])
    v.drain()
    nc.vector.bn_aggr(st[:, 12:14], st[:, 0:12])
    v.drain()
    nc.vector.tensor_scalar(st[:, 14:15], st[:, 13:14], EPS, None, ALU.add).then_inc(var_ready, 1)


def norm_apply(nc, out, x, st):
    return nc.vector.tensor_scalar(out, x, st[:, 12:13], st[:, 15:16], ALU.subtract, ALU.mult)


def norm_power(nc, st, nhalf):
    return nc.gpsimd.tensor_tensor(st[:, 15:16], st[:, 14:15], nhalf, ALU.pow)


def rows(x_dram, it, p):
    return x_dram[bass.ds(it * (2 * P) + p * P, P), :]


class Norm:

    def __init__(self, nc, sb, sem, slots, x_in):
        self.nc, self.x_in = nc, x_in
        self.xn = sb("xn", [P, 2, D])
        self.st = sb("st", [P, 2, 16])
        self.nhalf = sb("nhalf", [P, 1])
        self.landed = slots("xn", unit=16)
        self.var_ready = [sem(f"var_ready{p}") for p in range(2)]
        self.rstd_ready = [sem(f"rstd_ready{p}") for p in range(2)]
        self.ready = [sem(f"xn_ready{p}") for p in range(2)]

    def load(self, sp, it):
        for p in range(2):
            sp.wait_ge(self.landed[p].free, self.landed[p].turn(it))
            sp.dma_start(self.xn[:, p, :], rows(self.x_in, it, p)).then_inc(self.landed[p].full, 16)

    def vector(self, v, it):
        for p in range(2):
            v.wait_ge(self.landed[p].full, self.landed[p].turn(it))
            norm_stats(self.nc, v, self.xn[:, p, :], self.st[:, p, :], self.var_ready[p])
        for p in range(2):
            v.wait_ge(self.rstd_ready[p], it + 1)
            norm_apply(self.nc, self.xn[:, p, :], self.xn[:, p, :], self.st[:, p, :]).then_inc(self.ready[p], 1)

    def pool(self, pool, it):
        for p in range(2):
            pool.wait_ge(self.var_ready[p], it + 1)
            norm_power(self.nc, self.st[:, p, :], self.nhalf[:, :]).then_inc(self.rstd_ready[p], 1)


def each_step(engine, body):
    with engine.Fori(0, PAIRS - 1) as it:
        body(it, True)
    body(PAIRS - 1, False)


def copy_banks(nc, act, banks, bank, it, PS, out, chunks):
    n = out.shape[1]
    for i, (b, k) in enumerate(banks):
        act.wait_ge(bank[b].full, bank[b].turn(it, k))
        m = min(chunks, n - i * chunks)
        nc.scalar.activation(out[:, i * chunks:i * chunks + m, :],
                             PS[:, b, 0:m * out.shape[2]].rearrange("p (c t) -> p c t", c=m),
                             ACT.Copy).then_inc(bank[b].free, 1)


def transpose_chunks(nc, pe, banks, bank, it, PS, src, ident, n):
    for i, (b, k) in enumerate(banks):
        pe.wait_ge(bank[b].free, bank[b].turn(it, k))
        for c in range(4 * i, min(4 * i + 4, n)):
            last = nc.tensor.transpose(PS[:, b, (c % 4) * P:(c % 4 + 1) * P], src[:, c * P:(c + 1) * P], ident[:, :])
        if i < len(banks) - 1:
            last.then_inc(bank[b].full, 1)
        else:
            pe.drain().then_inc(bank[b].full, 1)
    return pe.drain()


def clear(nc, ctx):
    for s in ctx.sems:
        nc.sync.sem_clear(s)
    nc.all_engine_barrier()



HEADS, KV_HEADS, HD = 32, 8, 32
REP = HEADS // KV_HEADS
QK = D + KV_HEADS * HD
QKV = D + 2 * KV_HEADS * HD


def self_attention(nc, x_in, x_out, w_qkv, w_o, cos_sin, causal, eye):
    with ExitStack() as ctx:
        sb, sem, slots = makers(ctx, nc, "a_")
        PS = ctx.enter_context(nc.psum_tensor("a_ps", [P, 8, BANK], F32))
        wqkv = sb("wqkv", [P, DC, QKV])
        wo = sb("wo", [P, DC, D])
        cs = sb("cs", [P, 2, HD])
        ident = sb("ident", [P, P])
        mask = sb("mask", [P, P])
        ident16 = sb("ident16", [P, P], BF16)
        mask16 = sb("mask16", [P, P], BF16)
        nhalf = sb("nhalf", [P, 1])
        xt = sb("xt", [P, 2, D])
        xn = sb("xn", [P, 2, D])
        st = sb("st", [P, 2, 16])
        xT = sb("xT", [P, 2, DC, P])
        qk = sb("qk", [P, 2, QK])
        rot = sb("rot", [P, QK])
        vs = sb("vs", [P, 2, KV_HEADS * HD])
        qkT = sb("qkT", [P, 2, QK // P, P])
        nmax = sb("nmax", [P, 3, REP])
        probs = sb("probs", [P, 2, REP, P])
        probsT = sb("probsT", [P, 2, REP, P])
        rsum = sb("rsum", [P, 2, HEADS])
        rinv = sb("rinv", [P, 2, HEADS])
        o = sb("o", [P, 2, D])

        loaded = sem("loaded")
        made = sem("made")
        x_tile = slots("x", unit=16)
        var_ready = [sem(f"var_ready{p}") for p in range(2)]
        rstd_ready = [sem(f"rstd_ready{p}") for p in range(2)]
        xn_s = slots("xn")
        xT_s = slots("xT", uses=2)
        qk_s = slots("qk")
        qkT_s = slots("qkT")
        vs_ready = sem("vs_ready")
        max_ready = sem("max_ready")
        probs_s = slots("probs", uses=KV_HEADS)
        probsT_s = slots("probsT", uses=KV_HEADS)
        o_s = slots("o")
        sum_ready = sem("sum_ready")
        y_ready = [sem(f"y_ready{p}") for p in range(2)]

        plan = Plan(8)
        for p in range(2):
            plan.add(("xT", p), 6, 7)
        for p in range(2):
            plan.add(("qkv", p), 3 * p, 3 * p + 1, 3 * p + 2)
        for p in range(2):
            plan.add(("qkT", p), 3 * p, 3 * p + 1, 3 * p + 2)
        for p in range(2):
            for g in range(KV_HEADS + 2):
                if g < KV_HEADS:
                    plan.add(("scores", p, g), g % 3)
                if 0 <= g - 1 < KV_HEADS:
                    plan.add(("probsT", p, g - 1), 3 + (g - 1) % 2)
                if 0 <= g - 2 < KV_HEADS and (g - 2) % 4 == 0:
                    plan.add(("o", p, (g - 2) // 4), 6 + (g - 2) // 4)
        plan.add(("oT", 0), 3, 4)
        plan.add(("oT", 1), 0, 1)
        plan.add(("y", 0), 6, 7)
        plan.add(("y", 1), 3, 4)
        bank = [Slot(sem, f"bank{b}", plan.uses[b]) for b in range(8)]
        LOADS = 16 * 9

        with nc.Block() as block:

            @block.sync
            def _(sp):
                sp.dma_start(ident[:, :], eye).then_inc(loaded, 16)
                sp.dma_start(cs[:, :, :], cos_sin).then_inc(loaded, 16)
                sp.dma_start(mask[:, :], causal).then_inc(loaded, 16)
                wq_rows = w_qkv.rearrange("(c p) n -> p c n", p=P)
                wo_rows = w_o.rearrange("(c p) n -> p c n", p=P)
                for c in range(0, DC, 2):
                    sp.dma_start(wqkv[:, c:c + 2, :], wq_rows[:, c:c + 2, :]).then_inc(loaded, 16)
                for c in range(0, DC, 4):
                    sp.dma_start(wo[:, c:c + 4, :], wo_rows[:, c:c + 4, :]).then_inc(loaded, 16)
                open_slots(sp, x_tile)
                with sp.Fori(0, PAIRS) as it:
                    for p in range(2):
                        sp.wait_ge(x_tile[p].free, x_tile[p].turn(it))
                        sp.dma_start(xt[:, p, :], rows(x_in, it, p)).then_inc(x_tile[p].full, 16)
                    for p in range(2):
                        sp.wait_ge(y_ready[p], it + 1)
                        sp.dma_start(rows(x_out, it, p), xt[:, p, :]).then_inc(x_tile[p].free, 16)
                for p in range(2):
                    sp.wait_ge(x_tile[p].free, 16 * (PAIRS + 1))

            @block.gpsimd
            def _(pool):
                pool.memset(nhalf[:, :], -0.5).then_inc(made, 1)
                pool.wait_ge(loaded, LOADS)
                pool.tensor_copy(ident16[:, :], ident[:, :]).then_inc(made, 1)
                pool.tensor_copy(mask16[:, :], mask[:, :]).then_inc(made, 1)
                pool.wait_ge(made, 3)
                with pool.Fori(0, PAIRS) as it:
                    for p in range(2):
                        pool.wait_ge(var_ready[p], it + 1)
                        norm_power(nc, st[:, p, :], nhalf[:, :]).then_inc(rstd_ready[p], 1)

            @block.vector
            def _(v):
                open_slots(v, bank)
                open_slots(v, xn_s + xT_s + qk_s + qkT_s + probs_s + probsT_s + o_s)
                v.wait_ge(made, 3)
                with v.Fori(0, PAIRS) as it:
                    for p in range(2):
                        v.wait_ge(x_tile[p].full, x_tile[p].turn(it))
                        norm_stats(nc, v, xt[:, p, :], st[:, p, :], var_ready[p])
                    for p in range(2):
                        v.wait_ge(rstd_ready[p], it + 1)
                        v.wait_ge(xn_s[p].free, xn_s[p].turn(it))
                        norm_apply(nc, xn[:, p, :], xt[:, p, :], st[:, p, :]).then_inc(xn_s[p].full, 1)

                    for p in range(2):
                        banks = plan.of("qkv", p)
                        v.drain()
                        v.wait_ge(qk_s[p].free, qk_s[p].turn(it))
                        for b, k in banks:
                            v.wait_ge(bank[b].full, bank[b].turn(it, k))
                        b0 = banks[0][0]
                        src = PS[:, b0:b0 + 3, :].rearrange("p b n -> p (b n)")
                        heads = src[:, 0:QK].rearrange("p (h d) -> p h d", d=HD)
                        out = qk[:, p, :].rearrange("p (h d) -> p h d", d=HD)
                        turned = rot[:, :].rearrange("p (h d) -> p h d", d=HD)
                        n, h = QK // HD, HD // 2
                        nc.vector.tensor_tensor(out, heads, cs[:, 0:1, :].to_broadcast([P, n, HD]), ALU.mult)
                        nc.vector.tensor_tensor(turned[:, :, 0:h], heads[:, :, h:HD],
                                                cs[:, 1:2, 0:h].to_broadcast([P, n, h]), ALU.mult)
                        nc.vector.tensor_tensor(turned[:, :, h:HD], heads[:, :, 0:h],
                                                cs[:, 1:2, h:HD].to_broadcast([P, n, h]), ALU.mult)
                        nc.vector.tensor_copy(vs[:, p, :], src[:, QK:QKV]).then_inc(vs_ready, 1)
                        for b, k in banks:
                            v.drain().then_inc(bank[b].free, 1)
                        nc.vector.tensor_tensor(qk[:, p, :], qk[:, p, :], rot[:, :], ALU.add).then_inc(qk_s[p].full, 1)

                    for p in range(2):
                        for g in range(KV_HEADS + 1):
                            if g < KV_HEADS:
                                (b, k), = plan.of("scores", p, g)
                                v.wait_ge(bank[b].full, bank[b].turn(it, k))
                                nc.vector.tensor_reduce(nmax[:, g % 3, :],
                                                        PS[:, b, :].rearrange("p (r k) -> p r k", r=REP),
                                                        AX.X, ALU.max, negate=True)
                                v.drain()
                                nc.vector.tensor_scalar(nmax[:, g % 3, :], nmax[:, g % 3, :], HD ** -0.5, None,
                                                        ALU.mult).then_inc(max_ready, 1)
                            if g >= 1:
                                (b, k), = plan.of("probsT", p, g - 1)
                                s = probsT_s[(g - 1) % 2]
                                v.wait_ge(bank[b].full, bank[b].turn(it, k))
                                v.wait_ge(s.free, s.turn(it, (p * KV_HEADS + g - 1) // 2))
                                nc.vector.tensor_copy(probsT[:, (g - 1) % 2, :, :].rearrange("p r q -> p (r q)"),
                                                      PS[:, b, :]).then_inc(s.full, 1)
                                v.drain().then_inc(bank[b].free, 1)
                        v.wait_ge(sum_ready, 2 * it + p + 1)
                        v.wait_ge(o_s[p].free, o_s[p].turn(it))
                        nc.vector.reciprocal(rinv[:, p, :], rsum[:, p, :])
                        v.drain()
                        half = HEADS // 2
                        for i in range(2):
                            (b, k), = plan.of("o", p, i)
                            v.wait_ge(bank[b].full, bank[b].turn(it, k))
                            last = nc.vector.tensor_tensor(
                                o[:, p, i * BANK:(i + 1) * BANK].rearrange("p (h d) -> p h d", d=HD),
                                PS[:, b, :].rearrange("p (h d) -> p h d", d=HD),
                                rinv[:, p, i * half:(i + 1) * half].unsqueeze(2).to_broadcast([P, half, HD]),
                                ALU.mult).then_inc(bank[b].free, 1)
                        v.drain().then_inc(o_s[p].full, 1)

                    for p in range(2):
                        for i, (b, k) in enumerate(plan.of("y", p)):
                            v.wait_ge(bank[b].full, bank[b].turn(it, k))
                            part = xt[:, p, i * BANK:(i + 1) * BANK]
                            nc.vector.tensor_tensor(part, part, PS[:, b, :], ALU.add).then_inc(bank[b].free, 1)
                        v.drain().then_inc(y_ready[p], 1)

            @block.scalar
            def _(act):
                with act.Fori(0, PAIRS) as it:
                    for p in range(2):
                        act.wait_ge(xT_s[p].free, xT_s[p].turn(it, 0))
                        copy_banks(nc, act, plan.of("xT", p), bank, it, PS, xT[:, p, :, :], 4)
                        act.drain().then_inc(xT_s[p].full, 1)
                    for p in range(2):
                        act.wait_ge(qkT_s[p].free, qkT_s[p].turn(it))
                        copy_banks(nc, act, plan.of("qkT", p), bank, it, PS, qkT[:, p, :, :], 4)
                        act.drain().then_inc(qkT_s[p].full, 1)
                    for p in range(2):
                        for g in range(KV_HEADS):
                            (b, k), = plan.of("scores", p, g)
                            s = probs_s[g % 2]
                            act.wait_ge(max_ready, it * (2 * KV_HEADS) + (p * KV_HEADS + g + 1))
                            act.wait_ge(s.free, s.turn(it, (p * KV_HEADS + g) // 2))
                            for r in range(REP):
                                h = g * REP + r
                                nc.scalar.activation(probs[:, g % 2, r, :], PS[:, b, r * P:(r + 1) * P], ACT.Exp,
                                                     bias=nmax[:, g % 3, r:r + 1], scale=HD ** -0.5,
                                                     accum_out=rsum[:, p, h:h + 1])
                            act.drain().then_inc(s.full, 1)
                            act.drain().then_inc(bank[b].free, 1)
                        act.drain().then_inc(sum_ready, 1)
                    for p in range(2):
                        act.wait_ge(xT_s[p].free, xT_s[p].turn(it, 1))
                        copy_banks(nc, act, plan.of("oT", p), bank, it, PS, xT[:, p, :, :], 4)
                        act.drain().then_inc(xT_s[p].full, 1)

            @block.tensor
            def _(pe):
                pe.wait_ge(loaded, LOADS)
                pe.wait_ge(made, 3)
                with pe.Fori(0, PAIRS) as it:
                    for p in range(2):
                        pe.wait_ge(xn_s[p].full, xn_s[p].turn(it))
                        transpose_chunks(nc, pe, plan.of("xT", p), bank, it, PS, xn[:, p, :], ident, DC).then_inc(xn_s[p].free, 1)
                    for p in range(2):
                        pe.wait_ge(xT_s[p].full, xT_s[p].turn(it, 0))
                        for i, (b, k) in enumerate(plan.of("qkv", p)):
                            pe.wait_ge(bank[b].free, bank[b].turn(it, k))
                            for c in range(DC):
                                last = nc.tensor.matmul(PS[:, b, :], xT[:, p, c, :], wqkv[:, c, i * BANK:(i + 1) * BANK],
                                                        start=(c == 0), stop=(c == DC - 1))
                            last.then_inc(bank[b].full, 1)
                        pe.drain().then_inc(xT_s[p].free, 1)
                    for p in range(2):
                        pe.wait_ge(qk_s[p].full, qk_s[p].turn(it))
                        transpose_chunks(nc, pe, plan.of("qkT", p), bank, it, PS, qk[:, p, :], ident, QK // P).then_inc(qk_s[p].free, 1)
                    for p in range(2):
                        pe.wait_ge(qkT_s[p].full, qkT_s[p].turn(it))
                        pe.wait_ge(vs_ready, 2 * it + p + 1)
                        for g in range(KV_HEADS + 2):
                            if g < KV_HEADS:
                                (b, k), = plan.of("scores", p, g)
                                kc, slot = g // 4, 32 * (g % 4)
                                pe.wait_ge(bank[b].free, bank[b].turn(it, k))
                                nc.tensor.matmul(PS[:, b, :].rearrange("p (r k) -> p r k", r=REP), ident16[:, :],
                                                 mask16[:, :].unsqueeze(1).to_broadcast([P, REP, P]),
                                                 start=True, stop=False)
                                for r in range(REP):
                                    last = nc.tensor.matmul(PS[:, b, r * P:(r + 1) * P],
                                                            qkT[slot:slot + HD, p, kc * REP + r, :],
                                                            qkT[slot:slot + HD, p, D // P + kc, :],
                                                            start=False, stop=(r == REP - 1))
                                last.then_inc(bank[b].full, 1)
                            if 0 <= g - 1 < KV_HEADS:
                                (b, k), = plan.of("probsT", p, g - 1)
                                s = probs_s[(g - 1) % 2]
                                pe.wait_ge(bank[b].free, bank[b].turn(it, k))
                                pe.wait_ge(s.full, s.turn(it, (p * KV_HEADS + g - 1) // 2))
                                for r in range(REP):
                                    last = nc.tensor.transpose(PS[:, b, r * P:(r + 1) * P], probs[:, (g - 1) % 2, r, :], ident[:, :])
                                last.then_inc(s.free, 1)
                                pe.drain().then_inc(bank[b].full, 1)
                            if g >= 2:
                                e = g - 2
                                (b, k), = plan.of("o", p, e // 4)
                                s = probsT_s[e % 2]
                                if e % 4 == 0:
                                    pe.wait_ge(bank[b].free, bank[b].turn(it, k))
                                pe.wait_ge(s.full, s.turn(it, (p * KV_HEADS + e) // 2))
                                for r in range(REP):
                                    h = (e % 4) * REP + r
                                    last = nc.tensor.matmul(PS[:, b, h * HD:(h + 1) * HD], probsT[:, e % 2, r, :],
                                                            vs[:, p, e * HD:(e + 1) * HD], start=True, stop=True)
                                last.then_inc(s.free, 1)
                                if e % 4 == 3:
                                    pe.drain().then_inc(bank[b].full, 1)
                        pe.drain().then_inc(qkT_s[p].free, 1)
                    for p in range(2):
                        pe.wait_ge(o_s[p].full, o_s[p].turn(it))
                        transpose_chunks(nc, pe, plan.of("oT", p), bank, it, PS, o[:, p, :], ident, DC).then_inc(o_s[p].free, 1)
                    for p in range(2):
                        pe.wait_ge(xT_s[p].full, xT_s[p].turn(it, 1))
                        for i, (b, k) in enumerate(plan.of("y", p)):
                            pe.wait_ge(bank[b].free, bank[b].turn(it, k))
                            for c in range(DC):
                                last = nc.tensor.matmul(PS[:, b, :], xT[:, p, c, :], wo[:, c, i * BANK:(i + 1) * BANK],
                                                        start=(c == 0), stop=(c == DC - 1))
                            last.then_inc(bank[b].full, 1)
                        pe.drain().then_inc(xT_s[p].free, 1)
        clear(nc, ctx)



X_HEADS, WINDOW = 8, 16
X_HD = P // X_HEADS
LEFT = WINDOW // 2
NQ = 104
NK = NQ + WINDOW - 1
BLOCKS = 10
assert BLOCKS * NQ >= D
PADDED = (BLOCKS - 1) * NQ + NK
QUADS = X_HEADS // 2
UNITS = (BLOCKS // 2) * QUADS
VW = X_HD + 1


def window_attention(nc, x_in, x_out, ctx_in, w_x, b_x, v_row, band, eye):
    with ExitStack() as ctx:
        sb, sem, slots = makers(ctx, nc, "w_")
        PS = ctx.enter_context(nc.psum_tensor("w_ps", [P, 8, BANK], F32))
        w = sb("w", [P, 5, P])
        bias = sb("bias", [P, 4])
        vrow = sb("vrow", [1, P + PADDED])
        ident = sb("ident", [P, P])
        ident16 = sb("ident16", [P, P], BF16)
        mask = sb("mask", [P, NK])
        mask16 = sb("mask16", [P, NK], BF16)
        nhalf = sb("nhalf", [P, 1])
        xt = sb("xt", [P, 2, D])
        xn = sb("xn", [P, 2, D])
        st = sb("st", [P, 2, 16])
        cpad = sb("cpad", [P, 2, PADDED])
        kpad = sb("kpad", [P, 2, PADDED])
        q = sb("q", [P, 2, 2, BLOCKS * NQ])
        vT = sb("vT", [P, 2, BLOCKS, X_HEADS, VW])
        nmax = sb("nmax", [P, 3, 4])
        probs = sb("probs", [P, 2, 4, NK])
        probsT = sb("probsT", [P, 2, 4, NQ])
        rinv = sb("rinv", [P, 2, X_HEADS])
        o = sb("o", [P, 2, 2, P])
        oT = sb("oT", [P, 2, BLOCKS * NQ])

        loaded = sem("loaded")
        made = sem("made")
        x_tile = slots("x", unit=16)
        c_tile = slots("ctx", unit=16)
        var_ready = [sem(f"var_ready{p}") for p in range(2)]
        rstd_ready = [sem(f"rstd_ready{p}") for p in range(2)]
        xn_s = slots("xn")
        qk_s = slots("qk")
        vT_s = slots("vT")
        max_ready = sem("max_ready")
        probs_s = slots("probs", uses=UNITS)
        probsT_s = slots("probsT", uses=UNITS)
        o_s = slots("o", uses=BLOCKS // 2)
        oT_s = slots("oT")
        y_ready = [sem(f"y_ready{p}") for p in range(2)]

        plan = Plan(8)
        for p in range(2):
            plan.add(("q", p), 0, 1, 2, 3)
            plan.add(("k", p), 4, 5)
            plan.add(("v", p), 6, 7, 0)
        for p in range(2):
            for u in range(UNITS + 4):
                if u < UNITS:
                    plan.add(("scores", p, u), u % 3)
                if 0 <= u - 1 < UNITS:
                    plan.add(("probsT", p, u - 1), 3 + (u - 1) % 2)
                if 0 <= u - 2 < UNITS and (u - 2) % QUADS == 0:
                    plan.add(("o", p, (u - 2) // QUADS), 5 + (u - 2) // QUADS % 2)
                if u >= 7 and (u - 7) % QUADS == 0:
                    plan.add(("oT", p, (u - 7) // QUADS), 7)
        for p in range(2):
            plan.add(("y", p), 2 * p, 2 * p + 1)
        bank = [Slot(sem, f"bank{b}", plan.uses[b]) for b in range(8)]
        LOADS = 16 * 5

        def o_turn(it, p, i):
            n = p * (BLOCKS // 2) + i
            return n % 2, n // 2

        with nc.Block() as block:

            @block.sync
            def _(sp):
                sp.dma_start(ident[:, :], eye).then_inc(loaded, 16)
                sp.dma_start(w[:, :, :], w_x).then_inc(loaded, 16)
                sp.dma_start(bias[:, :], b_x).then_inc(loaded, 16)
                sp.dma_start(vrow[:, :], v_row).then_inc(loaded, 16)
                sp.dma_start(mask[:, :], band).then_inc(loaded, 16)
                open_slots(sp, x_tile)
                sp.wait_ge(made, 6)
                with sp.Fori(0, PAIRS) as it:
                    for p in range(2):
                        sp.wait_ge(c_tile[p].free, c_tile[p].turn(it))
                        sp.dma_start(cpad[:, p, LEFT:LEFT + D], rows(ctx_in, it, p)).then_inc(c_tile[p].full, 16)
                        sp.wait_ge(x_tile[p].free, x_tile[p].turn(it))
                        sp.dma_start(xt[:, p, :], rows(x_in, it, p)).then_inc(x_tile[p].full, 16)
                    for p in range(2):
                        sp.wait_ge(y_ready[p], it + 1)
                        sp.dma_start(rows(x_out, it, p), xt[:, p, :]).then_inc(x_tile[p].free, 16)
                for p in range(2):
                    sp.wait_ge(x_tile[p].free, 16 * (PAIRS + 1))

            @block.gpsimd
            def _(pool):
                pool.memset(nhalf[:, :], -0.5).then_inc(made, 1)
                pool.memset(cpad[:, :, :], 0.0).then_inc(made, 1)
                pool.memset(kpad[:, :, :], 0.0).then_inc(made, 1)
                pool.memset(q[:, :, :, :], 0.0).then_inc(made, 1)
                pool.memset(vT[:, :, :, :, :], 1.0).then_inc(made, 1)
                pool.memset(oT[:, :, :], 0.0).then_inc(made, 1)
                pool.wait_ge(loaded, LOADS)
                pool.tensor_copy(ident16[:, :], ident[:, :]).then_inc(made, 1)
                pool.tensor_copy(mask16[:, :], mask[:, :]).then_inc(made, 1)
                pool.wait_ge(made, 8)
                with pool.Fori(0, PAIRS) as it:
                    for p in range(2):
                        pool.wait_ge(var_ready[p], it + 1)
                        norm_power(nc, st[:, p, :], nhalf[:, :]).then_inc(rstd_ready[p], 1)

            @block.vector
            def _(v):
                open_slots(v, bank)
                open_slots(v, xn_s + qk_s + vT_s + probs_s + probsT_s + o_s + oT_s + c_tile)
                v.wait_ge(made, 8)
                with v.Fori(0, PAIRS) as it:
                    for p in range(2):
                        v.wait_ge(x_tile[p].full, x_tile[p].turn(it))
                        norm_stats(nc, v, xt[:, p, :], st[:, p, :], var_ready[p])
                    for p in range(2):
                        v.wait_ge(rstd_ready[p], it + 1)
                        v.wait_ge(xn_s[p].free, xn_s[p].turn(it))
                        norm_apply(nc, xn[:, p, :], xt[:, p, :], st[:, p, :]).then_inc(xn_s[p].full, 1)
                    for p in range(2):
                        v.wait_ge(vT_s[p].free, vT_s[p].turn(it))
                        for i, (b, k) in enumerate(plan.of("v", p)):
                            m = min(4, BLOCKS - 4 * i)
                            v.wait_ge(bank[b].full, bank[b].turn(it, k))
                            nc.vector.tensor_copy(vT[0:NK, p, 4 * i:4 * i + m, :, 0:X_HD],
                                                  PS[0:NK, b, 0:m * P].rearrange("p (m h d) -> p m h d", m=m, d=X_HD)
                                                  ).then_inc(bank[b].free, 1)
                        v.drain().then_inc(vT_s[p].full, 1)

                    for p in range(2):
                        for u in range(UNITS + 3):
                            if u < UNITS:
                                (b, k), = plan.of("scores", p, u)
                                v.wait_ge(bank[b].full, bank[b].turn(it, k))
                                nc.vector.tensor_reduce(nmax[0:NQ, u % 3, :],
                                                        PS[0:NQ, b, 0:4 * NK].rearrange("p (r k) -> p r k", r=4),
                                                        AX.X, ALU.max, negate=True)
                                v.drain()
                                nc.vector.tensor_scalar(nmax[0:NQ, u % 3, :], nmax[0:NQ, u % 3, :], X_HD ** -0.5, None,
                                                        ALU.mult).then_inc(max_ready, 1)
                            if 0 <= u - 1 < UNITS:
                                (b, k), = plan.of("probsT", p, u - 1)
                                s = probsT_s[(u - 1) % 2]
                                v.wait_ge(bank[b].full, bank[b].turn(it, k))
                                v.wait_ge(s.free, s.turn(it, (p * UNITS + u - 1) // 2))
                                nc.vector.tensor_copy(probsT[0:NK, (u - 1) % 2, :, :].rearrange("p r q -> p (r q)"),
                                                      PS[0:NK, b, 0:4 * NQ]).then_inc(s.full, 1)
                                v.drain().then_inc(bank[b].free, 1)
                            if u >= 6 and (u - 6) % QUADS == 0:
                                i = (u - 6) // QUADS
                                (b, k), = plan.of("o", p, i)
                                n, turn = o_turn(it, p, i)
                                v.wait_ge(bank[b].full, bank[b].turn(it, k))
                                v.wait_ge(o_s[n].free, o_s[n].turn(it, turn))
                                sums = PS[0:NQ, b, 0:2 * X_HEADS * VW].rearrange("p (m d) -> p m d", d=VW)
                                rv = rinv[0:NQ, :, :].rearrange("p m h -> p (m h)").unsqueeze(2)
                                nc.vector.reciprocal(rv, sums[:, :, X_HD:VW])
                                v.drain()
                                nc.vector.tensor_tensor(o[0:NQ, n, :, :].rearrange("p m (h d) -> p (m h) d", d=X_HD),
                                                        sums[:, :, 0:X_HD], rv.to_broadcast([NQ, 2 * X_HEADS, X_HD]),
                                                        ALU.mult).then_inc(o_s[n].full, 1)
                                v.drain().then_inc(bank[b].free, 1)

                    for p in range(2):
                        for i, (b, k) in enumerate(plan.of("y", p)):
                            v.wait_ge(bank[b].full, bank[b].turn(it, k))
                            part = xt[:, p, i * BANK:(i + 1) * BANK]
                            nc.vector.scalar_tensor_tensor(part, PS[:, b, :], bias[:, 3:4], part, ALU.add, ALU.add
                                                           ).then_inc(bank[b].free, 1)
                        v.drain().then_inc(y_ready[p], 1)

            @block.scalar
            def _(act):
                act.wait_ge(made, 8)
                with act.Fori(0, PAIRS) as it:
                    for p in range(2):
                        act.wait_ge(qk_s[p].free, qk_s[p].turn(it))
                        for i, (b, k) in enumerate(plan.of("q", p)):
                            act.wait_ge(bank[b].full, bank[b].turn(it, k))
                            e, t = i // 2, (i % 2) * BANK
                            nc.scalar.activation(q[:, p, e, t:t + BANK], PS[:, b, :], ACT.Identity, bias=bias[:, e:e + 1]
                                                 ).then_inc(bank[b].free, 1)
                        for i, (b, k) in enumerate(plan.of("k", p)):
                            act.wait_ge(bank[b].full, bank[b].turn(it, k))
                            nc.scalar.activation(kpad[:, p, LEFT + i * BANK:LEFT + (i + 1) * BANK], PS[:, b, :], ACT.Identity,
                                                 bias=bias[:, 2:3]).then_inc(bank[b].free, 1)
                        act.drain().then_inc(qk_s[p].full, 1)
                    for p in range(2):
                        act.wait_ge(oT_s[p].free, oT_s[p].turn(it))

                        def heads_out(i):
                            (b, k), = plan.of("oT", p, i)
                            act.wait_ge(bank[b].full, bank[b].turn(it, k))
                            nc.scalar.activation(oT[:, p, 2 * NQ * i:2 * NQ * (i + 1)], PS[:, b, 0:2 * NQ], ACT.Copy
                                                 ).then_inc(bank[b].free, 1)

                        for u in range(UNITS):
                            (b, k), = plan.of("scores", p, u)
                            s = probs_s[u % 2]
                            act.wait_ge(max_ready, it * (2 * UNITS) + (p * UNITS + u + 1))
                            act.wait_ge(s.free, s.turn(it, (p * UNITS + u) // 2))
                            for r in range(4):
                                nc.scalar.activation(probs[0:NQ, u % 2, r, :], PS[0:NQ, b, r * NK:(r + 1) * NK], ACT.Exp,
                                                     bias=nmax[0:NQ, u % 3, r:r + 1], scale=X_HD ** -0.5)
                            act.drain().then_inc(s.full, 1)
                            act.drain().then_inc(bank[b].free, 1)
                            if u >= 8 and (u - 8) % QUADS == 0:
                                heads_out((u - 8) // QUADS)
                        heads_out(BLOCKS // 2 - 2)
                        heads_out(BLOCKS // 2 - 1)
                        act.drain().then_inc(oT_s[p].full, 1)

            @block.tensor
            def _(pe):
                pe.wait_ge(loaded, LOADS)
                pe.wait_ge(made, 8)
                with pe.Fori(0, PAIRS) as it:
                    for p in range(2):
                        pe.wait_ge(xn_s[p].full, xn_s[p].turn(it))
                        for i, (b, k) in enumerate(plan.of("q", p)):
                            t = (i % 2) * BANK
                            pe.wait_ge(bank[b].free, bank[b].turn(it, k))
                            nc.tensor.matmul(PS[:, b, :], w[:, i // 2, :], xn[:, p, t:t + BANK], start=True, stop=True
                                             ).then_inc(bank[b].full, 1)
                        pe.drain().then_inc(xn_s[p].free, 1)
                        pe.wait_ge(c_tile[p].full, c_tile[p].turn(it))
                        for i, (b, k) in enumerate(plan.of("k", p)):
                            t = LEFT + i * BANK
                            pe.wait_ge(bank[b].free, bank[b].turn(it, k))
                            nc.tensor.matmul(PS[:, b, :], w[:, 2, :], cpad[:, p, t:t + BANK], start=True, stop=True
                                             ).then_inc(bank[b].full, 1)
                        for i, (b, k) in enumerate(plan.of("v", p)):
                            pe.wait_ge(bank[b].free, bank[b].turn(it, k))
                            for m in range(4 * i, min(4 * i + 4, BLOCKS)):
                                out = PS[0:NK, b, (m % 4) * P:(m % 4 + 1) * P]
                                nc.tensor.matmul(out, cpad[:, p, NQ * m:NQ * m + NK], w[:, 3, :], start=True, stop=False)
                                last = nc.tensor.matmul(out, vrow[0:1, P + NQ * m:P + NQ * m + NK], vrow[0:1, 0:P],
                                                        start=False, stop=True)
                            last.then_inc(bank[b].full, 1)
                        pe.drain().then_inc(c_tile[p].free, 16)

                    for p in range(2):
                        pe.wait_ge(qk_s[p].full, qk_s[p].turn(it))
                        pe.wait_ge(vT_s[p].full, vT_s[p].turn(it))
                        for u in range(UNITS + 4):
                            if u < UNITS:
                                (b, k), = plan.of("scores", p, u)
                                i, quad = u // QUADS, 32 * (u % QUADS)
                                pe.wait_ge(bank[b].free, bank[b].turn(it, k))
                                nc.tensor.matmul(PS[0:NQ, b, 0:4 * NK].rearrange("p (r k) -> p r k", r=4), ident16[:, 0:NQ],
                                                 mask16[:, :].unsqueeze(1).to_broadcast([P, 4, NK]), start=True, stop=False)
                                for r in range(4):
                                    t, e = NQ * (2 * i + r // 2), r % 2
                                    last = nc.tensor.matmul(PS[0:NQ, b, r * NK:(r + 1) * NK],
                                                            q[quad:quad + 32, p, e, t:t + NQ],
                                                            kpad[quad:quad + 32, p, t:t + NK], start=False, stop=(r == 3))
                                last.then_inc(bank[b].full, 1)
                            if 0 <= u - 1 < UNITS:
                                n = u - 1
                                (b, k), = plan.of("probsT", p, n)
                                s = probs_s[n % 2]
                                pe.wait_ge(bank[b].free, bank[b].turn(it, k))
                                pe.wait_ge(s.full, s.turn(it, (p * UNITS + n) // 2))
                                for r in range(4):
                                    last = nc.tensor.transpose(PS[0:NK, b, r * NQ:(r + 1) * NQ], probs[0:NQ, n % 2, r, :],
                                                               ident[0:NQ, 0:NQ])
                                last.then_inc(s.free, 1)
                                pe.drain().then_inc(bank[b].full, 1)
                            if 0 <= u - 2 < UNITS:
                                n = u - 2
                                i, quad = n // QUADS, n % QUADS
                                (b, k), = plan.of("o", p, i)
                                s = probsT_s[n % 2]
                                if quad == 0:
                                    pe.wait_ge(bank[b].free, bank[b].turn(it, k))
                                pe.wait_ge(s.full, s.turn(it, (p * UNITS + n) // 2))
                                for r in range(4):
                                    m, h = r // 2, 2 * quad + r % 2
                                    c = (m * X_HEADS + h) * VW
                                    last = nc.tensor.matmul(PS[0:NQ, b, c:c + VW], probsT[0:NK, n % 2, r, :],
                                                            vT[0:NK, p, 2 * i + m, h, :], start=True, stop=True)
                                last.then_inc(s.free, 1)
                                if quad == QUADS - 1:
                                    pe.drain().then_inc(bank[b].full, 1)
                            if u >= 7 and (u - 7) % QUADS == 0:
                                i = (u - 7) // QUADS
                                (b, k), = plan.of("oT", p, i)
                                n, turn = o_turn(it, p, i)
                                pe.wait_ge(bank[b].free, bank[b].turn(it, k))
                                pe.wait_ge(o_s[n].full, o_s[n].turn(it, turn))
                                for m in range(2):
                                    last = nc.tensor.transpose(PS[:, b, m * NQ:(m + 1) * NQ], o[0:NQ, n, m, :], ident[0:NQ, 0:NQ])
                                last.then_inc(o_s[n].free, 1)
                                pe.drain().then_inc(bank[b].full, 1)
                        pe.drain().then_inc(qk_s[p].free, 1)
                        pe.drain().then_inc(vT_s[p].free, 1)
                    for p in range(2):
                        pe.wait_ge(oT_s[p].full, oT_s[p].turn(it))
                        for i, (b, k) in enumerate(plan.of("y", p)):
                            pe.wait_ge(bank[b].free, bank[b].turn(it, k))
                            nc.tensor.matmul(PS[:, b, :], w[:, 4, :], oT[:, p, i * BANK:(i + 1) * BANK], start=True, stop=True
                                             ).then_inc(bank[b].full, 1)
                        pe.drain().then_inc(oT_s[p].free, 1)
        clear(nc, ctx)



EXPERTS, RANK, TOP = 64, 16, 16
LORA_SCALE = 2.0
TAKEN = -3.0e38


def lora_mixture(nc, x_in, x_out, w_a, w_b, eye):
    with ExitStack() as ctx:
        sb, sem, slots = makers(ctx, nc, "m_")
        PS = ctx.enter_context(nc.psum_tensor("m_ps", [P, 8, BANK], F32))
        ER = EXPERTS * RANK
        wa = sb("wa", [P, DC, ER + EXPERTS])
        wb = sb("wb", [P, ER // P, D])
        ident = sb("ident", [P, P])
        xr = sb("xr", [P, 2, D])
        xT = sb("xT", [P, 2, DC, P])
        h = sb("h", [P, 2, ER])
        sc = sb("sc", [P, 2, 3, EXPERTS])
        best = sb("best", [P, 2, 16])
        nbest = sb("nbest", [P, 2, 1])
        e = sb("e", [P, 2, EXPERTS])
        gate = sb("gate", [P, 2, EXPERTS])
        gsum = sb("gsum", [P, 2, 2])
        norm = Norm(nc, sb, sem, slots, x_in)

        loaded = sem("loaded")
        made = sem("made")
        x_tile = slots("x", unit=16)
        xT_s = slots("xT", uses=2)
        h_s = slots("h")
        sc_ready = sem("sc_ready")
        e_ready = sem("e_ready")
        y_ready = [sem(f"y_ready{p}") for p in range(2)]

        plan = Plan(8)
        for p in range(2):
            plan.add(("xT", p), 6, 7)
            plan.add(("h", p), 3 * p, 3 * p + 1, 3 * p + 2)
        for p in range(2):
            plan.add(("hT", p), 6, 7)
            plan.add(("y", p), 3 * p, 3 * p + 1)
        bank = [Slot(sem, f"bank{b}", plan.uses[b]) for b in range(8)]
        LOADS = 16 * 5

        with nc.Block() as block:

            @block.sync
            def _(sp):
                sp.dma_start(ident[:, :], eye).then_inc(loaded, 16)
                open_slots(sp, x_tile + norm.landed)
                norm.load(sp, 0)
                wa_rows = w_a.rearrange("(c p) n -> p c n", p=P)
                wb_rows = w_b.rearrange("(c p) n -> p c n", p=P)
                for c in range(0, DC, 4):
                    sp.dma_start(wa[:, c:c + 4, :], wa_rows[:, c:c + 4, :]).then_inc(loaded, 16)
                for c in range(0, DC, 4):
                    sp.dma_start(wb[:, c:c + 4, :], wb_rows[:, c:c + 4, :]).then_inc(loaded, 16)

                def body(it, more):
                    if more:
                        norm.load(sp, it + 1)
                    for p in range(2):
                        sp.wait_ge(x_tile[p].free, x_tile[p].turn(it))
                        sp.dma_start(xr[:, p, :], rows(x_in, it, p)).then_inc(x_tile[p].full, 16)
                    for p in range(2):
                        sp.wait_ge(y_ready[p], it + 1)
                        sp.dma_start(rows(x_out, it, p), xr[:, p, :]).then_inc(x_tile[p].free, 16)

                each_step(sp, body)
                for p in range(2):
                    sp.wait_ge(x_tile[p].free, 16 * (PAIRS + 1))

            @block.gpsimd
            def _(pool):
                pool.memset(norm.nhalf[:, :], -0.5).then_inc(made, 1)
                pool.wait_ge(made, 1)
                norm.pool(pool, 0)
                with pool.Fori(0, PAIRS - 1) as it:
                    norm.pool(pool, it + 1)

            @block.vector
            def _(v):
                open_slots(v, bank)
                open_slots(v, xT_s + h_s)
                norm.vector(v, 0)

                def body(it, more):
                    for p in range(2):
                        scores, left8, left = sc[:, p, 0, :], sc[:, p, 1, :], sc[:, p, 2, :]
                        b, k = plan.of("h", p)[2]
                        v.drain()
                        v.wait_ge(bank[b].full, bank[b].turn(it, k))
                        v.wait_ge(e_ready, 2 * it + p + 1)
                        nc.vector.tensor_copy(scores, PS[:, b, 0:EXPERTS]).then_inc(bank[b].free, 1)
                        v.drain()
                        nc.vector.max(best[:, p, 0:8], scores)
                        v.drain()
                        nc.vector.tensor_scalar(nbest[:, p, :], best[:, p, 0:1], -1.0, None, ALU.mult).then_inc(sc_ready, 1)
                        nc.vector.match_replace(left8, best[:, p, 0:8], scores, TAKEN)
                        v.drain()
                        nc.vector.max(best[:, p, 8:16], left8)
                        v.drain()
                        nc.vector.match_replace(left, best[:, p, 8:16], left8, TAKEN)
                        v.drain()
                        v.wait_ge(e_ready, 2 * it + p + 3)
                        nc.vector.scalar_tensor_tensor(gate[:, p, :], left, TAKEN, e[:, p, :], ALU.is_le, ALU.mult,
                                                       accum_out=gsum[:, p, 0:1])
                        v.drain()
                        nc.vector.reciprocal(gsum[:, p, 1:2], gsum[:, p, 0:1])
                        v.drain()
                        nc.vector.tensor_scalar(gate[:, p, :], gate[:, p, :], gsum[:, p, 1:2], LORA_SCALE, ALU.mult, ALU.mult)
                        v.drain()
                        v.wait_ge(h_s[p].free, h_s[p].turn(it))
                        n = BANK // RANK
                        for i, (b, k) in enumerate(plan.of("h", p)[0:2]):
                            v.wait_ge(bank[b].full, bank[b].turn(it, k))
                            nc.vector.tensor_tensor(h[:, p, i * BANK:(i + 1) * BANK].rearrange("p (e r) -> p e r", r=RANK),
                                                    PS[:, b, :].rearrange("p (e r) -> p e r", r=RANK),
                                                    gate[:, p, i * n:(i + 1) * n].unsqueeze(2).to_broadcast([P, n, RANK]),
                                                    ALU.mult).then_inc(bank[b].free, 1)
                        v.drain().then_inc(h_s[p].full, 1)
                    if more:
                        norm.vector(v, it + 1)
                    for p in range(2):
                        v.wait_ge(x_tile[p].full, x_tile[p].turn(it))
                        for i, (b, k) in enumerate(plan.of("y", p)):
                            v.wait_ge(bank[b].full, bank[b].turn(it, k))
                            part = xr[:, p, i * BANK:(i + 1) * BANK]
                            nc.vector.tensor_tensor(part, part, PS[:, b, :], ALU.add).then_inc(bank[b].free, 1)
                        v.drain().then_inc(y_ready[p], 1)

                each_step(v, body)

            @block.scalar
            def _(act):
                act.nop().then_inc(e_ready, 2)

                def body(it, more):
                    for p in range(2):
                        act.wait_ge(xT_s[p].free, xT_s[p].turn(it, 0))
                        copy_banks(nc, act, plan.of("xT", p), bank, it, PS, xT[:, p, :, :], 4)
                        act.drain().then_inc(xT_s[p].full, 1)
                    for p in range(2):
                        act.wait_ge(sc_ready, 2 * it + p + 1)
                        nc.scalar.activation(e[:, p, :], sc[:, p, 0, :], ACT.Exp, bias=nbest[:, p, :]).then_inc(e_ready, 1)
                    for p in range(2):
                        act.wait_ge(xT_s[p].free, xT_s[p].turn(it, 1))
                        copy_banks(nc, act, plan.of("hT", p), bank, it, PS, xT[:, p, :, :], 4)
                        act.drain().then_inc(xT_s[p].full, 1)

                each_step(act, body)

            @block.tensor
            def _(pe):
                pe.wait_ge(loaded, LOADS)

                def body(it, more):
                    for p in range(2):
                        pe.wait_ge(norm.ready[p], it + 1)
                        transpose_chunks(nc, pe, plan.of("xT", p), bank, it, PS, norm.xn[:, p, :], ident, DC
                                         ).then_inc(norm.landed[p].free, 16)
                        pe.wait_ge(xT_s[p].full, xT_s[p].turn(it, 0))
                        for i, (b, k) in sorted(enumerate(plan.of("h", p)), key=lambda x: -x[0]):
                            n = min(BANK, ER + EXPERTS - i * BANK)
                            pe.wait_ge(bank[b].free, bank[b].turn(it, k))
                            for c in range(DC):
                                last = nc.tensor.matmul(PS[:, b, 0:n], xT[:, p, c, :], wa[:, c, i * BANK:i * BANK + n],
                                                        start=(c == 0), stop=(c == DC - 1))
                            last.then_inc(bank[b].full, 1)
                        pe.drain().then_inc(xT_s[p].free, 1)
                    for p in range(2):
                        pe.wait_ge(h_s[p].full, h_s[p].turn(it))
                        transpose_chunks(nc, pe, plan.of("hT", p), bank, it, PS, h[:, p, :], ident, ER // P).then_inc(h_s[p].free, 1)
                        pe.wait_ge(xT_s[p].full, xT_s[p].turn(it, 1))
                        for i, (b, k) in enumerate(plan.of("y", p)):
                            pe.wait_ge(bank[b].free, bank[b].turn(it, k))
                            for c in range(ER // P):
                                last = nc.tensor.matmul(PS[:, b, :], xT[:, p, c, :], wb[:, c, i * BANK:(i + 1) * BANK],
                                                        start=(c == 0), stop=(c == ER // P - 1))
                            last.then_inc(bank[b].full, 1)
                        pe.drain().then_inc(xT_s[p].free, 1)

                each_step(pe, body)
        clear(nc, ctx)



I = 2752
KEEP = I - int(0.5 * I)
IB = [(i * BANK, min(BANK, I - i * BANK)) for i in range((I + BANK - 1) // BANK)]
IC = [(i * P, min(P, I - i * P)) for i in range((I + P - 1) // P)]
HIGH_BITS, LOW_BITS = 15, 16


def sparse_gate(nc, x_in, s_out, w_gate, eye):
    with ExitStack() as ctx:
        sb, sem, slots = makers(ctx, nc, "g_")
        PS = ctx.enter_context(nc.psum_tensor("g_ps", [P, 8, BANK], F32))
        wg = sb("wg", [P, DC, I])
        ident = sb("ident", [P, P])
        xT = sb("xT", [P, 2, DC, P])
        s = sb("s", [P, 2, I])
        high = sb("high", [P, I], U16)
        low = sb("low", [P, I], U16)
        spare = sb("spare", [P, I], U16)
        out = sb("out", [P, 2, I])
        tile1 = sb("tile1", [P, 16])
        count, keys, lost = tile1[:, 0:1], tile1[:, 1:2], tile1[:, 2:3]
        steps, wanted, base, trial = tile1[:, 4:6], tile1[:, 6:7], tile1[:, 7:8], tile1[:, 8:9]
        thr = sb("thr", [P, 2], U16)
        norm = Norm(nc, sb, sem, slots, x_in)

        loaded = sem("loaded")
        made = sem("made")
        xT_s = slots("xT")
        s_s = slots("s")
        out_s = slots("out", unit=16)
        out_ready = [sem(f"out_ready{p}") for p in range(2)]

        plan = Plan(8)
        for p in range(2):
            plan.add(("xT", p), 6, 7)
            plan.add(("s", p), 0, 1, 2, 3, 4, 5)
        bank = [Slot(sem, f"bank{b}", plan.uses[b]) for b in range(8)]
        LOADS = 16 * 5

        with nc.Block() as block:

            @block.sync
            def _(sp):
                sp.dma_start(ident[:, :], eye).then_inc(loaded, 16)
                open_slots(sp, norm.landed + out_s)
                norm.load(sp, 0)
                w_rows = w_gate.rearrange("(c p) n -> p c n", p=P)
                for c in range(0, DC, 2):
                    sp.dma_start(wg[:, c:c + 2, :], w_rows[:, c:c + 2, :]).then_inc(loaded, 16)

                def body(it, more):
                    if more:
                        norm.load(sp, it + 1)
                    for p in range(2):
                        sp.wait_ge(out_ready[p], it + 1)
                        sp.dma_start(rows(s_out, it, p), out[:, p, :]).then_inc(out_s[p].free, 16)

                each_step(sp, body)
                for p in range(2):
                    sp.wait_ge(out_s[p].free, 16 * (PAIRS + 1))

            @block.gpsimd
            def _(pool):
                pool.memset(norm.nhalf[:, :], -0.5).then_inc(made, 1)
                pool.wait_ge(made, 1)
                norm.pool(pool, 0)
                with pool.Fori(0, PAIRS - 1) as it:
                    norm.pool(pool, it + 1)

            @block.vector
            def _(v):
                open_slots(v, bank)
                open_slots(v, xT_s + s_s)
                norm.vector(v, 0)

                def search(keys_u16, bits):
                    nc.vector.memset(steps[:, 0:1], -float(2 ** (bits - 1)))
                    nc.vector.memset(steps[:, 1:2], float(2 ** (bits - 2)))
                    nc.vector.memset(trial, float(2 ** (bits - 1)))
                    v.drain()
                    with v.Fori(0, bits):
                        nc.vector.tensor_scalar(spare[:, :], keys_u16, trial, None, ALU.is_ge, ALU.add, accum_out=count)
                        v.drain()
                        nc.vector.tensor_scalar(lost, count, wanted, steps[:, 0:1], ALU.is_lt, ALU.mult)
                        v.drain()
                        nc.vector.tensor_scalar(trial, trial, lost, steps[:, 1:2], ALU.add, ALU.add)
                        v.drain()
                        nc.vector.tensor_scalar(steps, steps, 0.5, None, ALU.mult)
                        v.drain()
                    nc.vector.tensor_scalar(trial, trial, -0.5, None, ALU.add)
                    v.drain()

                def body(it, more):
                    for p in range(2):
                        v.wait_ge(s_s[p].full, s_s[p].turn(it))
                        halves = s[:, p, :].bitcast(U16).rearrange("p (n w) -> p n w", w=2)
                        nc.vector.tensor_scalar(high[:, :], halves[:, :, 1], 0x7fff, None, ALU.bitwise_and)
                        nc.vector.memset(wanted, float(KEEP))
                        v.drain()
                        search(high[:, :], HIGH_BITS)
                        nc.vector.tensor_scalar(base, trial, 1.0, None, ALU.add)
                        nc.vector.tensor_copy(thr[:, 1:2], trial)
                        nc.vector.scalar_tensor_tensor(low[:, :], high[:, :], trial, halves[:, :, 0], ALU.is_equal, ALU.mult)
                        v.drain()
                        nc.vector.tensor_scalar(spare[:, :], high[:, :], base, None, ALU.is_ge, ALU.add, accum_out=count)
                        v.drain()
                        nc.vector.tensor_scalar(wanted, count, -1.0, float(KEEP), ALU.mult, ALU.add)
                        v.drain()
                        search(low[:, :], LOW_BITS)
                        nc.vector.tensor_copy(thr[:, 0:1], trial)
                        v.drain()
                        v.wait_ge(out_s[p].free, out_s[p].turn(it))
                        nc.vector.tensor_scalar(out[:, p, :].bitcast(U32), s[:, p, :].bitcast(U32), 0x7fffffff, None,
                                                ALU.bitwise_and)
                        v.drain()
                        nc.vector.scalar_tensor_tensor(out[:, p, :], out[:, p, :], thr[:, :].bitcast(F32), s[:, p, :],
                                                       ALU.is_ge, ALU.mult).then_inc(out_ready[p], 1)
                        v.drain().then_inc(s_s[p].free, 1)
                        if more and p == 0:
                            norm.vector(v, it + 1)

                each_step(v, body)

            @block.scalar
            def _(act):
                def body(it, more):
                    for p in range(2):
                        act.wait_ge(xT_s[p].free, xT_s[p].turn(it))
                        copy_banks(nc, act, plan.of("xT", p), bank, it, PS, xT[:, p, :, :], 4)
                        act.drain().then_inc(xT_s[p].full, 1)
                        act.wait_ge(s_s[p].free, s_s[p].turn(it))
                        for (b, k), (i, n) in zip(plan.of("s", p), IB):
                            act.wait_ge(bank[b].full, bank[b].turn(it, k))
                            nc.scalar.activation(s[:, p, i:i + n], PS[:, b, 0:n], ACT.Silu).then_inc(bank[b].free, 1)
                        act.drain().then_inc(s_s[p].full, 1)

                each_step(act, body)

            @block.tensor
            def _(pe):
                pe.wait_ge(loaded, LOADS)

                def body(it, more):
                    for p in range(2):
                        pe.wait_ge(norm.ready[p], it + 1)
                        transpose_chunks(nc, pe, plan.of("xT", p), bank, it, PS, norm.xn[:, p, :], ident, DC
                                         ).then_inc(norm.landed[p].free, 16)
                        pe.wait_ge(xT_s[p].full, xT_s[p].turn(it))
                        for (b, k), (i, n) in zip(plan.of("s", p), IB):
                            pe.wait_ge(bank[b].free, bank[b].turn(it, k))
                            for c in range(DC):
                                last = nc.tensor.matmul(PS[:, b, 0:n], xT[:, p, c, :], wg[:, c, i:i + n],
                                                        start=(c == 0), stop=(c == DC - 1))
                            last.then_inc(bank[b].full, 1)
                        pe.drain().then_inc(xT_s[p].free, 1)

                each_step(pe, body)
        clear(nc, ctx)



def sparse_ffn(nc, x_in, s_in, x_out, w_up, w_down, eye):
    with ExitStack() as ctx:
        sb, sem, slots = makers(ctx, nc, "f_")
        PS = ctx.enter_context(nc.psum_tensor("f_ps", [P, 8, BANK], F32))
        wu = sb("wu", [P, DC, I])
        wd = sb("wd", [P, len(IC), D])
        ident = sb("ident", [P, P])
        xT = sb("xT", [P, DC, P])
        s = sb("s", [P, I])
        sT = sb("sT", [P, len(IC), P])
        xr = sb("xr", [P, D])
        norm = Norm(nc, sb, sem, slots, x_in)

        loaded = sem("loaded")
        made = sem("made")
        x_tile, = slots("x", unit=16, uses=2, n=1)
        s_tile, = slots("s", unit=16, uses=2, n=1)
        xT_s, = slots("xT", uses=2, n=1)
        h_ready = sem("h_ready")
        sT_s, = slots("sT", uses=2, n=1)
        y_ready = sem("y_ready")

        plan = Plan(8)
        plan.add(("xT", 0), 6, 7)
        for p in range(2):
            plan.add(("u", p), 0, 1, 2, 3, 4, 5)
            if p == 0:
                plan.add(("xT", 1), 6, 7)
            plan.add(("sT", p), 6, 7, 6, 7, 6, 7)
            plan.add(("y", p), 2 * p, 2 * p + 1)
        bank = [Slot(sem, f"bank{b}", plan.uses[b]) for b in range(8)]
        LOADS = 16 * 10

        with nc.Block() as block:

            @block.sync
            def _(sp):
                sp.dma_start(ident[:, :], eye).then_inc(loaded, 16)
                open_slots(sp, norm.landed + [x_tile])
                norm.load(sp, 0)
                w_rows = w_up.rearrange("(c p) n -> p c n", p=P)
                for c in range(0, DC, 2):
                    sp.dma_start(wu[:, c:c + 2, :], w_rows[:, c:c + 2, :]).then_inc(loaded, 16)
                full = I // P
                d_rows = w_down[0:full * P, :].rearrange("(c p) n -> p c n", p=P)
                for c in range(0, full, 6):
                    n = min(6, full - c)
                    sp.dma_start(wd[:, c:c + n, :], d_rows[:, c:c + n, :]).then_inc(loaded, 16)
                sp.dma_start(wd[0:I - full * P, full, :], w_down[full * P:I, :]).then_inc(loaded, 16)

                def body(it, more):
                    for p in range(2):
                        sp.wait_ge(s_tile.free, s_tile.turn(it, p))
                        sp.dma_start(s[:, :], rows(s_in, it, p)).then_inc(s_tile.full, 16)
                        if more and p == 1:
                            norm.load(sp, it + 1)
                        sp.wait_ge(x_tile.free, x_tile.turn(it, p))
                        sp.dma_start(xr[:, :], rows(x_in, it, p)).then_inc(x_tile.full, 16)
                        sp.wait_ge(y_ready, 2 * it + p + 1)
                        sp.dma_start(rows(x_out, it, p), xr[:, :]).then_inc(x_tile.free, 16)

                each_step(sp, body)
                sp.wait_ge(x_tile.free, 16 * (BATCHES + 1))

            @block.gpsimd
            def _(pool):
                pool.memset(norm.nhalf[:, :], -0.5).then_inc(made, 1)
                pool.wait_ge(made, 1)
                norm.pool(pool, 0)
                with pool.Fori(0, PAIRS - 1) as it:
                    norm.pool(pool, it + 1)

            @block.vector
            def _(v):
                open_slots(v, bank)
                open_slots(v, [xT_s, sT_s, s_tile])
                norm.vector(v, 0)

                def body(it, more):
                    for p in range(2):
                        v.wait_ge(s_tile.full, s_tile.turn(it, p))
                        for (b, k), (i, n) in zip(plan.of("u", p), IB):
                            v.wait_ge(bank[b].full, bank[b].turn(it, k))
                            nc.vector.tensor_tensor(s[:, i:i + n], s[:, i:i + n], PS[:, b, 0:n], ALU.mult
                                                    ).then_inc(bank[b].free, 1)
                        v.drain().then_inc(h_ready, 1)
                        if more and p == 1:
                            norm.vector(v, it + 1)
                        v.wait_ge(x_tile.full, x_tile.turn(it, p))
                        for i, (b, k) in enumerate(plan.of("y", p)):
                            v.wait_ge(bank[b].full, bank[b].turn(it, k))
                            part = xr[:, i * BANK:(i + 1) * BANK]
                            nc.vector.tensor_tensor(part, part, PS[:, b, :], ALU.add).then_inc(bank[b].free, 1)
                        v.drain().then_inc(y_ready, 1)

                each_step(v, body)

            @block.scalar
            def _(act):
                def body(it, more):
                    for p in range(2):
                        act.wait_ge(xT_s.free, xT_s.turn(it, p))
                        copy_banks(nc, act, plan.of("xT", p), bank, it, PS, xT[:, :, :], 4)
                        act.drain().then_inc(xT_s.full, 1)
                    for p in range(2):
                        act.wait_ge(sT_s.free, sT_s.turn(it, p))
                        for j, (b, k) in enumerate(plan.of("sT", p)):
                            c, m = 4 * j, min(4, I // P - 4 * j)
                            act.wait_ge(bank[b].full, bank[b].turn(it, k))
                            if m < 4:
                                q = I - (I // P) * P
                                nc.scalar.activation(sT[0:q, c + m, :], PS[0:q, b, m * P:(m + 1) * P], ACT.Copy)
                            nc.scalar.activation(sT[:, c:c + m, :], PS[:, b, 0:m * P].rearrange("p (c t) -> p c t", c=m), ACT.Copy)
                            act.drain().then_inc(bank[b].free, 1)
                        act.drain().then_inc(sT_s.full, 1)

                each_step(act, body)

            @block.tensor
            def _(pe):
                pe.wait_ge(loaded, LOADS)

                def body(it, more):
                    def transpose_x(p):
                        pe.wait_ge(norm.ready[p], it + 1)
                        transpose_chunks(nc, pe, plan.of("xT", p), bank, it, PS, norm.xn[:, p, :], ident, DC
                                         ).then_inc(norm.landed[p].free, 16)

                    transpose_x(0)
                    for p in range(2):
                        pe.wait_ge(xT_s.full, xT_s.turn(it, p))
                        for (b, k), (i, n) in zip(plan.of("u", p), IB):
                            pe.wait_ge(bank[b].free, bank[b].turn(it, k))
                            for c in range(DC):
                                last = nc.tensor.matmul(PS[:, b, 0:n], xT[:, c, :], wu[:, c, i:i + n],
                                                        start=(c == 0), stop=(c == DC - 1))
                            last.then_inc(bank[b].full, 1)
                        pe.drain().then_inc(xT_s.free, 1)
                        if p == 0:
                            transpose_x(1)
                        pe.wait_ge(h_ready, 2 * it + p + 1)
                        for j, (b, k) in enumerate(plan.of("sT", p)):
                            pe.wait_ge(bank[b].free, bank[b].turn(it, k))
                            for c in range(4 * j, min(4 * j + 4, len(IC))):
                                i, n = IC[c]
                                last = nc.tensor.transpose(PS[0:n, b, (c % 4) * P:(c % 4 + 1) * P], s[:, i:i + n], ident[:, :])
                            last.then_inc(bank[b].full, 1)
                        pe.drain().then_inc(s_tile.free, 16)
                        pe.wait_ge(sT_s.full, sT_s.turn(it, p))
                        for j, (b, k) in enumerate(plan.of("y", p)):
                            pe.wait_ge(bank[b].free, bank[b].turn(it, k))
                            for c, (i, n) in enumerate(IC):
                                last = nc.tensor.matmul(PS[:, b, :], sT[0:n, c, :], wd[0:n, c, j * BANK:(j + 1) * BANK],
                                                        start=(c == 0), stop=(c == len(IC) - 1))
                            last.then_inc(bank[b].full, 1)
                        pe.drain().then_inc(sT_s.free, 1)

                each_step(pe, body)
        clear(nc, ctx)



LAGS = P
TOPLAGS = 9
Q1, Q2, K1, K2 = range(4)
VE1, VE2, VO1, VO2, WE1, WE2, WO1, WO2 = range(4, 12)
INV, INV_E, INV_O = range(12, 15)
MATRICES = 15


def autocorrelation(nc, x_in, x_out, ctx_in, dft, eye):
    with ExitStack() as ctx:
        sb, sem, slots = makers(ctx, nc, "c_")
        PS = ctx.enter_context(nc.psum_tensor("c_ps", [P, 8, BANK], F32))
        mats = sb("mats", [P, MATRICES, P])
        ident = sb("ident", [P, P])
        xr = sb("xr", [P, 2, D])
        kv = sb("kv", [P, 2, D])
        kf = sb("kf", [P, 2, D])
        prod = sb("prod", [P, 2, 2, D])
        vf = sb("vf", [P, 2, 4, D])
        wprod = sb("wprod", [P, 4, D])
        wT = sb("wT", [P, D])
        best = sb("best", [P, DC, 8])
        ninth = sb("ninth", [P, DC, 8])
        late = sb("late", [P, DC, 8])
        nbest = sb("nbest", [P, 2, DC])
        left = sb("left", [P, 2, DC, LAGS])
        corr = sb("corr", [P, 2, DC, LAGS])
        e = sb("e", [P, 2, DC, LAGS])
        wsum = sb("wsum", [P, 2, DC])
        norm = Norm(nc, sb, sem, slots, x_in)

        loaded = sem("loaded")
        made = sem("made")
        x_tile = slots("x", unit=16)
        kv_tile = slots("kv", unit=16)
        kf_s, = slots("kf", uses=2, n=1)
        prod_s = slots("prod")
        vf_s = slots("vf")
        corr_s = slots("corr")
        nbest_ready = sem("nbest_ready")
        e_ready = sem("e_ready")
        w_s = slots("w")
        wT_s, = slots("wT", uses=2, n=1)
        wprod_s, = slots("wprod", uses=2, n=1)
        y_ready = [sem(f"y_ready{p}") for p in range(2)]

        A, B, C, E = (0, 1), (2, 3), (4, 5), (6, 7)
        plan = Plan(8)
        for p in range(2):
            for i, (name, pair) in enumerate([("k", A), ("k", B), ("q", C), ("q", E)]):
                plan.add((name, p, i % 2), *pair)
        for p in range(2):
            plan.add(("corr", p), *(A, B)[p])
        for p in range(2):
            for i in range(4):
                plan.add(("v", p, i), *(C, E)[i % 2])
        for p in range(2):
            plan.add(("wT", p), *(C, B)[p])
            for i in range(4):
                plan.add(("w", p, i), *((E, A, C, E), (C, E, A, B))[p][i])
            plan.add(("y", p), *(A, C)[p])
        bank = [Slot(sem, f"bank{b}", plan.uses[b]) for b in range(8)]
        LOADS = 16 * 2

        with nc.Block() as block:

            @block.sync
            def _(sp):
                sp.dma_start(mats[:, :, :], dft).then_inc(loaded, 16)
                sp.dma_start(ident[:, :], eye).then_inc(loaded, 16)
                open_slots(sp, x_tile + norm.landed)
                norm.load(sp, 0)

                def body(it, more):
                    for p in range(2):
                        sp.wait_ge(kv_tile[p].free, kv_tile[p].turn(it))
                        sp.dma_start(kv[:, p, :], rows(ctx_in, it, p)).then_inc(kv_tile[p].full, 16)
                    if more:
                        norm.load(sp, it + 1)
                    for p in range(2):
                        sp.wait_ge(x_tile[p].free, x_tile[p].turn(it))
                        sp.dma_start(xr[:, p, :], rows(x_in, it, p)).then_inc(x_tile[p].full, 16)
                    for p in range(2):
                        sp.wait_ge(y_ready[p], it + 1)
                        sp.dma_start(rows(x_out, it, p), xr[:, p, :]).then_inc(x_tile[p].free, 16)

                each_step(sp, body)
                for p in range(2):
                    sp.wait_ge(x_tile[p].free, 16 * (PAIRS + 1))

            @block.gpsimd
            def _(pool):
                pool.memset(norm.nhalf[:, :], -0.5).then_inc(made, 1)
                pool.wait_ge(made, 1)
                norm.pool(pool, 0)
                with pool.Fori(0, PAIRS - 1) as it:
                    norm.pool(pool, it + 1)

            @block.vector
            def _(v):
                open_slots(v, bank)
                open_slots(v, kv_tile + prod_s + corr_s + vf_s + w_s + [kf_s, wT_s, wprod_s])
                norm.vector(v, 0)

                def body(it, more):
                    for p in range(2):
                        v.wait_ge(kf_s.full, kf_s.turn(it, p))
                        v.wait_ge(prod_s[p].free, prod_s[p].turn(it))
                        for i in range(2):
                            for j, (b, k) in enumerate(plan.of("q", p, i)):
                                t = slice(j * BANK, (j + 1) * BANK)
                                v.wait_ge(bank[b].full, bank[b].turn(it, k))
                                nc.vector.tensor_tensor(prod[:, p, i, t], PS[:, b, :], kf[:, i, t], ALU.mult
                                                        ).then_inc(bank[b].free, 1)
                        v.drain().then_inc(prod_s[p].full, 1)
                        v.drain().then_inc(kf_s.free, 1)
                    for p in range(2):
                        v.wait_ge(corr_s[p].full, corr_s[p].turn(it))
                        v.wait_ge(w_s[p].free, w_s[p].turn(it))
                        nc.vector.memset(late[:, :, 1:8], TAKEN)
                        for c in range(DC):
                            nc.vector.max(best[:, c, :], corr[:, p, c, :])
                        v.drain()
                        nc.vector.tensor_scalar(nbest[:, p, :], best[:, :, 0], -1.0, None, ALU.mult).then_inc(nbest_ready, 1)
                        for c in range(DC):
                            nc.vector.match_replace(left[:, p, c, :], best[:, c, :], corr[:, p, c, :], TAKEN)
                        v.drain()
                        for c in range(DC):
                            nc.vector.max(ninth[:, c, :], left[:, p, c, :])
                        v.drain()
                        nc.vector.tensor_copy(late[:, :, 0], ninth[:, :, 0])
                        v.drain()
                        for c in range(DC):
                            nc.vector.match_replace(left[:, p, c, :], late[:, c, :], left[:, p, c, :], TAKEN)
                        v.drain()
                        v.wait_ge(e_ready, 2 * it + p + 1)
                        lf = left[:, p, :, :].rearrange("p c n -> p (c n)")
                        nc.vector.scalar_tensor_tensor(lf, lf, TAKEN, e[:, p, :, :].rearrange("p c n -> p (c n)"),
                                                       ALU.is_le, ALU.mult)
                        v.drain().then_inc(corr_s[p].free, 1)
                        nc.vector.tensor_reduce(wsum[:, p, :], left[:, p, :, :], AX.X, ALU.add)
                        v.drain()
                        nc.vector.reciprocal(wsum[:, p, :], wsum[:, p, :])
                        v.drain()
                        nc.vector.tensor_tensor(left[:, p, :, :], left[:, p, :, :],
                                                wsum[:, p, :].unsqueeze(2).to_broadcast([P, DC, LAGS]), ALU.mult
                                                ).then_inc(w_s[p].full, 1)
                    for p in range(2):
                        v.wait_ge(vf_s[p].full, vf_s[p].turn(it))
                        v.wait_ge(wprod_s.free, wprod_s.turn(it, p))
                        for i in range(4):
                            for j, (b, k) in enumerate(plan.of("w", p, i)):
                                t = slice(j * BANK, (j + 1) * BANK)
                                v.wait_ge(bank[b].full, bank[b].turn(it, k))
                                nc.vector.tensor_tensor(wprod[:, i, t], PS[:, b, :], vf[:, p, i, t], ALU.mult
                                                        ).then_inc(bank[b].free, 1)
                        v.drain().then_inc(wprod_s.full, 1)
                        v.drain().then_inc(vf_s[p].free, 1)
                        if more and p == 0:
                            norm.vector(v, it + 1)
                        v.wait_ge(x_tile[p].full, x_tile[p].turn(it))
                        for i, (b, k) in enumerate(plan.of("y", p)):
                            v.wait_ge(bank[b].full, bank[b].turn(it, k))
                            part = xr[:, p, i * BANK:(i + 1) * BANK]
                            nc.vector.tensor_tensor(part, part, PS[:, b, :], ALU.add).then_inc(bank[b].free, 1)
                        v.drain().then_inc(y_ready[p], 1)

                each_step(v, body)

            @block.scalar
            def _(act):
                def body(it, more):
                    def evacuate(banks, out):
                        for j, (b, k) in enumerate(banks):
                            act.wait_ge(bank[b].full, bank[b].turn(it, k))
                            nc.scalar.activation(out[:, j * BANK:(j + 1) * BANK], PS[:, b, :], ACT.Copy).then_inc(bank[b].free, 1)

                    for p in range(2):
                        act.wait_ge(kf_s.free, kf_s.turn(it, p))
                        for i in range(2):
                            evacuate(plan.of("k", p, i), kf[:, i, :])
                        act.drain().then_inc(kf_s.full, 1)

                    def exps(p):
                        act.wait_ge(nbest_ready, 2 * it + p + 1)
                        act.wait_ge(w_s[p].free, w_s[p].turn(it))
                        for c in range(DC):
                            nc.scalar.activation(e[:, p, c, :], corr[:, p, c, :], ACT.Exp, bias=nbest[:, p, c:c + 1])
                        act.drain().then_inc(e_ready, 1)

                    def spectrum(p):
                        act.wait_ge(vf_s[p].free, vf_s[p].turn(it))
                        for i in range(4):
                            evacuate(plan.of("v", p, i), vf[:, p, i, :])
                        act.drain().then_inc(vf_s[p].full, 1)

                    for p in range(2):
                        act.wait_ge(corr_s[p].free, corr_s[p].turn(it))
                        evacuate(plan.of("corr", p), corr[:, p, :, :].rearrange("p c n -> p (c n)"))
                        act.drain().then_inc(corr_s[p].full, 1)
                    spectrum(0)
                    exps(0)
                    spectrum(1)
                    exps(1)
                    for p in range(2):
                        act.wait_ge(wT_s.free, wT_s.turn(it, p))
                        evacuate(plan.of("wT", p), wT[:, :])
                        act.drain().then_inc(wT_s.full, 1)

                each_step(act, body)

            @block.tensor
            def _(pe):
                pe.wait_ge(loaded, LOADS)

                def body(it, more):
                    def transform(banks, matrices, srcs):
                        for j, (b, k) in enumerate(banks):
                            pe.wait_ge(bank[b].free, bank[b].turn(it, k))
                            for n, (m, src) in enumerate(zip(matrices, srcs)):
                                last = nc.tensor.matmul(PS[:, b, :], mats[:, m, :], src[:, j * BANK:(j + 1) * BANK],
                                                        start=(n == 0), stop=(n == len(srcs) - 1))
                            last.then_inc(bank[b].full, 1)

                    for p in range(2):
                        pe.wait_ge(kv_tile[p].full, kv_tile[p].turn(it))
                        for i in range(2):
                            transform(plan.of("k", p, i), [K1 + i], [kv[:, p, :]])
                        pe.wait_ge(norm.ready[p], it + 1)
                        for i in range(2):
                            transform(plan.of("q", p, i), [Q1 + i], [norm.xn[:, p, :]])
                        pe.drain().then_inc(norm.landed[p].free, 16)
                    for p in range(2):
                        pe.wait_ge(prod_s[p].full, prod_s[p].turn(it))
                        for j, (b, k) in enumerate(plan.of("corr", p)):
                            pe.wait_ge(bank[b].free, bank[b].turn(it, k))
                            for c in range(4 * j, 4 * j + 4):
                                for i in range(2):
                                    last = nc.tensor.matmul(PS[:, b, (c % 4) * P:(c % 4 + 1) * P],
                                                            prod[:, p, i, c * P:(c + 1) * P], mats[:, INV, :],
                                                            start=(i == 0), stop=(i == 1))
                            last.then_inc(bank[b].full, 1)
                        pe.drain().then_inc(prod_s[p].free, 1)
                    for p in range(2):
                        for i in range(4):
                            transform(plan.of("v", p, i), [VE1 + i], [kv[:, p, :]])
                        pe.drain().then_inc(kv_tile[p].free, 16)
                    for p in range(2):
                        pe.wait_ge(w_s[p].full, w_s[p].turn(it))
                        transpose_chunks(nc, pe, plan.of("wT", p), bank, it, PS,
                                         left[:, p, :, :].rearrange("p c n -> p (c n)"), ident, DC).then_inc(w_s[p].free, 1)
                        pe.wait_ge(wT_s.full, wT_s.turn(it, p))
                        for i in range(4):
                            transform(plan.of("w", p, i), [WE1 + i], [wT[:, :]])
                        pe.drain().then_inc(wT_s.free, 1)
                        pe.wait_ge(wprod_s.full, wprod_s.turn(it, p))
                        transform(plan.of("y", p), [INV_E, INV_E, INV_O, INV_O], [wprod[:, i, :] for i in range(4)])
                        pe.drain().then_inc(wprod_s.free, 1)

                each_step(pe, body)
        clear(nc, ctx)



ROUTED, R = 8, 16
ER = ROUTED * R


def routed_linear(nc, x_in, x_out, w_base, w_la, w_lb, b_base, b_router, eye):
    with ExitStack() as ctx:
        sb, sem, slots = makers(ctx, nc, "r_")
        PS = ctx.enter_context(nc.psum_tensor("r_ps", [P, 8, BANK], F32))
        wb = sb("wb", [P, DC, D])
        wa = sb("wa", [P, DC, ER + ROUTED])
        wlb = sb("wlb", [P, D])
        ident = sb("ident", [P, P])
        bb = sb("bb", [P, D])
        br = sb("br", [P, ROUTED])
        xr = sb("xr", [P, 2, D])
        xT = sb("xT", [P, 2, DC, P])
        z = sb("z", [P, 2, ROUTED])
        runs = sb("runs", [P, 4, 4 + ROUTED])
        inv_k = sb("inv_k", [P, ROUTED])
        tau = sb("tau", [P, 2, 1])
        gate = sb("gate", [P, 2, ROUTED])
        h = sb("h", [P, 2, ER])
        hT = sb("hT", [P, 2, P])
        norm = Norm(nc, sb, sem, slots, x_in)

        loaded = sem("loaded")
        made = sem("made")
        x_tile = slots("x", unit=16)
        biased = [sem(f"biased{p}") for p in range(2)]
        xT_s = slots("xT")
        h_s = slots("h")
        hT_s = slots("hT")
        y_ready = [sem(f"y_ready{p}") for p in range(2)]

        plan = Plan(8)
        for p in range(2):
            plan.add(("xT", p), 6, 7)
            plan.add(("h", p), 2 + 3 * p)
            plan.add(("y", p), 3 * p, 3 * p + 1)
            plan.add(("hT", p), 6)
        bank = [Slot(sem, f"bank{b}", plan.uses[b]) for b in range(8)]
        LOADS = 16 * 9

        with nc.Block() as block:

            @block.sync
            def _(sp):
                sp.dma_start(ident[:, :], eye).then_inc(loaded, 16)
                open_slots(sp, x_tile + norm.landed)
                norm.load(sp, 0)
                sp.dma_start(wa[:, :, :], w_la.rearrange("(c p) n -> p c n", p=P)).then_inc(loaded, 16)
                w_rows = w_base.rearrange("(c p) n -> p c n", p=P)
                for c in range(0, DC, 2):
                    sp.dma_start(wb[:, c:c + 2, :], w_rows[:, c:c + 2, :]).then_inc(loaded, 16)
                sp.dma_start(wlb[:, :], w_lb).then_inc(loaded, 16)
                sp.dma_start(bb[:, :], b_base.to_broadcast([P, D])).then_inc(loaded, 16)
                sp.dma_start(br[:, :], b_router.to_broadcast([P, ROUTED])).then_inc(loaded, 16)

                def body(it, more):
                    if more:
                        norm.load(sp, it + 1)
                    for p in range(2):
                        sp.wait_ge(x_tile[p].free, x_tile[p].turn(it))
                        sp.dma_start(xr[:, p, :], rows(x_in, it, p)).then_inc(x_tile[p].full, 16)
                    for p in range(2):
                        sp.wait_ge(y_ready[p], it + 1)
                        sp.dma_start(rows(x_out, it, p), xr[:, p, :]).then_inc(x_tile[p].free, 16)

                each_step(sp, body)
                for p in range(2):
                    sp.wait_ge(x_tile[p].free, 16 * (PAIRS + 1))

            @block.gpsimd
            def _(pool):
                pool.memset(norm.nhalf[:, :], -0.5).then_inc(made, 1)
                pool.memset(runs[:, :, :], 0.0).then_inc(made, 1)
                for k in range(ROUTED):
                    pool.memset(inv_k[:, k:k + 1], 1.0 / (k + 1)).then_inc(made, 1)
                pool.wait_ge(made, 2 + ROUTED)
                norm.pool(pool, 0)
                pool.wait_ge(loaded, LOADS)

                def body(it, more):
                    for p in range(2):
                        pool.wait_ge(x_tile[p].full, x_tile[p].turn(it))
                        pool.tensor_tensor(xr[:, p, :], xr[:, p, :], bb[:, :], ALU.add).then_inc(biased[p], 1)
                    if more:
                        norm.pool(pool, it + 1)

                each_step(pool, body)

            @block.vector
            def _(v):
                open_slots(v, bank)
                open_slots(v, xT_s + h_s + hT_s)
                v.wait_ge(made, 2 + ROUTED)
                norm.vector(v, 0)
                v.wait_ge(loaded, LOADS)

                def body(it, more):
                    for p in range(2):
                        (b, k), = plan.of("h", p)
                        v.wait_ge(bank[b].full, bank[b].turn(it, k))
                        nc.vector.tensor_tensor(z[:, p, :], PS[:, b, ER:ER + ROUTED], br[:, :], ALU.add)
                        v.drain()
                        nc.vector.max(runs[:, 0, 4:4 + ROUTED], z[:, p, :])
                        v.drain()
                        for i in range(3):
                            d = 4 - 2 ** i
                            nc.vector.tensor_tensor(runs[:, i + 1, 4:4 + ROUTED], runs[:, i, 4:4 + ROUTED],
                                                    runs[:, i, d:d + ROUTED], ALU.add)
                            v.drain()
                        nc.vector.scalar_tensor_tensor(runs[:, 0, 4:4 + ROUTED], runs[:, 3, 4:4 + ROUTED], -1.0, inv_k[:, :],
                                                       ALU.add, ALU.mult)
                        v.drain()
                        nc.vector.tensor_reduce(tau[:, p, :], runs[:, 0, 4:4 + ROUTED], AX.X, ALU.max)
                        v.drain()
                        nc.vector.tensor_scalar(gate[:, p, :], z[:, p, :], tau[:, p, :], 0.0, ALU.subtract, ALU.max)
                        v.drain()
                        v.wait_ge(h_s[p].free, h_s[p].turn(it))
                        nc.vector.tensor_tensor(h[:, p, :].rearrange("p (e r) -> p e r", r=R),
                                                PS[:, b, 0:ER].rearrange("p (e r) -> p e r", r=R),
                                                gate[:, p, :].unsqueeze(2).to_broadcast([P, ROUTED, R]), ALU.mult
                                                ).then_inc(h_s[p].full, 1)
                        v.drain().then_inc(bank[b].free, 1)
                    if more:
                        norm.vector(v, it + 1)
                    for p in range(2):
                        v.wait_ge(biased[p], it + 1)
                        for i, (b, k) in enumerate(plan.of("y", p)):
                            v.wait_ge(bank[b].full, bank[b].turn(it, k))
                            part = xr[:, p, i * BANK:(i + 1) * BANK]
                            nc.vector.tensor_tensor(part, part, PS[:, b, :], ALU.add).then_inc(bank[b].free, 1)
                        v.drain().then_inc(y_ready[p], 1)

                each_step(v, body)

            @block.scalar
            def _(act):
                def body(it, more):
                    for p in range(2):
                        act.wait_ge(xT_s[p].free, xT_s[p].turn(it))
                        copy_banks(nc, act, plan.of("xT", p), bank, it, PS, xT[:, p, :, :], 4)
                        act.drain().then_inc(xT_s[p].full, 1)
                        (b, k), = plan.of("hT", p)
                        act.wait_ge(hT_s[p].free, hT_s[p].turn(it))
                        act.wait_ge(bank[b].full, bank[b].turn(it, k))
                        nc.scalar.activation(hT[:, p, :], PS[:, b, 0:P], ACT.Copy).then_inc(bank[b].free, 1)
                        act.drain().then_inc(hT_s[p].full, 1)

                each_step(act, body)

            @block.tensor
            def _(pe):
                pe.wait_ge(loaded, LOADS)

                def body(it, more):
                    for p in range(2):
                        pe.wait_ge(norm.ready[p], it + 1)
                        transpose_chunks(nc, pe, plan.of("xT", p), bank, it, PS, norm.xn[:, p, :], ident, DC
                                         ).then_inc(norm.landed[p].free, 16)
                        pe.wait_ge(xT_s[p].full, xT_s[p].turn(it))
                        (b, k), = plan.of("h", p)
                        pe.wait_ge(bank[b].free, bank[b].turn(it, k))
                        for c in range(DC):
                            last = nc.tensor.matmul(PS[:, b, 0:ER + ROUTED], xT[:, p, c, :], wa[:, c, :],
                                                    start=(c == 0), stop=(c == DC - 1))
                        last.then_inc(bank[b].full, 1)
                        for i, (b, k) in enumerate(plan.of("y", p)):
                            pe.wait_ge(bank[b].free, bank[b].turn(it, k))
                            for c in range(DC):
                                nc.tensor.matmul(PS[:, b, :], xT[:, p, c, :], wb[:, c, i * BANK:(i + 1) * BANK],
                                                 start=(c == 0), stop=False)
                        pe.drain().then_inc(xT_s[p].free, 1)
                        pe.wait_ge(h_s[p].full, h_s[p].turn(it))
                        transpose_chunks(nc, pe, plan.of("hT", p), bank, it, PS, h[:, p, :], ident, 1).then_inc(h_s[p].free, 1)
                        pe.wait_ge(hT_s[p].full, hT_s[p].turn(it))
                        for i, (b, k) in enumerate(plan.of("y", p)):
                            nc.tensor.matmul(PS[:, b, :], hT[:, p, :], wlb[:, i * BANK:(i + 1) * BANK],
                                             start=False, stop=True).then_inc(bank[b].full, 1)
                        pe.drain().then_inc(hT_s[p].free, 1)

                each_step(pe, body)
        clear(nc, ctx)


def program(nc, d, out):
    xs = [d['x']] + [nc.dram_tensor(f'x{i}', (BATCHES * P, D), F32, kind='Internal').ap() for i in range(1, 6)] + [out]
    self_attention(nc, xs[0], xs[1], d['w_qkv'], d['w_o'], d['cos_sin'], d['causal'], d['eye'])
    window_attention(nc, xs[1], xs[2], d['ctx'], d['wx'], d['bx'], d['vrow'], d['band'], d['eye'])
    lora_mixture(nc, xs[2], xs[3], d['w_a'], d['w_b'], d['eye'])
    h = nc.dram_tensor('sparse_gate', (BATCHES * P, I), F32, kind='Internal').ap()
    sparse_gate(nc, xs[3], h, d['w_gate'], d['eye'])
    sparse_ffn(nc, xs[3], h, xs[4], d['w_up'], d['w_down'], d['eye'])
    autocorrelation(nc, xs[4], xs[5], d['ctx'], d['dft'], d['eye'])
    routed_linear(nc, xs[5], xs[6], d['w_base'], d['w_la'], d['w_lb'], d['b_base'], d['b_router'], d['eye'])



def dft_matrices():
    import numpy as np

    half = P // 2
    t = np.arange(P)

    def spectrum(size, freqs, pad):
        phase = -2.0 * np.pi * np.outer(np.arange(size), freqs) / size
        re, im = np.cos(phase), np.sin(phase)
        if pad:
            re[P - 1], im[P - 1] = re[P - 1:size - 1].sum(0), im[P - 1:size - 1].sum(0)
        return re[:P], im[:P]

    def block(size, freqs, ends, pad):
        re, im = spectrum(size, freqs, pad)
        a1, a2 = np.concatenate([re, im], 1), np.concatenate([im, -re], 1)
        re, im = spectrum(size, freqs, False)
        b1, b2 = np.concatenate([re, re], 1), np.concatenate([im, im], 1)
        if ends:
            a1[:, half] = spectrum(size, [size // 2], pad)[0][:, 0]
            b1[:, half] = spectrum(size, [size // 2], False)[0][:, 0]
            a2[:, half] = 0.0
            b2[:, half] = 0.0
        return a1, a2, b1, b2

    def inverse(size, freqs, ends):
        phase = 2.0 * np.pi * np.outer(freqs, t) / size
        out = np.concatenate([2.0 * np.cos(phase), -2.0 * np.sin(phase)], 0) / size
        if ends:
            out[0] /= 2.0
            out[half] = np.cos(np.pi * t) / size
        return out

    g = np.arange(half)
    q1, q2, k1, k2 = block(P, g, True, False)
    e1, e2, we1, we2 = block(2 * P, 2 * g, True, True)
    o1, o2, wo1, wo2 = block(2 * P, 2 * g + 1, False, True)
    mats = [q1, q2, k1, k2, e1, e2, o1, o2, we1, we2, wo1, wo2,
            inverse(P, g, True), inverse(2 * P, 2 * g, True), inverse(2 * P, 2 * g + 1, False)]
    return np.stack(mats, 1).astype(np.float32)


def layouts(inputs):
    import numpy as np

    a = {k: np.asarray(v) for k, v in inputs.items()}
    lay = {}
    wq = a["L0_attn_Wq"].reshape(2, 4, REP, HD, D).transpose(0, 2, 1, 3, 4).reshape(D, D)
    lay["w_qkv"] = np.concatenate([wq, a["L0_attn_Wk"], a["L0_attn_Wv"]], axis=0).T
    lay["w_o"] = a["L0_attn_Wo"].T
    inv = (1.0 / np.float32(10000.0) ** (np.arange(0, HD, 2, dtype=np.float32) / np.float32(HD))).astype(np.float32)
    freqs = np.outer(np.arange(P, dtype=np.float32), inv).astype(np.float32)
    cos, sin = np.cos(freqs), np.sin(freqs)
    lay["cos_sin"] = np.stack([np.concatenate([cos, cos], 1), np.concatenate([-sin, sin], 1)], 1).astype(np.float32)
    i = np.arange(P)
    lay["causal"] = np.where(i[:, None] < i[None, :], MASKED, 0.0).astype(np.float32)
    lay["eye"] = np.eye(P, dtype=np.float32)
    lay["x"] = a["x"].reshape(BATCHES * P, D)
    lay["ctx"] = a["ctx_4096"].reshape(BATCHES * P, D)
    wq, bq = a["L0_xattn_Wq"], a["L0_xattn_bq"]
    odd = (i // X_HD) % 2 == 1
    zero = np.zeros_like(wq)
    w = [np.where(odd[:, None], zero, wq), np.where(odd[:, None], wq, zero)] + [a["L0_xattn_W" + n] for n in "kvo"]
    lay["wx"] = np.stack([m.T for m in w], 1)
    lay["bx"] = np.stack([np.where(odd, 0, bq), np.where(odd, bq, 0), a["L0_xattn_bk"], a["L0_xattn_bo"]], 1).astype(np.float32)
    ones = np.zeros(PADDED, np.float32)
    ones[LEFT:LEFT + D] = 1.0
    lay["vrow"] = np.concatenate([a["L0_xattn_bv"], ones])[None, :]
    past = np.arange(NK)[None, :] - i[:, None]
    lay["band"] = np.where((past >= 0) & (past < WINDOW), 0.0, MASKED).astype(np.float32)
    lay["w_a"] = np.concatenate([a["L0_ffn_A"].reshape(EXPERTS * RANK, D), a["L0_ffn_Wr"]], 0).T
    lay["w_b"] = a["L0_ffn_B"].transpose(0, 2, 1).reshape(EXPERTS * RANK, D)
    lay["w_gate"] = a["L1_attn_w_gate"].T
    lay["w_up"] = a["L1_attn_w_up"].T
    lay["w_down"] = a["L1_attn_w_down"].T
    lay["dft"] = dft_matrices()
    lay["w_base"] = a["L1_ffn_W_base"].T
    lay["w_la"] = np.concatenate([a["L1_ffn_lora_A"].transpose(1, 0, 2).reshape(D, ER), a["L1_ffn_W_router"].T], 1)
    lay["w_lb"] = a["L1_ffn_lora_B"].reshape(ER, D)
    lay["b_base"] = a["L1_ffn_b_base"][None, :]
    lay["b_router"] = a["L1_ffn_b_router"][None, :]
    return {k: np.ascontiguousarray(v) for k, v in lay.items()}


def kernel(**inputs):
    import concourse.bacc as bacc
    from concourse.bass_utils import run_bass_kernel_spmd as run

    nc = bacc.Bacc("TRN2", target_bir_lowering=False, num_devices=1, dynamic_dma_scratch_size=1024)
    lay = layouts(inputs)
    d = {k: nc.dram_tensor("in_" + k, v.shape, mybir.dt.from_np(v.dtype), kind="ExternalInput").ap() for k, v in lay.items()}
    out = nc.dram_tensor("out_x", (BATCHES * P, D), F32, kind="ExternalOutput").ap()
    program(nc, d, out)
    r = run(nc, [{"in_" + k: v for k, v in lay.items()}], core_ids=[0])
    return r.results[0]["out_x"].reshape(BATCHES, P, D)
```

```python
from contextlib import ExitStack

import concourse.bass as bass
from concourse import mybir

ALU = mybir.AluOpType
ACT = mybir.ActivationFunctionType
F32 = mybir.dt.float32
BF16 = mybir.dt.bfloat16
U16 = mybir.dt.uint16
U32 = mybir.dt.uint32
AX = mybir.AxisListType

P = 128
BATCHES = 16
D = 1024
DC = D // P
PAIRS = BATCHES // 2
BANK = 512
EPS = 1e-5
MASKED = -1e30


class Slot:

    def __init__(self, sem, name, uses=1, unit=1):
        self.full = sem(name + "_full")
        self.free = sem(name + "_free")
        self.uses = uses
        self.unit = unit

    def turn(self, it, k=0):
        return (it * self.uses + (k + 1)) * self.unit


class Plan:

    def __init__(self, banks):
        self.uses = [0] * banks
        self.table = {}

    def add(self, key, *banks):
        self.table[key] = [(b, self.take(b)) for b in banks]

    def take(self, b):
        self.uses[b] += 1
        return self.uses[b] - 1

    def of(self, *key):
        return self.table[key]


def makers(ctx, nc, prefix):
    ctx.sems = []

    def sb(name, shape, dt=F32):
        return ctx.enter_context(nc.sbuf_tensor(prefix + name, shape, dt))

    def sem(name):
        s = ctx.enter_context(nc.semaphore(prefix + name))
        ctx.sems.append(s)
        return s

    def slots(name, uses=1, unit=1, n=2):
        return [Slot(sem, f"{name}{i}", uses, unit) for i in range(n)]

    return sb, sem, slots


def open_slots(engine, slots):
    for s in slots:
        engine.nop().then_inc(s.free, s.unit)


def norm_stats(nc, v, x, st, var_ready):
    nc.vector.bn_stats(st[:, 0:6], x[:, 0:BANK])
    nc.vector.bn_stats(st[:, 6:12], x[:, BANK:D])
    v.drain()
    nc.vector.bn_aggr(st[:, 12:14], st[:, 0:12])
    v.drain()
    nc.vector.tensor_scalar(st[:, 14:15], st[:, 13:14], EPS, None, ALU.add).then_inc(var_ready, 1)


def norm_apply(nc, out, x, st):
    return nc.vector.tensor_scalar(out, x, st[:, 12:13], st[:, 15:16], ALU.subtract, ALU.mult)


def norm_power(nc, st, nhalf):
    return nc.gpsimd.tensor_tensor(st[:, 15:16], st[:, 14:15], nhalf, ALU.pow)


def rows(x_dram, it, p):
    return x_dram[bass.ds(it * (2 * P) + p * P, P), :]


class Norm:

    def __init__(self, nc, sb, sem, slots, x_in):
        self.nc, self.x_in = nc, x_in
        self.xn = sb("xn", [P, 2, D])
        self.st = sb("st", [P, 2, 16])
        self.nhalf = sb("nhalf", [P, 1])
        self.landed = slots("xn", unit=16)
        self.var_ready = [sem(f"var_ready{p}") for p in range(2)]
        self.rstd_ready = [sem(f"rstd_ready{p}") for p in range(2)]
        self.ready = [sem(f"xn_ready{p}") for p in range(2)]

    def load(self, sp, it):
        for p in range(2):
            self.load_one(sp, it, p)

    def load_one(self, sp, it, p):
        sp.wait_ge(self.landed[p].free, self.landed[p].turn(it))
        sp.dma_start(self.xn[:, p, :], rows(self.x_in, it, p)).then_inc(self.landed[p].full, 16)

    def vector(self, v, it):
        for p in range(2):
            self.stats_one(v, it, p)
        for p in range(2):
            self.apply_one(v, it, p)

    def stats_one(self, v, it, p):
        v.wait_ge(self.landed[p].full, self.landed[p].turn(it))
        norm_stats(self.nc, v, self.xn[:, p, :], self.st[:, p, :], self.var_ready[p])

    def apply_one(self, v, it, p):
        v.wait_ge(self.rstd_ready[p], it + 1)
        norm_apply(self.nc, self.xn[:, p, :], self.xn[:, p, :], self.st[:, p, :]).then_inc(self.ready[p], 1)

    def pool(self, pool, it):
        for p in range(2):
            pool.wait_ge(self.var_ready[p], it + 1)
            norm_power(self.nc, self.st[:, p, :], self.nhalf[:, :]).then_inc(self.rstd_ready[p], 1)


def each_step(engine, body):
    with engine.Fori(0, PAIRS - 1) as it:
        body(it, True)
    body(PAIRS - 1, False)


def each_two_steps(engine, body):
    with engine.Fori(0, PAIRS // 2 - 1) as i:
        for half in range(2):
            body(i * 2 + half, i, half, 2)
    for half in range(2):
        body(PAIRS - 2 + half, PAIRS // 2 - 1, half, 1 - half)


def copy_banks(nc, act, banks, bank, it, PS, out, chunks):
    n = out.shape[1]
    for i, (b, k) in enumerate(banks):
        act.wait_ge(bank[b].full, bank[b].turn(it, k))
        m = min(chunks, n - i * chunks)
        nc.scalar.activation(out[:, i * chunks:i * chunks + m, :],
                             PS[:, b, 0:m * out.shape[2]].rearrange("p (c t) -> p c t", c=m),
                             ACT.Copy).then_inc(bank[b].free, 1)


def transpose_chunks(nc, pe, banks, bank, it, PS, src, ident, n):
    for i, (b, k) in enumerate(banks):
        pe.wait_ge(bank[b].free, bank[b].turn(it, k))
        for c in range(4 * i, min(4 * i + 4, n)):
            last = nc.tensor.transpose(PS[:, b, (c % 4) * P:(c % 4 + 1) * P], src[:, c * P:(c + 1) * P], ident[:, :])
        if i < len(banks) - 1:
            last.then_inc(bank[b].full, 1)
        else:
            pe.drain().then_inc(bank[b].full, 1)
    return pe.drain()


def clear(nc, ctx):
    for s in ctx.sems:
        nc.sync.sem_clear(s)
    nc.all_engine_barrier()



HEADS, KV_HEADS, HD = 32, 8, 32
REP = HEADS // KV_HEADS
QK = D + KV_HEADS * HD
QKV = D + 2 * KV_HEADS * HD
HALF = KV_HEADS // 2

A_TURN = 2
A_MIX = 3
A_DENSE = {(0, 1, "xT"): 0, (0, 1, "qkv0a"): 1, (0, 1, "qkv0b"): 2, (0, 1, "qkv1a"): 3, (0, 1, "qkv1b"): 4,
           (0, 1, "qkv2a"): 5, (0, 1, "qkv2b"): 5, (0, 1, "qkT"): 6,
           (1, 0, "xT"): 6, (1, 0, "qkv0a"): 7, (1, 0, "qkv0b"): 8, (1, 0, "qkv1a"): 9, (1, 0, "qkv1b"): 10,
           (0, 0, "oT"): 11, (0, 0, "y0a"): 12, (0, 0, "y0b"): 13, (0, 0, "y1a"): 14, (0, 0, "y1b"): 15,
           (1, 0, "qkv2a"): 16, (1, 0, "qkv2b"): 18, (0, 1, "oT"): 19, (0, 1, "y0a"): 20, (0, 1, "y0b"): 20,
           (1, 0, "qkT"): 21, (0, 1, "y1a"): 22, (0, 1, "y1b"): 22}
A_STREAM = max(A_DENSE.values()) + 1


def dense_work(u, more):
    return [key for key, at in A_DENSE.items() if at == u and (more or not key[0])]


def self_attention(nc, x_in, x_out, w_qkv, w_o, cos_sin, causal, eye):
    with ExitStack() as ctx:
        sb, sem, slots = makers(ctx, nc, "a_")
        PS = ctx.enter_context(nc.psum_tensor("a_ps", [P, 8, BANK], F32))
        wqkv = sb("wqkv", [P, DC, QKV])
        wo = sb("wo", [P, DC, D])
        cs = sb("cs", [P, 2, HD])
        ident = sb("ident", [P, P])
        mask = sb("mask", [P, P])
        ident16 = sb("ident16", [P, P], BF16)
        mask16 = sb("mask16", [P, P], BF16)
        norm = Norm(nc, sb, sem, slots, x_in)
        xt = sb("xt", [P, 2, D])
        xT = sb("xT", [P, 2, DC, P])
        qk = sb("qk", [P, 2, QK])
        rot = sb("rot", [P, BANK])
        vs = sb("vs", [P, 2, KV_HEADS * HD])
        qkT = sb("qkT", [P, 2, QK // P, P])
        nmax = sb("nmax", [P, 4, REP])
        probs = sb("probs", [P, 3, REP, P])
        probsT = sb("probsT", [P, 2, REP, P])
        rsum = sb("rsum", [P, 2, HEADS])
        rinv = sb("rinv", [P, 2, HEADS])
        o = sb("o", [P, 2, D])
        oT = sb("oT", [P, 2, DC, P])

        loaded = sem("loaded")
        wo_loaded = sem("wo_loaded")
        made = sem("made")
        x_tile = slots("x", unit=16)
        xT_s = slots("xT")
        oT_s = slots("oT")
        qk_s = slots("qk")
        qkT_s = slots("qkT")
        max_ready = sem("max_ready")
        probs_done = sem("probs_done")
        probsT_s = slots("probsT", uses=KV_HEADS)
        o_s = slots("o")
        y_ready = [sem(f"y_ready{p}") for p in range(2)]

        units = 2 * KV_HEADS
        plan = Plan(6)
        ring = 0
        for u in range(A_STREAM):
            if u < units:
                plan.add(("scores", u), u % 3)
            if 0 <= u - A_TURN < units:
                plan.add(("probsT", u - A_TURN), 3 + ring % 2)
                ring += 1
            if 0 <= u - A_MIX < units and (u - A_MIX) % HALF == 0:
                plan.add(("o", (u - A_MIX) // HALF), 5)
            for ahead, p, name in dense_work(u, False):
                if name == "oT":
                    plan.add((name, p), 3 + ring % 2, 3 + (ring + 1) % 2)
                    ring += 2
                if name in ("y0a", "y1a"):
                    plan.add((name[0:2], p), 3 + ring % 2)
                    ring += 1
        bank = [Slot(sem, f"bank{b}", plan.uses[b]) for b in range(6)]
        project_plan = Plan(2)
        project_plan.add(("xT",), 0, 1)
        for i in range(3):
            project_plan.add((f"qkv{i}",), i % 2)
        project_plan.add(("qkT",), 1, 0, 1)
        project_bank = [Slot(sem, f"project_bank{b}", project_plan.uses[b]) for b in range(2)]
        PPS = PS[:, 6:8, :]

        def heads_done(u):
            i = (u - A_MIX - (HALF - 1)) / HALF
            return int(i) if i in range(2 * KV_HEADS // HALF) else None

        with nc.Block() as block:

            @block.sync
            def _(sp):
                norm.load_one(sp, 0, 0)
                sp.dma_start(ident[:, :], eye).then_inc(loaded, 16)
                wq_rows = w_qkv.rearrange("(c p) n -> p c n", p=P)
                wo_rows = w_o.rearrange("(c p) n -> p c n", p=P)
                for c in range(0, DC, 2):
                    sp.dma_start(wqkv[:, c:c + 2, :], wq_rows[:, c:c + 2, :]).then_inc(loaded, 16)
                norm.load_one(sp, 0, 1)
                sp.dma_start(cs[:, :, :], cos_sin).then_inc(loaded, 16)
                sp.dma_start(mask[:, :], causal).then_inc(loaded, 16)
                for c in range(0, DC, 4):
                    sp.dma_start(wo[:, c:c + 4, :], wo_rows[:, c:c + 4, :]).then_inc(wo_loaded, 16)
                open_slots(sp, x_tile)

                def body(it, more):
                    if more:
                        norm.load_one(sp, it + 1, 0)
                    for p in range(2):
                        sp.wait_ge(x_tile[p].free, x_tile[p].turn(it))
                        sp.dma_start(xt[:, p, :], rows(x_in, it, p)).then_inc(x_tile[p].full, 16)
                    if more:
                        norm.load_one(sp, it + 1, 1)
                    for p in range(2):
                        sp.wait_ge(y_ready[p], it + 1)
                        sp.dma_start(rows(x_out, it, p), xt[:, p, :]).then_inc(x_tile[p].free, 16)

                each_step(sp, body)
                for p in range(2):
                    sp.wait_ge(x_tile[p].free, 16 * (PAIRS + 1))

            @block.gpsimd
            def _(pool):
                pool.memset(norm.nhalf[:, :], -0.5).then_inc(made, 1)
                pool.wait_ge(loaded, 16 * 7)
                pool.tensor_copy(ident16[:, :], ident[:, :]).then_inc(made, 1)
                pool.tensor_copy(mask16[:, :], mask[:, :]).then_inc(made, 1)
                pool.wait_ge(made, 3)
                norm.pool(pool, 0)
                with pool.Fori(0, PAIRS - 1) as it:
                    norm.pool(pool, it + 1)

            @block.vector
            def _(v):
                open_slots(v, norm.landed + bank[3:] + project_bank)
                open_slots(v, xT_s + oT_s + qk_s + qkT_s + probsT_s + o_s)
                v.wait_ge(made, 3)
                norm.vector(v, 0)

                def rotate(it, p, i):
                    (b, k), = project_plan.of(f"qkv{i}")
                    width = min(BANK, QK - i * BANK)
                    n, h = width // HD, HD // 2
                    v.drain()
                    if i == 0:
                        v.wait_ge(qk_s[p].free, qk_s[p].turn(it))
                    v.wait_ge(project_bank[b].full, project_bank[b].turn(2 * it + p, k))
                    heads = PPS[:, b, 0:width].rearrange("p (h d) -> p h d", d=HD)
                    part = qk[:, p, i * BANK:i * BANK + width]
                    turned = rot[:, 0:width].rearrange("p (h d) -> p h d", d=HD)
                    nc.vector.tensor_tensor(part.rearrange("p (h d) -> p h d", d=HD), heads,
                                            cs[:, 0:1, :].to_broadcast([P, n, HD]), ALU.mult)
                    nc.vector.tensor_tensor(turned[:, :, 0:h], heads[:, :, h:HD],
                                            cs[:, 1:2, 0:h].to_broadcast([P, n, h]), ALU.mult)
                    last = nc.vector.tensor_tensor(turned[:, :, h:HD], heads[:, :, 0:h],
                                                   cs[:, 1:2, h:HD].to_broadcast([P, n, h]), ALU.mult)
                    if i == 2:
                        last = nc.vector.tensor_copy(vs[:, p, :], PPS[:, b, width:BANK])
                    last.then_inc(project_bank[b].free, 1)
                    v.drain()
                    last = nc.vector.tensor_tensor(part, part, rot[:, 0:width], ALU.add)
                    if i == 2:
                        last.then_inc(qk_s[p].full, 1)

                for i in range(3):
                    rotate(0, 0, i)

                def body(it, more):
                    for u in range(A_STREAM):
                        if u < units:
                            (b, k), = plan.of("scores", u)
                            v.wait_ge(bank[b].full, bank[b].turn(it, k))
                            nc.vector.tensor_reduce(nmax[:, u % 4, :],
                                                    PS[:, b, :].rearrange("p (r k) -> p r k", r=REP),
                                                    AX.X, ALU.max, negate=True)
                            v.drain()
                            nc.vector.tensor_scalar(nmax[:, u % 4, :], nmax[:, u % 4, :], HD ** -0.5, None,
                                                    ALU.mult).then_inc(max_ready, 1)
                        n = u - A_TURN
                        if 0 <= n < units:
                            (b, k), = plan.of("probsT", n)
                            s = probsT_s[n % 2]
                            v.wait_ge(bank[b].full, bank[b].turn(it, k))
                            v.wait_ge(s.free, s.turn(it, n // 2))
                            nc.vector.tensor_copy(probsT[:, n % 2, :, :].rearrange("p r q -> p (r q)"),
                                                  PS[:, b, :]).then_inc(s.full, 1)
                            v.drain().then_inc(bank[b].free, 1)
                        i = heads_done(u)
                        if i is not None:
                            (b, k), = plan.of("o", i)
                            p, i = i // 2, i % 2
                            v.wait_ge(bank[b].full, bank[b].turn(it, k))
                            if i == 0:
                                v.wait_ge(o_s[p].free, o_s[p].turn(it))
                            n = HEADS // 2
                            nc.vector.reciprocal(rinv[:, p, i * n:(i + 1) * n], rsum[:, p, i * n:(i + 1) * n])
                            v.drain()
                            nc.vector.tensor_tensor(
                                o[:, p, i * BANK:(i + 1) * BANK].rearrange("p (h d) -> p h d", d=HD),
                                PS[:, b, :].rearrange("p (h d) -> p h d", d=HD),
                                rinv[:, p, i * n:(i + 1) * n].unsqueeze(2).to_broadcast([P, n, HD]),
                                ALU.mult).then_inc(bank[b].free, 1)
                            if i == 1:
                                v.drain().then_inc(o_s[p].full, 1)
                        for ahead, p, name in dense_work(u, more):
                            if name[0:3] == "qkv" and name[4] == "b":
                                rotate(it + ahead, p, int(name[3]))
                            if name in ("y0b", "y1b"):
                                if name == "y0b":
                                    v.wait_ge(x_tile[p].full, x_tile[p].turn(it))
                                i = int(name[1])
                                (b, k), = plan.of(f"y{i}", p)
                                v.wait_ge(bank[b].full, bank[b].turn(it, k))
                                part = xt[:, p, i * BANK:(i + 1) * BANK]
                                nc.vector.tensor_tensor(part, part, PS[:, b, :], ALU.add).then_inc(bank[b].free, 1)
                                if name == "y1b":
                                    v.drain().then_inc(y_ready[p], 1)
                        if more:
                            for p in range(2):
                                if u == p * KV_HEADS + 3:
                                    norm.stats_one(v, it + 1, p)
                                if u == p * KV_HEADS + 5:
                                    norm.apply_one(v, it + 1, p)

                each_step(v, body)

            @block.scalar
            def _(act):
                def copies(it, p, name, out, ready):
                    n = out.shape[1]
                    for i, (b, k) in enumerate(project_plan.of(name)):
                        act.wait_ge(project_bank[b].full, project_bank[b].turn(2 * it + p, k))
                        m = min(4, n - 4 * i)
                        nc.scalar.activation(out[:, 4 * i:4 * i + m, :],
                                             PPS[:, b, 0:m * P].rearrange("p (c t) -> p c t", c=m),
                                             ACT.Copy).then_inc(project_bank[b].free, 1)
                    act.drain().then_inc(ready, 1)

                def turned(it, p, name):
                    if name == "xT":
                        act.wait_ge(xT_s[p].free, xT_s[p].turn(it))
                        copies(it, p, name, xT[:, p, :, :], xT_s[p].full)
                    if name == "qkT":
                        act.wait_ge(qkT_s[p].free, qkT_s[p].turn(it))
                        copies(it, p, name, qkT[:, p, :, :], qkT_s[p].full)

                turned(0, 0, "xT")
                turned(0, 0, "qkT")

                def body(it, more):
                    for u in range(A_STREAM):
                        if u < units:
                            (b, k), = plan.of("scores", u)
                            p, g = u // KV_HEADS, u % KV_HEADS
                            act.wait_ge(max_ready, it * units + (u + 1))
                            if u >= 3:
                                (t_bank, t_k), = plan.of("probsT", u - 3)
                                act.wait_ge(bank[t_bank].full, bank[t_bank].turn(it, t_k))
                            for r in range(REP):
                                h = g * REP + r
                                nc.scalar.activation(probs[:, u % 3, r, :], PS[:, b, r * P:(r + 1) * P], ACT.Exp,
                                                     bias=nmax[:, u % 4, r:r + 1], scale=HD ** -0.5,
                                                     accum_out=rsum[:, p, h:h + 1])
                            act.drain().then_inc(probs_done, 1)
                        for ahead, p, name in dense_work(u, more):
                            turned(it + ahead, p, name)
                            if name == "oT":
                                act.wait_ge(oT_s[p].free, oT_s[p].turn(it))
                                copy_banks(nc, act, plan.of("oT", p), bank, it, PS, oT[:, p, :, :], 4)
                                act.drain().then_inc(oT_s[p].full, 1)

                each_step(act, body)

            @block.tensor
            def _(pe):
                def project(it, p, name):
                    banks = project_plan.of(name[0:4])
                    if name == "xT":
                        pe.wait_ge(norm.ready[p], it + 1)
                        src, n, done = norm.xn[:, p, :], DC, (norm.landed[p].free, 16)
                    if name == "qkT":
                        pe.wait_ge(qk_s[p].full, qk_s[p].turn(it))
                        src, n, done = qk[:, p, :], QK // P, (qk_s[p].free, 1)
                    if name in ("xT", "qkT"):
                        for i, (b, k) in enumerate(banks):
                            pe.wait_ge(project_bank[b].free, project_bank[b].turn(2 * it + p, k))
                            for c in range(4 * i, min(4 * i + 4, n)):
                                last = nc.tensor.transpose(PPS[:, b, (c % 4) * P:(c % 4 + 1) * P], src[:, c * P:(c + 1) * P],
                                                           ident[:, :])
                            last.then_inc(project_bank[b].full, 1)
                        pe.drain().then_inc(*done)
                        return
                    (b, k), = banks
                    i, half = int(name[3]), "ab".index(name[4])
                    if half == 0:
                        if i == 0:
                            pe.wait_ge(xT_s[p].full, xT_s[p].turn(it))
                        pe.wait_ge(project_bank[b].free, project_bank[b].turn(2 * it + p, k))
                    for c in range(half * DC // 2, (half + 1) * DC // 2):
                        last = nc.tensor.matmul(PPS[:, b, :], xT[:, p, c, :], wqkv[:, c, i * BANK:(i + 1) * BANK],
                                                start=(c == 0), stop=(c == DC - 1))
                    if half == 1:
                        last.then_inc(project_bank[b].full, 1)
                    if half == 1 and i == 2:
                        pe.drain().then_inc(xT_s[p].free, 1)

                pe.wait_ge(loaded, 16 * 7)
                pe.wait_ge(made, 3)
                for name in ("xT", "qkv0a", "qkv0b", "qkv1a", "qkv1b", "qkv2a", "qkv2b", "qkT"):
                    project(0, 0, name)
                pe.wait_ge(wo_loaded, 16 * 2)

                def body(it, more):
                    for u in range(A_STREAM):
                        if u < units:
                            p, g = u // KV_HEADS, u % KV_HEADS
                            if g == 0:
                                pe.wait_ge(qkT_s[p].full, qkT_s[p].turn(it))
                            (b, k), = plan.of("scores", u)
                            kc, slot = g // 4, 32 * (g % 4)
                            if u >= 3:
                                pe.wait_ge(probs_done, it * units + (u - 2))
                            nc.tensor.matmul(PS[:, b, :].rearrange("p (r k) -> p r k", r=REP), ident16[:, :],
                                             mask16[:, :].unsqueeze(1).to_broadcast([P, REP, P]),
                                             start=True, stop=False)
                            for r in range(REP):
                                last = nc.tensor.matmul(PS[:, b, r * P:(r + 1) * P],
                                                        qkT[slot:slot + HD, p, kc * REP + r, :],
                                                        qkT[slot:slot + HD, p, D // P + kc, :],
                                                        start=False, stop=(r == REP - 1))
                            last.then_inc(bank[b].full, 1)
                            if g == KV_HEADS - 1:
                                pe.drain().then_inc(qkT_s[p].free, 1)
                        n = u - A_TURN
                        if 0 <= n < units:
                            (b, k), = plan.of("probsT", n)
                            pe.wait_ge(bank[b].free, bank[b].turn(it, k))
                            pe.wait_ge(probs_done, it * units + (n + 1))
                            for r in range(REP):
                                last = nc.tensor.transpose(PS[:, b, r * P:(r + 1) * P], probs[:, n % 3, r, :], ident[:, :])
                            last.then_inc(bank[b].full, 1)
                        n = u - A_MIX
                        if 0 <= n < units:
                            p, g = n // KV_HEADS, n % KV_HEADS
                            (b, k), = plan.of("o", n // HALF)
                            s = probsT_s[n % 2]
                            if g % HALF == 0:
                                pe.wait_ge(bank[b].free, bank[b].turn(it, k))
                            pe.wait_ge(s.full, s.turn(it, n // 2))
                            for r in range(REP):
                                h = (g % HALF) * REP + r
                                last = nc.tensor.matmul(PS[:, b, h * HD:(h + 1) * HD], probsT[:, n % 2, r, :],
                                                        vs[:, p, g * HD:(g + 1) * HD], start=True, stop=True)
                            last.then_inc(s.free, 1)
                            if g % HALF == HALF - 1:
                                pe.drain().then_inc(bank[b].full, 1)
                        for ahead, p, name in dense_work(u, more):
                            if name == "oT":
                                pe.wait_ge(o_s[p].full, o_s[p].turn(it))
                                transpose_chunks(nc, pe, plan.of("oT", p), bank, it, PS, o[:, p, :], ident, DC
                                                 ).then_inc(o_s[p].free, 1)
                            elif name[0] == "y":
                                i, half = int(name[1]), "ab".index(name[2])
                                (b, k), = plan.of(name[0:2], p)
                                if half == 0:
                                    if i == 0:
                                        pe.wait_ge(oT_s[p].full, oT_s[p].turn(it))
                                    pe.wait_ge(bank[b].free, bank[b].turn(it, k))
                                for c in range(half * DC // 2, (half + 1) * DC // 2):
                                    last = nc.tensor.matmul(PS[:, b, :], oT[:, p, c, :], wo[:, c, i * BANK:(i + 1) * BANK],
                                                            start=(c == 0), stop=(c == DC - 1))
                                if half == 1:
                                    last.then_inc(bank[b].full, 1)
                                if half == 1 and i == 1:
                                    pe.drain().then_inc(oT_s[p].free, 1)
                            else:
                                project(it + ahead, p, name)

                each_step(pe, body)
        clear(nc, ctx)



X_HEADS, WINDOW = 8, 16
X_HD = P // X_HEADS
LEFT = WINDOW // 2
NQ = 104
NK = NQ + WINDOW - 1
BLOCKS = 10
assert BLOCKS * NQ >= D
PADDED = (BLOCKS - 1) * NQ + NK
GROUP = 4
UNITS = (BLOCKS // 2) * GROUP
VW = X_HD + 1

TURN = 2
MIX = 3
PROJECT = {"q0": 2, "q1": 3, "k0": 7, "k1": 11, "v0": 12, "v1": 13, "v2": 14}
PROJECT_LATE = {"v0": 21, "v1": 22, "v2": 23}
STREAM = 2 * UNITS + 6


def projections(u):
    late = {n: UNITS + c for n, c in {**PROJECT, **PROJECT_LATE}.items()}
    return [(0, 1, n) for n, c in PROJECT.items() if c == u] + [(1, 0, n) for n, c in late.items() if c == u]


def window_attention(nc, x_in, x_out, ctx_in, w_x, b_x, head_rows, v_row, band, eye):
    with ExitStack() as ctx:
        sb, sem, slots = makers(ctx, nc, "w_")
        PS = ctx.enter_context(nc.psum_tensor("w_ps", [P, 8, BANK], F32))
        w = sb("w", [P, 4, P])
        bias = sb("bias", [P, 3])
        hrows = sb("hrows", [P, X_HEADS])
        hbias = sb("hbias", [P, X_HEADS])
        vrow = sb("vrow", [1, P + PADDED])
        ident = sb("ident", [P, P])
        ident16 = sb("ident16", [P, P], BF16)
        mask = sb("mask", [P, NK])
        mask16 = sb("mask16", [P, NK], BF16)
        norm = Norm(nc, sb, sem, slots, x_in)
        xn = norm.xn
        xt = sb("xt", [P, 2, D])
        cpad = sb("cpad", [P, 2, PADDED])
        kpad = sb("kpad", [P, 2, PADDED])
        q = sb("q", [P, 2, X_HEADS, BLOCKS * NQ])
        vT = sb("vT", [P, 2, BLOCKS, X_HEADS, VW])
        nmax = sb("nmax", [P, 4, 4])
        probs = sb("probs", [P, 3, 4, NK])
        probsT = sb("probsT", [P, 2, 4, NQ])
        rinv = sb("rinv", [P, 2, X_HEADS])
        o = sb("o", [P, 2, 2, P])
        oT = sb("oT", [P, 2, BLOCKS * NQ])

        loaded = sem("loaded")
        made = sem("made")
        x_tile = slots("x", unit=16)
        c_tile = slots("ctx", unit=16)
        qk_s = slots("qk")
        vT_s = slots("vT")
        max_ready = sem("max_ready")
        probs_done = sem("probs_done")
        probsT_s = slots("probsT", uses=UNITS)
        o_ready = sem("o_ready")
        oT_s = slots("oT")
        y_ready = [sem(f"y_ready{p}") for p in range(2)]

        plan = Plan(6)
        ring = 0
        for u in range(STREAM):
            if u < 2 * UNITS:
                plan.add(("scores", u), u % 3)
            if 0 <= u - TURN < 2 * UNITS:
                plan.add(("probsT", u - TURN), 3 + ring % 2)
                ring += 1
            if 0 <= u - MIX < 2 * UNITS and (u - MIX) % GROUP == 0:
                plan.add(("o", (u - MIX) // GROUP), 5)
            i = (u - MIX - GROUP) / GROUP
            if i in range(BLOCKS):
                plan.add(("oT", int(i)), 3 + ring % 2)
                ring += 1
            for p in range(2):
                if u == (p + 1) * UNITS + MIX + 2:
                    plan.add(("y", p), 3 + ring % 2, 3 + (ring + 1) % 2)
                    ring += 2
        bank = [Slot(sem, f"bank{b}", plan.uses[b]) for b in range(6)]
        q_bank = [Slot(sem, "project_bank0", 4), Slot(sem, "project_bank1", 3)]
        PROJECT_BANK = {"q0": (0, 0), "q1": (1, 0), "k0": (0, 1), "k1": (1, 1), "v0": (0, 2), "v1": (1, 2), "v2": (0, 3)}
        LOADS = 16 * 6

        def heads_done(u):
            i = (u - MIX - (GROUP - 1)) / GROUP
            return int(i) if i in range(BLOCKS) else None

        with nc.Block() as block:

            @block.sync
            def _(sp):
                sp.dma_start(ident[:, :], eye).then_inc(loaded, 16)
                sp.dma_start(w[:, :, :], w_x).then_inc(loaded, 16)
                sp.dma_start(bias[:, :], b_x).then_inc(loaded, 16)
                sp.dma_start(hrows[:, :], head_rows).then_inc(loaded, 16)
                sp.dma_start(vrow[:, :], v_row).then_inc(loaded, 16)
                sp.dma_start(mask[:, :], band).then_inc(loaded, 16)
                open_slots(sp, x_tile)
                sp.wait_ge(made, 6)

                def load(it, p):
                    norm.load_one(sp, it, p)
                    sp.wait_ge(c_tile[p].free, c_tile[p].turn(it))
                    sp.dma_start(cpad[:, p, LEFT:LEFT + D], rows(ctx_in, it, p)).then_inc(c_tile[p].full, 16)

                load(0, 0)
                load(0, 1)

                def body(it, more):
                    if more:
                        load(it + 1, 0)
                    for p in range(2):
                        sp.wait_ge(x_tile[p].free, x_tile[p].turn(it))
                        sp.dma_start(xt[:, p, :], rows(x_in, it, p)).then_inc(x_tile[p].full, 16)
                    if more:
                        load(it + 1, 1)
                    for p in range(2):
                        sp.wait_ge(y_ready[p], it + 1)
                        sp.dma_start(rows(x_out, it, p), xt[:, p, :]).then_inc(x_tile[p].free, 16)

                each_step(sp, body)
                for p in range(2):
                    sp.wait_ge(x_tile[p].free, 16 * (PAIRS + 1))

            @block.gpsimd
            def _(pool):
                pool.memset(norm.nhalf[:, :], -0.5).then_inc(made, 1)
                pool.memset(cpad[:, :, :], 0.0).then_inc(made, 1)
                pool.memset(kpad[:, :, :], 0.0).then_inc(made, 1)
                pool.memset(q[:, :, :, BLOCKS * NQ - (BLOCKS * NQ - D):BLOCKS * NQ], 0.0).then_inc(made, 1)
                pool.memset(vT[:, :, :, :, X_HD:VW], 1.0).then_inc(made, 1)
                pool.memset(oT[:, :, :], 0.0).then_inc(made, 1)
                pool.wait_ge(loaded, LOADS)
                pool.tensor_copy(ident16[:, :], ident[:, :]).then_inc(made, 1)
                pool.tensor_copy(mask16[:, :], mask[:, :]).then_inc(made, 1)
                pool.tensor_scalar(hbias[:, :], hrows[:, :], bias[:, 0:1], None, ALU.mult).then_inc(made, 1)
                pool.wait_ge(made, 9)
                norm.pool(pool, 0)
                with pool.Fori(0, PAIRS - 1) as it:
                    norm.pool(pool, it + 1)

            @block.vector
            def _(v):
                open_slots(v, bank[3:] + q_bank)
                open_slots(v, norm.landed + qk_s + vT_s + probsT_s + oT_s + c_tile)
                v.wait_ge(made, 9)
                norm.vector(v, 0)

                def values(it, p, i):
                    if i == 0:
                        v.wait_ge(vT_s[p].free, vT_s[p].turn(it))
                    b, k = PROJECT_BANK[f"v{i}"]
                    m = min(4, BLOCKS - 4 * i)
                    v.wait_ge(q_bank[b].full, q_bank[b].turn(2 * it + p, k))
                    nc.vector.tensor_copy(vT[0:NK, p, 4 * i:4 * i + m, :, 0:X_HD],
                                          PS[0:NK, 6 + b, 0:m * P].rearrange("p (m h d) -> p m h d", m=m, d=X_HD)
                                          ).then_inc(q_bank[b].free, 1)
                    if i == 2:
                        v.drain().then_inc(vT_s[p].full, 1)

                for i in range(3):
                    values(0, 0, i)

                def body(it, more):
                    for u in range(STREAM):
                        if u < 2 * UNITS:
                            (b, k), = plan.of("scores", u)
                            v.wait_ge(bank[b].full, bank[b].turn(it, k))
                            nc.vector.tensor_reduce(nmax[0:NQ, u % 4, :],
                                                    PS[0:NQ, b, 0:4 * NK].rearrange("p (r k) -> p r k", r=4),
                                                    AX.X, ALU.max, negate=True).then_inc(max_ready, 1)
                        n = u - TURN
                        if 0 <= n < 2 * UNITS:
                            (b, k), = plan.of("probsT", n)
                            s = probsT_s[n % 2]
                            v.wait_ge(bank[b].full, bank[b].turn(it, k))
                            v.wait_ge(s.free, s.turn(it, n // 2))
                            nc.vector.tensor_copy(probsT[0:NK, n % 2, :, :].rearrange("p r q -> p (r q)"),
                                                  PS[0:NK, b, 0:4 * NQ]).then_inc(s.full, 1)
                            v.drain().then_inc(bank[b].free, 1)
                        i = heads_done(u)
                        if i is not None:
                            (b, k), = plan.of("o", i)
                            v.wait_ge(bank[b].full, bank[b].turn(it, k))
                            if i >= 2:
                                t_bank, t_k = plan.of("oT", i - 2)[0]
                                v.wait_ge(bank[t_bank].full, bank[t_bank].turn(it, t_k))
                            sums = PS[0:NQ, b, 0:2 * X_HEADS * VW].rearrange("p (m d) -> p m d", d=VW)
                            rv = rinv[0:NQ, :, :].rearrange("p m h -> p (m h)").unsqueeze(2)
                            nc.vector.reciprocal(rv, sums[:, :, X_HD:VW])
                            v.drain()
                            nc.vector.tensor_tensor(o[0:NQ, i % 2, :, :].rearrange("p m (h d) -> p (m h) d", d=X_HD),
                                                    sums[:, :, 0:X_HD], rv.to_broadcast([NQ, 2 * X_HEADS, X_HD]),
                                                    ALU.mult).then_inc(o_ready, 1)
                            v.drain().then_inc(bank[b].free, 1)
                        for ahead, p, name in projections(u - 1):
                            if name[0] == "v" and (more or not ahead):
                                values(it + ahead, p, int(name[1]))
                        if more:
                            for p in range(2):
                                if u == p * UNITS + 6:
                                    norm.stats_one(v, it + 1, p)
                                if u == p * UNITS + 8:
                                    norm.apply_one(v, it + 1, p)
                        for p in range(2):
                            if u == (p + 1) * UNITS + MIX + 2:
                                v.wait_ge(x_tile[p].full, x_tile[p].turn(it))
                                for i, (b, k) in enumerate(plan.of("y", p)):
                                    v.wait_ge(bank[b].full, bank[b].turn(it, k))
                                    part = xt[:, p, i * BANK:(i + 1) * BANK]
                                    nc.vector.scalar_tensor_tensor(part, PS[:, b, :], bias[:, 2:3], part, ALU.add, ALU.add
                                                                   ).then_inc(bank[b].free, 1)
                                v.drain().then_inc(y_ready[p], 1)

                each_step(v, body)

            @block.scalar
            def _(act):
                act.wait_ge(made, 9)

                def queries(it, p, i, first, last):
                    b, k = PROJECT_BANK[f"q{i}"]
                    if first == 0:
                        act.wait_ge(q_bank[b].full, q_bank[b].turn(2 * it + p, k))
                        if i == 0:
                            act.wait_ge(qk_s[p].free, qk_s[p].turn(it))
                    for h in range(first, last):
                        done = nc.scalar.activation(q[:, p, h, i * BANK:(i + 1) * BANK], PS[:, 6 + b, :], ACT.Identity,
                                                    bias=hbias[:, h:h + 1], scale=hrows[:, h:h + 1])
                    if last == X_HEADS:
                        done.then_inc(q_bank[b].free, 1)

                def keys(it, p, i):
                    b, k = PROJECT_BANK[f"k{i}"]
                    act.wait_ge(q_bank[b].full, q_bank[b].turn(2 * it + p, k))
                    nc.scalar.activation(kpad[:, p, LEFT + i * BANK:LEFT + (i + 1) * BANK], PS[:, 6 + b, :], ACT.Identity,
                                         bias=bias[:, 1:2]).then_inc(q_bank[b].free, 1)
                    if i == 1:
                        act.drain().then_inc(qk_s[p].full, 1)

                def project(it, p, turn):
                    if 3 <= turn < 11:
                        i, first = (turn - 3) // 4, (turn - 3) % 4 * 2
                        queries(it, p, i, first, first + 2)
                    if 11 <= turn < 13:
                        keys(it, p, turn - 11)

                for turn in range(3, 13):
                    project(0, 0, turn)

                def body(it, more):
                    for u in range(STREAM):
                        if u < 2 * UNITS:
                            (b, k), = plan.of("scores", u)
                            act.wait_ge(max_ready, it * (2 * UNITS) + (u + 1))
                            if u >= 3:
                                (t_bank, t_k), = plan.of("probsT", u - 3)
                                act.wait_ge(bank[t_bank].full, bank[t_bank].turn(it, t_k))
                            for r in range(4):
                                nc.scalar.activation(probs[0:NQ, u % 3, r, :], PS[0:NQ, b, r * NK:(r + 1) * NK], ACT.Exp,
                                                     bias=nmax[0:NQ, u % 4, r:r + 1])
                            act.drain().then_inc(probs_done, 1)
                        i = heads_done(u - 1)
                        if i is not None:
                            p, j = i // (BLOCKS // 2), i % (BLOCKS // 2)
                            if j == 0:
                                act.wait_ge(oT_s[p].free, oT_s[p].turn(it))
                            (b, k), = plan.of("oT", i)
                            act.wait_ge(bank[b].full, bank[b].turn(it, k))
                            nc.scalar.activation(oT[:, p, 2 * NQ * j:2 * NQ * (j + 1)], PS[:, b, 0:2 * NQ], ACT.Copy
                                                 ).then_inc(bank[b].free, 1)
                            if j == BLOCKS // 2 - 1:
                                act.drain().then_inc(oT_s[p].full, 1)
                        if u < UNITS:
                            project(it, 1, u)
                        elif more:
                            project(it + 1, 0, u - UNITS)

                each_step(act, body)

            @block.tensor
            def _(pe):
                pe.wait_ge(loaded, LOADS)
                pe.wait_ge(made, 9)

                def project(it, p, name):
                    b, k = PROJECT_BANK[name]
                    i = int(name[1])
                    if name == "q0":
                        pe.wait_ge(norm.ready[p], it + 1)
                    if name == "k0":
                        pe.wait_ge(c_tile[p].full, c_tile[p].turn(it))
                    pe.wait_ge(q_bank[b].free, q_bank[b].turn(2 * it + p, k))
                    if name[0] == "q":
                        last = nc.tensor.matmul(PS[:, 6 + b, :], w[:, 0, :], xn[:, p, i * BANK:(i + 1) * BANK],
                                                start=True, stop=True)
                    elif name[0] == "k":
                        t = LEFT + i * BANK
                        last = nc.tensor.matmul(PS[:, 6 + b, :], w[:, 1, :], cpad[:, p, t:t + BANK], start=True, stop=True)
                    else:
                        for m in range(4 * i, min(4 * i + 4, BLOCKS)):
                            out = PS[0:NK, 6 + b, (m % 4) * P:(m % 4 + 1) * P]
                            nc.tensor.matmul(out, cpad[:, p, NQ * m:NQ * m + NK], w[:, 2, :], start=True, stop=False)
                            last = nc.tensor.matmul(out, vrow[0:1, P + NQ * m:P + NQ * m + NK], vrow[0:1, 0:P],
                                                    start=False, stop=True)
                    last.then_inc(q_bank[b].full, 1)
                    if name == "q1":
                        pe.drain().then_inc(norm.landed[p].free, 16)
                    if name == "v2":
                        pe.drain().then_inc(c_tile[p].free, 16)

                for name in PROJECT:
                    project(0, 0, name)

                def body(it, more):
                    for u in range(STREAM):
                        if u < 2 * UNITS:
                            p, j = u // UNITS, u % UNITS
                            if j == 0:
                                pe.wait_ge(qk_s[p].full, qk_s[p].turn(it))
                            (b, k), = plan.of("scores", u)
                            i, pair = j // GROUP, j % GROUP
                            if u >= 3:
                                pe.wait_ge(probs_done, it * (2 * UNITS) + (u - 2))
                            nc.tensor.matmul(PS[0:NQ, b, 0:4 * NK].rearrange("p (r k) -> p r k", r=4), ident16[:, 0:NQ],
                                             mask16[:, :].unsqueeze(1).to_broadcast([P, 4, NK]), start=True, stop=False)
                            for r in range(4):
                                t, h = NQ * (2 * i + r // 2), 2 * pair + r % 2
                                last = nc.tensor.matmul(PS[0:NQ, b, r * NK:(r + 1) * NK], q[:, p, h, t:t + NQ],
                                                        kpad[:, p, t:t + NK], start=False, stop=(r == 3))
                            last.then_inc(bank[b].full, 1)
                            if j == UNITS - 1:
                                pe.drain().then_inc(qk_s[p].free, 1)
                        n = u - TURN
                        if 0 <= n < 2 * UNITS:
                            (b, k), = plan.of("probsT", n)
                            pe.wait_ge(bank[b].free, bank[b].turn(it, k))
                            pe.wait_ge(probs_done, it * (2 * UNITS) + (n + 1))
                            for r in range(4):
                                last = nc.tensor.transpose(PS[0:NK, b, r * NQ:(r + 1) * NQ], probs[0:NQ, n % 3, r, :],
                                            ident[0:NQ, 0:NQ])
                            last.then_inc(bank[b].full, 1)
                        n = u - MIX
                        if 0 <= n < 2 * UNITS:
                            p, j = n // UNITS, n % UNITS
                            i, pair = j // GROUP, j % GROUP
                            (b, k), = plan.of("o", n // GROUP)
                            s = probsT_s[n % 2]
                            if j == 0:
                                pe.wait_ge(vT_s[p].full, vT_s[p].turn(it))
                            if pair == 0:
                                pe.wait_ge(bank[b].free, bank[b].turn(it, k))
                            pe.wait_ge(s.full, s.turn(it, n // 2))
                            for r in range(4):
                                m, h = r // 2, 2 * pair + r % 2
                                c = (m * X_HEADS + h) * VW
                                last = nc.tensor.matmul(PS[0:NQ, b, c:c + VW], probsT[0:NK, n % 2, r, :],
                                                        vT[0:NK, p, 2 * i + m, h, :], start=True, stop=True)
                            last.then_inc(s.free, 1)
                            if pair == GROUP - 1:
                                pe.drain().then_inc(bank[b].full, 1)
                            if j == UNITS - 1:
                                pe.drain().then_inc(vT_s[p].free, 1)
                        i = heads_done(u - 1)
                        if i is not None:
                            (b, k), = plan.of("oT", i)
                            pe.wait_ge(bank[b].free, bank[b].turn(it, k))
                            pe.wait_ge(o_ready, it * BLOCKS + (i + 1))
                            for m in range(2):
                                last = nc.tensor.transpose(PS[:, b, m * NQ:(m + 1) * NQ], o[0:NQ, i % 2, m, :], ident[0:NQ, 0:NQ])
                            last.then_inc(bank[b].full, 1)
                        for ahead, p, name in projections(u):
                            if more or not ahead:
                                project(it + ahead, p, name)
                        for p in range(2):
                            if u == (p + 1) * UNITS + MIX + 2:
                                pe.wait_ge(oT_s[p].full, oT_s[p].turn(it))
                                for i, (b, k) in enumerate(plan.of("y", p)):
                                    pe.wait_ge(bank[b].free, bank[b].turn(it, k))
                                    nc.tensor.matmul(PS[:, b, :], w[:, 3, :], oT[:, p, i * BANK:(i + 1) * BANK],
                                                     start=True, stop=True).then_inc(bank[b].full, 1)
                                pe.drain().then_inc(oT_s[p].free, 1)

                each_step(pe, body)
        clear(nc, ctx)



EXPERTS, RANK, TOP = 64, 16, 16
LORA_SCALE = 2.0
TAKEN = -3.0e38


def lora_mixture(nc, x_in, x_out, w_a, w_b, eye):
    with ExitStack() as ctx:
        sb, sem, slots = makers(ctx, nc, "m_")
        PS = ctx.enter_context(nc.psum_tensor("m_ps", [P, 8, BANK], F32))
        ER = EXPERTS * RANK
        wa = sb("wa", [P, DC, ER + EXPERTS])
        wb = sb("wb", [P, ER // P, D])
        ident = sb("ident", [P, P])
        xr = sb("xr", [P, 2, D])
        xT = sb("xT", [P, 2, DC, P])
        h = sb("h", [P, 2, ER])
        sc = sb("sc", [P, 2, 3, EXPERTS])
        best = sb("best", [P, 2, 16])
        nbest = sb("nbest", [P, 2, 1])
        e = sb("e", [P, 2, EXPERTS])
        gate = sb("gate", [P, 2, EXPERTS])
        gsum = sb("gsum", [P, 2, 2])
        norm = Norm(nc, sb, sem, slots, x_in)

        loaded = sem("loaded")
        made = sem("made")
        x_tile = slots("x", unit=16)
        xT_s = slots("xT", uses=2)
        h_s = slots("h")
        sc_ready = sem("sc_ready")
        e_ready = sem("e_ready")
        y_ready = [sem(f"y_ready{p}") for p in range(2)]

        plan = Plan(8)
        for p in range(2):
            plan.add(("xT", p), 6, 7)
            plan.add(("h", p), 3 * p, 3 * p + 1, 3 * p + 2)
        for p in range(2):
            plan.add(("hT", p), 6, 7)
            plan.add(("y", p), 3 * p, 3 * p + 1)
        bank = [Slot(sem, f"bank{b}", plan.uses[b]) for b in range(8)]
        LOADS = 16 * 5

        with nc.Block() as block:

            @block.sync
            def _(sp):
                sp.dma_start(ident[:, :], eye).then_inc(loaded, 16)
                open_slots(sp, x_tile + norm.landed)
                norm.load(sp, 0)
                wa_rows = w_a.rearrange("(c p) n -> p c n", p=P)
                wb_rows = w_b.rearrange("(c p) n -> p c n", p=P)
                for c in range(0, DC, 4):
                    sp.dma_start(wa[:, c:c + 4, :], wa_rows[:, c:c + 4, :]).then_inc(loaded, 16)
                for c in range(0, DC, 4):
                    sp.dma_start(wb[:, c:c + 4, :], wb_rows[:, c:c + 4, :]).then_inc(loaded, 16)

                def body(it, more):
                    if more:
                        norm.load(sp, it + 1)
                    for p in range(2):
                        sp.wait_ge(x_tile[p].free, x_tile[p].turn(it))
                        sp.dma_start(xr[:, p, :], rows(x_in, it, p)).then_inc(x_tile[p].full, 16)
                    for p in range(2):
                        sp.wait_ge(y_ready[p], it + 1)
                        sp.dma_start(rows(x_out, it, p), xr[:, p, :]).then_inc(x_tile[p].free, 16)

                each_step(sp, body)
                for p in range(2):
                    sp.wait_ge(x_tile[p].free, 16 * (PAIRS + 1))

            @block.gpsimd
            def _(pool):
                pool.memset(norm.nhalf[:, :], -0.5).then_inc(made, 1)
                pool.wait_ge(made, 1)
                norm.pool(pool, 0)
                with pool.Fori(0, PAIRS - 1) as it:
                    norm.pool(pool, it + 1)

            @block.vector
            def _(v):
                open_slots(v, bank)
                open_slots(v, xT_s + h_s)
                norm.vector(v, 0)

                def body(it, more):
                    for p in range(2):
                        scores, left8, left = sc[:, p, 0, :], sc[:, p, 1, :], sc[:, p, 2, :]
                        b, k = plan.of("h", p)[2]
                        v.drain()
                        v.wait_ge(bank[b].full, bank[b].turn(it, k))
                        v.wait_ge(e_ready, 2 * it + p + 1)
                        nc.vector.tensor_copy(scores, PS[:, b, 0:EXPERTS]).then_inc(bank[b].free, 1)
                        v.drain()
                        nc.vector.max(best[:, p, 0:8], scores)
                        v.drain()
                        nc.vector.tensor_scalar(nbest[:, p, :], best[:, p, 0:1], -1.0, None, ALU.mult).then_inc(sc_ready, 1)
                        nc.vector.match_replace(left8, best[:, p, 0:8], scores, TAKEN)
                        v.drain()
                        nc.vector.max(best[:, p, 8:16], left8)
                        v.drain()
                        nc.vector.match_replace(left, best[:, p, 8:16], left8, TAKEN)
                        v.drain()
                        v.wait_ge(e_ready, 2 * it + p + 3)
                        nc.vector.scalar_tensor_tensor(gate[:, p, :], left, TAKEN, e[:, p, :], ALU.is_le, ALU.mult,
                                                       accum_out=gsum[:, p, 0:1])
                        v.drain()
                        nc.vector.reciprocal(gsum[:, p, 1:2], gsum[:, p, 0:1])
                        v.drain()
                        nc.vector.tensor_scalar(gate[:, p, :], gate[:, p, :], gsum[:, p, 1:2], LORA_SCALE, ALU.mult, ALU.mult)
                        v.drain()
                        v.wait_ge(h_s[p].free, h_s[p].turn(it))
                        n = BANK // RANK
                        for i, (b, k) in enumerate(plan.of("h", p)[0:2]):
                            v.wait_ge(bank[b].full, bank[b].turn(it, k))
                            nc.vector.tensor_tensor(h[:, p, i * BANK:(i + 1) * BANK].rearrange("p (e r) -> p e r", r=RANK),
                                                    PS[:, b, :].rearrange("p (e r) -> p e r", r=RANK),
                                                    gate[:, p, i * n:(i + 1) * n].unsqueeze(2).to_broadcast([P, n, RANK]),
                                                    ALU.mult).then_inc(bank[b].free, 1)
                        v.drain().then_inc(h_s[p].full, 1)
                    if more:
                        norm.vector(v, it + 1)
                    for p in range(2):
                        v.wait_ge(x_tile[p].full, x_tile[p].turn(it))
                        for i, (b, k) in enumerate(plan.of("y", p)):
                            v.wait_ge(bank[b].full, bank[b].turn(it, k))
                            part = xr[:, p, i * BANK:(i + 1) * BANK]
                            nc.vector.tensor_tensor(part, part, PS[:, b, :], ALU.add).then_inc(bank[b].free, 1)
                        v.drain().then_inc(y_ready[p], 1)

                each_step(v, body)

            @block.scalar
            def _(act):
                act.nop().then_inc(e_ready, 2)

                def body(it, more):
                    for p in range(2):
                        act.wait_ge(xT_s[p].free, xT_s[p].turn(it, 0))
                        copy_banks(nc, act, plan.of("xT", p), bank, it, PS, xT[:, p, :, :], 4)
                        act.drain().then_inc(xT_s[p].full, 1)
                    for p in range(2):
                        act.wait_ge(sc_ready, 2 * it + p + 1)
                        nc.scalar.activation(e[:, p, :], sc[:, p, 0, :], ACT.Exp, bias=nbest[:, p, :]).then_inc(e_ready, 1)
                    for p in range(2):
                        act.wait_ge(xT_s[p].free, xT_s[p].turn(it, 1))
                        copy_banks(nc, act, plan.of("hT", p), bank, it, PS, xT[:, p, :, :], 4)
                        act.drain().then_inc(xT_s[p].full, 1)

                each_step(act, body)

            @block.tensor
            def _(pe):
                pe.wait_ge(loaded, LOADS)

                def body(it, more):
                    for p in range(2):
                        pe.wait_ge(norm.ready[p], it + 1)
                        transpose_chunks(nc, pe, plan.of("xT", p), bank, it, PS, norm.xn[:, p, :], ident, DC
                                         ).then_inc(norm.landed[p].free, 16)
                        pe.wait_ge(xT_s[p].full, xT_s[p].turn(it, 0))
                        for i, (b, k) in sorted(enumerate(plan.of("h", p)), key=lambda x: -x[0]):
                            n = min(BANK, ER + EXPERTS - i * BANK)
                            pe.wait_ge(bank[b].free, bank[b].turn(it, k))
                            for c in range(DC):
                                last = nc.tensor.matmul(PS[:, b, 0:n], xT[:, p, c, :], wa[:, c, i * BANK:i * BANK + n],
                                                        start=(c == 0), stop=(c == DC - 1))
                            last.then_inc(bank[b].full, 1)
                        pe.drain().then_inc(xT_s[p].free, 1)
                    for p in range(2):
                        pe.wait_ge(h_s[p].full, h_s[p].turn(it))
                        transpose_chunks(nc, pe, plan.of("hT", p), bank, it, PS, h[:, p, :], ident, ER // P).then_inc(h_s[p].free, 1)
                        pe.wait_ge(xT_s[p].full, xT_s[p].turn(it, 1))
                        for i, (b, k) in enumerate(plan.of("y", p)):
                            pe.wait_ge(bank[b].free, bank[b].turn(it, k))
                            for c in range(ER // P):
                                last = nc.tensor.matmul(PS[:, b, :], xT[:, p, c, :], wb[:, c, i * BANK:(i + 1) * BANK],
                                                        start=(c == 0), stop=(c == ER // P - 1))
                            last.then_inc(bank[b].full, 1)
                        pe.drain().then_inc(xT_s[p].free, 1)

                each_step(pe, body)
        clear(nc, ctx)



I = 2752
KEEP = I - int(0.5 * I)
IB = [(i * BANK, min(BANK, I - i * BANK)) for i in range((I + BANK - 1) // BANK)]
IC = [(i * P, min(P, I - i * P)) for i in range((I + P - 1) // P)]
HIGH_BITS, LOW_BITS = 15, 16


ACT_COLS = 1040
DVE_COLS = I - ACT_COLS
UP_BLOCKS = 8
UP = I // UP_BLOCKS
assert UP * UP_BLOCKS == I
DOWN_COLS = len(IC) * D


def sparse_gate(nc, x_in, s_out, u_out, w_gate, w_up, w_down, eye, weights, wd_loaded):
    with ExitStack() as ctx:
        sb, sem, slots = makers(ctx, nc, "g_")
        PS = ctx.enter_context(nc.psum_tensor("g_ps", [P, 8, BANK], F32))
        wg = weights[:, 0:DC * I].rearrange("p (c n) -> p c n", c=DC)
        wu = sb("wu", [P, 2, DC, UP])
        u = sb("u", [P, 2, UP])
        ident = sb("ident", [P, P])
        xT = sb("xT", [P, 2, DC, P])
        s = sb("s", [P, 4, I])
        high = sb("high", [P, 2, I], U16)
        low = sb("low", [P, 2, I], U16)
        spare = sb("spare", [P, 2, DVE_COLS], U16)
        spare_act = sb("spare_act", [P, 2, ACT_COLS], BF16)
        magnitude = sb("magnitude", [P, I])
        small = sb("small", [P, 8, 2])
        trial, upper, counted, signs, excess, short, wanted = (small[:, i, :] for i in range(7))
        thr = sb("thr", [P, 2, 2], U16)
        norm = Norm(nc, sb, sem, slots, x_in)

        loaded = sem("loaded")
        made = sem("made")
        xT_s = slots("xT")
        s_s = slots("s", n=4, unit=16)
        wu_loaded = [sem(f"wu_loaded{b}") for b in range(2)]
        u_stored = [sem(f"u_stored{p}") for p in range(2)]
        gate_done = sem("gate_done")
        trial_ready = sem("trial_ready")
        signs_ready = sem("signs_ready")
        out_ready = [sem(f"out_ready{p}") for p in range(2)]
        COUNTS = HIGH_BITS + 1 + LOW_BITS

        plan = Plan(8)
        for p in range(2):
            plan.add(("xT", p), 2 * p, 2 * p + 1)
        for p in range(2):
            plan.add(("s", p), *[(4 + 6 * p + n) % 8 for n in range(len(IB))])
        for n in range(2 * UP_BLOCKS):
            plan.add(("u", n // 2, n % 2), n % 8)
        widths = [(("s", p, n), IB[n][1]) for p in range(2) for n in range(len(IB))]
        widths += [(("u", n // 2, n % 2), UP) for n in range(2 * UP_BLOCKS)]
        pieces, columns = [[] for n in range(COUNTS)], 0
        for key, width in widths:
            columns += width
            pieces[min(columns * COUNTS // (4 * I), COUNTS - 1)].append(key)
        bank = [Slot(sem, f"bank{b}", plan.uses[b]) for b in range(8)]
        LOADS = 16 * 5

        with nc.Block() as block:

            @block.sync
            def _(sp):
                sp.dma_start(ident[:, :], eye).then_inc(loaded, 16)
                open_slots(sp, norm.landed + s_s)
                norm.load(sp, 0)
                w_rows = w_gate.rearrange("(c p) n -> p c n", p=P)
                for c in range(0, DC, 2):
                    sp.dma_start(wg[:, c:c + 2, :], w_rows[:, c:c + 2, :]).then_inc(loaded, 16)
                norm.load(sp, 1)

                def body(j, i, half, left):
                    if left == 2:
                        norm.load(sp, j + 2)
                    if left == 0:
                        sp.wait_ge(gate_done, 1)
                        load_down(sp, weights, w_down, wd_loaded)
                    for p in range(2):
                        sp.wait_ge(out_ready[p], j + 1)
                        b = 2 * half + p
                        sp.dma_start(rows(s_out, j, p), s[:, b, :]).then_inc(s_s[b].free, 16)

                each_two_steps(sp, body)
                for b in range(4):
                    sp.wait_ge(s_s[b].free, 16 * (PAIRS // 2 + 1))
                for p in range(2):
                    sp.wait_ge(u_stored[p], 16 * (PAIRS * UP_BLOCKS + 1))

            @block.gpsimd
            def _(pool):
                pool.memset(norm.nhalf[:, :], -0.5).then_inc(made, 1)
                pool.wait_ge(made, 1)
                norm.pool(pool, 0)
                with pool.Fori(0, PAIRS - 1) as it:
                    norm.pool(pool, it + 1)

            @block.vector
            def _(v):
                open_slots(v, bank)
                open_slots(v, xT_s)
                norm.vector(v, 0)
                norm.vector(v, 1)

                def count(n):
                    keys = high if n <= HIGH_BITS else low
                    for p in range(2):
                        nc.vector.tensor_scalar(spare[:, p, :], keys[:, p, 0:DVE_COLS], trial[:, p:p + 1], None,
                                                ALU.is_ge, ALU.add, accum_out=counted[:, p:p + 1])

                def search(j, bits, n0):
                    for n in range(bits):
                        bit = 2.0 ** (bits - 1 - n)
                        count(n0 + n)
                        nc.vector.tensor_scalar(upper, trial, bit / 2, None, ALU.add)
                        v.drain()
                        nc.vector.scalar_tensor_tensor(excess, counted, 2.0, wanted, ALU.mult, ALU.subtract)
                        v.drain()
                        v.wait_ge(signs_ready, j * COUNTS + n0 + n + 1)
                        nc.vector.tensor_tensor(short, signs, excess, ALU.is_gt)
                        v.drain()
                        last = nc.vector.scalar_tensor_tensor(trial, short, -bit, upper, ALU.mult, ALU.add)
                        if n < bits - 1:
                            last.then_inc(trial_ready, 1)
                        v.drain()

                def body(j, i, half, left):
                    halves = []
                    for p in range(2):
                        b = s_s[2 * half + p]
                        v.wait_ge(b.full, b.turn(i))
                        halves.append(s[:, 2 * half + p, :].bitcast(U16).rearrange("p (n w) -> p n w", w=2))
                        nc.vector.tensor_scalar(high[:, p, :], halves[p][:, :, 1], 0x7fff, None, ALU.bitwise_and)
                    nc.vector.memset(wanted, float(2 * KEEP - ACT_COLS))
                    nc.vector.memset(trial, 2.0 ** (HIGH_BITS - 1) - 0.5)
                    v.drain().then_inc(trial_ready, 1)
                    search(j, HIGH_BITS, 0)
                    nc.vector.tensor_copy(thr[:, :, 1], trial)
                    nc.vector.tensor_scalar(upper, trial, 0.5, None, ALU.add)
                    for p in range(2):
                        nc.vector.scalar_tensor_tensor(low[:, p, :], high[:, p, :], trial[:, p:p + 1], halves[p][:, :, 0],
                                                       ALU.is_equal, ALU.mult)
                    v.drain()
                    nc.vector.tensor_copy(trial, upper).then_inc(trial_ready, 1)
                    v.drain()
                    count(HIGH_BITS)
                    v.drain()
                    v.wait_ge(signs_ready, j * COUNTS + HIGH_BITS + 1)
                    nc.vector.scalar_tensor_tensor(excess, counted, -2.0, signs, ALU.mult, ALU.add)
                    v.drain()
                    nc.vector.tensor_scalar(wanted, excess, float(2 * KEEP - 2 * ACT_COLS), None, ALU.add)
                    nc.vector.memset(trial, 2.0 ** (LOW_BITS - 1) - 0.5)
                    v.drain().then_inc(trial_ready, 1)
                    if left == 2:
                        norm.vector(v, j + 2)
                    search(j, LOW_BITS, HIGH_BITS + 1)
                    nc.vector.tensor_copy(thr[:, :, 0], trial)
                    v.drain()
                    for p in range(2):
                        part = s[:, 2 * half + p, :]
                        nc.vector.tensor_scalar(magnitude[:, :].bitcast(U32), part.bitcast(U32), 0x7fffffff,
                                                None, ALU.bitwise_and)
                        v.drain()
                        nc.vector.scalar_tensor_tensor(part, magnitude[:, :], thr[:, p, :].bitcast(F32), part,
                                                       ALU.is_ge, ALU.mult).then_inc(out_ready[p], 1)
                        v.drain()

                each_two_steps(v, body)

            @block.scalar
            def _(act):
                up_rows = w_up.rearrange("(c p) n -> p c n", p=P)

                def load_up(block):
                    act.dma_start(wu[:, block % 2, :, :], up_rows[:, :, block * UP:(block + 1) * UP]
                                  ).then_inc(wu_loaded[block % 2], 16)

                def x_turned(j):
                    for p in range(2):
                        act.wait_ge(xT_s[p].free, xT_s[p].turn(j))
                        copy_banks(nc, act, plan.of("xT", p), bank, j, PS, xT[:, p, :, :], 4)
                        act.drain().then_inc(xT_s[p].full, 1)
                    for block in range(2):
                        load_up(block)

                def piece(j, i, half, kind, first, second):
                    if kind == "s":
                        p, n = first, second
                        b, k = plan.of("s", p)[n]
                        c, m = IB[n]
                        slot = s_s[2 * half + p]
                        if n == 0:
                            act.wait_ge(slot.free, slot.turn(i))
                        act.wait_ge(bank[b].full, bank[b].turn(j, k))
                        nc.scalar.activation(s[:, 2 * half + p, c:c + m], PS[:, b, 0:m], ACT.Silu).then_inc(bank[b].free, 1)
                        if n == len(IB) - 1:
                            act.drain().then_inc(slot.full, 16)
                    else:
                        block, p = first, second
                        (b, k), = plan.of("u", block, p)
                        act.wait_ge(bank[b].full, bank[b].turn(j, k))
                        act.wait_ge(u_stored[p], 16 * (j * UP_BLOCKS + (block + 1)))
                        nc.scalar.activation(u[:, p, :], PS[:, b, 0:UP], ACT.Copy).then_inc(bank[b].free, 1)
                        act.drain()
                        act.dma_start(rows(u_out, j, p)[:, block * UP:(block + 1) * UP], u[:, p, :]).then_inc(u_stored[p], 16)
                        if p == 1 and block + 2 < UP_BLOCKS:
                            load_up(block + 2)

                for p in range(2):
                    act.nop().then_inc(u_stored[p], 16)
                x_turned(0)
                for key in sum(pieces, []):
                    piece(0, 0, 0, *key)

                def body(j, i, half, left):
                    if left:
                        x_turned(j + 1)
                    for n in range(COUNTS):
                        keys = high if n <= HIGH_BITS else low
                        act.wait_ge(trial_ready, j * COUNTS + n + 1)
                        for p in range(2):
                            nc.scalar.activation(spare_act[:, p, :], keys[:, p, DVE_COLS:I], ACT.Sign, scale=-1.0,
                                                 bias=trial[:, p:p + 1], accum_out=signs[:, p:p + 1])
                        act.drain().then_inc(signs_ready, 1)
                        if left:
                            for key in pieces[n]:
                                piece(j + 1, i + half, 1 - half, *key)

                each_two_steps(act, body)

            @block.tensor
            def _(pe):
                pe.wait_ge(loaded, LOADS)

                def body(j, more):
                    for p in range(2):
                        pe.wait_ge(norm.ready[p], j + 1)
                        transpose_chunks(nc, pe, plan.of("xT", p), bank, j, PS, norm.xn[:, p, :], ident, DC
                                         ).then_inc(norm.landed[p].free, 16)
                    for p in range(2):
                        pe.wait_ge(xT_s[p].full, xT_s[p].turn(j))
                        for (b, k), (i, n) in zip(plan.of("s", p), IB):
                            pe.wait_ge(bank[b].free, bank[b].turn(j, k))
                            for c in range(DC):
                                last = nc.tensor.matmul(PS[:, b, 0:n], xT[:, p, c, :], wg[:, c, i:i + n],
                                                        start=(c == 0), stop=(c == DC - 1))
                            last.then_inc(bank[b].full, 1)
                    if not more:
                        pe.drain().then_inc(gate_done, 1)
                    for block in range(UP_BLOCKS):
                        pe.wait_ge(wu_loaded[block % 2], 16 * (j * (UP_BLOCKS // 2) + (block // 2 + 1)))
                        for p in range(2):
                            (b, k), = plan.of("u", block, p)
                            pe.wait_ge(bank[b].free, bank[b].turn(j, k))
                            for c in range(DC):
                                last = nc.tensor.matmul(PS[:, b, 0:UP], xT[:, p, c, :], wu[:, block % 2, c, :],
                                                        start=(c == 0), stop=(c == DC - 1))
                            last.then_inc(bank[b].full, 1)
                    for p in range(2):
                        pe.drain().then_inc(xT_s[p].free, 1)

                each_step(pe, body)
        clear(nc, ctx)


def load_down(sp, weights, w_down, wd_loaded):
    wd = weights[:, :].rearrange("p (c n) -> p c n", n=D)
    full = I // P
    d_rows = w_down[0:full * P, :].rearrange("(c p) n -> p c n", p=P)
    for c in range(0, full, 7):
        sp.dma_start(wd[:, c:c + 7, :], d_rows[:, c:c + 7, :]).then_inc(wd_loaded, 16)
    sp.dma_start(wd[0:I - full * P, full, :], w_down[full * P:I, :]).then_inc(wd_loaded, 16)


DOWN_LOADS = 16 * (I // P // 7 + 1)
assert I // P % 7 == 0



def sparse_ffn(nc, x_in, s_in, u_in, x_out, eye, weights, wd_loaded):
    with ExitStack() as ctx:
        sb, sem, slots = makers(ctx, nc, "f_")
        PS = ctx.enter_context(nc.psum_tensor("f_ps", [P, 8, BANK], F32))
        wd = weights[:, :].rearrange("p (c n) -> p c n", n=D)
        ident = sb("ident", [P, P])
        s = sb("s", [P, 2, I])
        u = sb("u", [P, 2, I])
        sT = sb("sT", [P, 2, len(IC), P])
        xr = sb("xr", [P, 2, D])

        loaded = sem("loaded")
        x_tile = slots("x", unit=16)
        s_tile = slots("s", unit=32)
        h_ready = sem("h_ready")
        sT_s = slots("sT")
        y_ready = [sem(f"y_ready{p}") for p in range(2)]

        plan = Plan(4)
        for p in range(2):
            plan.add(("y", p), 2 * p, 2 * p + 1)
        bank = [Slot(sem, f"bank{b}", plan.uses[b]) for b in range(4)]
        turn_plan = Plan(3)
        turn_plan.add(("sT",), 0, 1, 2, 0, 1, 2)
        turn_bank = [Slot(sem, f"turn_bank{b}", turn_plan.uses[b]) for b in range(3)]
        TPS = PS[:, 4:7, :]

        def ahead(engine, work, others):
            work(0, 0)

            def body(it, more):
                work(it, 1)
                others(it, 0)
                if more:
                    work(it + 1, 0)
                others(it, 1)

            each_step(engine, body)

        with nc.Block() as block:

            @block.sync
            def _(sp):
                sp.dma_start(ident[:, :], eye).then_inc(loaded, 16)
                open_slots(sp, x_tile + s_tile)

                def load_gate(it, p):
                    sp.wait_ge(s_tile[p].free, s_tile[p].turn(it))
                    sp.dma_start(s[:, p, :], rows(s_in, it, p)).then_inc(s_tile[p].full, 16)
                    sp.dma_start(u[:, p, :], rows(u_in, it, p)).then_inc(s_tile[p].full, 16)

                def load_x(it, p):
                    sp.wait_ge(x_tile[p].free, x_tile[p].turn(it))
                    sp.dma_start(xr[:, p, :], rows(x_in, it, p)).then_inc(x_tile[p].full, 16)

                def store(it, p):
                    sp.wait_ge(y_ready[p], it + 1)
                    sp.dma_start(rows(x_out, it, p), xr[:, p, :]).then_inc(x_tile[p].free, 16)

                for p in range(2):
                    load_gate(0, p)
                    load_x(0, p)

                def body(it, more):
                    for p in range(2):
                        if more:
                            load_gate(it + 1, p)
                        store(it, p)
                        if more:
                            load_x(it + 1, p)

                each_step(sp, body)
                for p in range(2):
                    sp.wait_ge(x_tile[p].free, 16 * (PAIRS + 1))

            @block.vector
            def _(v):
                open_slots(v, bank + turn_bank + sT_s)

                def gate(it, p):
                    v.wait_ge(s_tile[p].full, s_tile[p].turn(it))
                    nc.vector.tensor_tensor(s[:, p, :], s[:, p, :], u[:, p, :], ALU.mult).then_inc(h_ready, 1)

                def add(it, p):
                    v.wait_ge(x_tile[p].full, x_tile[p].turn(it))
                    for i, (b, k) in enumerate(plan.of("y", p)):
                        v.wait_ge(bank[b].full, bank[b].turn(it, k))
                        part = xr[:, p, i * BANK:(i + 1) * BANK]
                        nc.vector.tensor_tensor(part, part, PS[:, b, :], ALU.add).then_inc(bank[b].free, 1)
                    v.drain().then_inc(y_ready[p], 1)

                gate(0, 0)
                gate(0, 1)

                def body(it, more):
                    for p in range(2):
                        if more:
                            gate(it + 1, p)
                        add(it, p)

                each_step(v, body)

            @block.scalar
            def _(act):
                def copies(it, p):
                    act.wait_ge(sT_s[p].free, sT_s[p].turn(it))
                    for j, (b, k) in enumerate(turn_plan.of("sT")):
                        c, m = 4 * j, min(4, I // P - 4 * j)
                        act.wait_ge(turn_bank[b].full, turn_bank[b].turn(2 * it + p, k))
                        if m < 4:
                            q = I - (I // P) * P
                            nc.scalar.activation(sT[0:q, p, c + m, :], TPS[0:q, b, m * P:(m + 1) * P], ACT.Copy)
                        nc.scalar.activation(sT[:, p, c:c + m, :], TPS[:, b, 0:m * P].rearrange("p (c t) -> p c t", c=m),
                                             ACT.Copy)
                        act.drain().then_inc(turn_bank[b].free, 1)
                    act.drain().then_inc(sT_s[p].full, 1)

                ahead(act, copies, lambda it, p: None)

            @block.tensor
            def _(pe):
                def transposes(it, p):
                    pe.wait_ge(h_ready, 2 * it + p + 1)
                    for j, (b, k) in enumerate(turn_plan.of("sT")):
                        pe.wait_ge(turn_bank[b].free, turn_bank[b].turn(2 * it + p, k))
                        for c in range(4 * j, min(4 * j + 4, len(IC))):
                            i, n = IC[c]
                            last = nc.tensor.transpose(TPS[0:n, b, (c % 4) * P:(c % 4 + 1) * P], s[:, p, i:i + n], ident[:, :])
                        last.then_inc(turn_bank[b].full, 1)
                    pe.drain().then_inc(s_tile[p].free, 32)

                def down(it, p):
                    pe.wait_ge(sT_s[p].full, sT_s[p].turn(it))
                    for j, (b, k) in enumerate(plan.of("y", p)):
                        pe.wait_ge(bank[b].free, bank[b].turn(it, k))
                        for c, (i, n) in enumerate(IC):
                            last = nc.tensor.matmul(PS[:, b, :], sT[0:n, p, c, :], wd[0:n, c, j * BANK:(j + 1) * BANK],
                                                    start=(c == 0), stop=(c == len(IC) - 1))
                        last.then_inc(bank[b].full, 1)
                    pe.drain().then_inc(sT_s[p].free, 1)

                pe.wait_ge(loaded, 16)
                pe.wait_ge(wd_loaded, DOWN_LOADS)
                ahead(pe, transposes, down)
        clear(nc, ctx)
        nc.sync.sem_clear(wd_loaded)
        nc.all_engine_barrier()



LAGS = P
TOPLAGS = 9
Q1, Q2, K1, K2 = range(4)
VE1, VE2, VO1, VO2, WE1, WE2, WO1, WO2 = range(4, 12)
INV, INV_E, INV_O = range(12, 15)
MATRICES = 15


def autocorrelation(nc, x_in, x_out, ctx_in, dft, eye):
    with ExitStack() as ctx:
        sb, sem, slots = makers(ctx, nc, "c_")
        PS = ctx.enter_context(nc.psum_tensor("c_ps", [P, 8, BANK], F32))
        mats = sb("mats", [P, MATRICES, P])
        ident = sb("ident", [P, P])
        xr = sb("xr", [P, 2, D])
        kv = sb("kv", [P, 2, D])
        kf = sb("kf", [P, 2, D])
        prod = sb("prod", [P, 2, 2, D])
        vf = sb("vf", [P, 2, 4, D])
        wprod = sb("wprod", [P, 4, D])
        wT = sb("wT", [P, D])
        best = sb("best", [P, DC, 8])
        ninth = sb("ninth", [P, DC, 8])
        late = sb("late", [P, DC, 8])
        nbest = sb("nbest", [P, 2, DC])
        left = sb("left", [P, 2, DC, LAGS])
        corr = sb("corr", [P, 2, DC, LAGS])
        e = sb("e", [P, 2, DC, LAGS])
        wsum = sb("wsum", [P, 2, DC])
        norm = Norm(nc, sb, sem, slots, x_in)

        loaded = sem("loaded")
        made = sem("made")
        x_tile = slots("x", unit=16)
        kv_tile = slots("kv", unit=16)
        kf_s, = slots("kf", uses=2, n=1)
        prod_s = slots("prod")
        vf_s = slots("vf")
        corr_s = slots("corr")
        nbest_ready = sem("nbest_ready")
        e_ready = sem("e_ready")
        w_s = slots("w")
        wT_s, = slots("wT", uses=2, n=1)
        wprod_s, = slots("wprod", uses=2, n=1)
        y_ready = [sem(f"y_ready{p}") for p in range(2)]

        A, B, C, E = (0, 1), (2, 3), (4, 5), (6, 7)
        plan = Plan(8)
        for p in range(2):
            for i, (name, pair) in enumerate([("k", A), ("k", B), ("q", C), ("q", E)]):
                plan.add((name, p, i % 2), *pair)
        for p in range(2):
            plan.add(("corr", p), *(A, B)[p])
        for p in range(2):
            for i in range(4):
                plan.add(("v", p, i), *(C, E)[i % 2])
        for p in range(2):
            plan.add(("wT", p), *(C, B)[p])
            for i in range(4):
                plan.add(("w", p, i), *((E, A, C, E), (C, E, A, B))[p][i])
            plan.add(("y", p), *(A, C)[p])
        bank = [Slot(sem, f"bank{b}", plan.uses[b]) for b in range(8)]
        LOADS = 16 * 2

        with nc.Block() as block:

            @block.sync
            def _(sp):
                sp.dma_start(mats[:, :, :], dft).then_inc(loaded, 16)
                sp.dma_start(ident[:, :], eye).then_inc(loaded, 16)
                open_slots(sp, x_tile + norm.landed)
                norm.load(sp, 0)

                def body(it, more):
                    for p in range(2):
                        sp.wait_ge(kv_tile[p].free, kv_tile[p].turn(it))
                        sp.dma_start(kv[:, p, :], rows(ctx_in, it, p)).then_inc(kv_tile[p].full, 16)
                    if more:
                        norm.load(sp, it + 1)
                    for p in range(2):
                        sp.wait_ge(x_tile[p].free, x_tile[p].turn(it))
                        sp.dma_start(xr[:, p, :], rows(x_in, it, p)).then_inc(x_tile[p].full, 16)
                    for p in range(2):
                        sp.wait_ge(y_ready[p], it + 1)
                        sp.dma_start(rows(x_out, it, p), xr[:, p, :]).then_inc(x_tile[p].free, 16)

                each_step(sp, body)
                for p in range(2):
                    sp.wait_ge(x_tile[p].free, 16 * (PAIRS + 1))

            @block.gpsimd
            def _(pool):
                pool.memset(norm.nhalf[:, :], -0.5).then_inc(made, 1)
                pool.wait_ge(made, 1)
                norm.pool(pool, 0)
                with pool.Fori(0, PAIRS - 1) as it:
                    norm.pool(pool, it + 1)

            @block.vector
            def _(v):
                open_slots(v, bank)
                open_slots(v, kv_tile + prod_s + corr_s + vf_s + w_s + [kf_s, wT_s, wprod_s])
                norm.vector(v, 0)

                def body(it, more):
                    for p in range(2):
                        v.wait_ge(kf_s.full, kf_s.turn(it, p))
                        v.wait_ge(prod_s[p].free, prod_s[p].turn(it))
                        for i in range(2):
                            for j, (b, k) in enumerate(plan.of("q", p, i)):
                                t = slice(j * BANK, (j + 1) * BANK)
                                v.wait_ge(bank[b].full, bank[b].turn(it, k))
                                nc.vector.tensor_tensor(prod[:, p, i, t], PS[:, b, :], kf[:, i, t], ALU.mult
                                                        ).then_inc(bank[b].free, 1)
                        v.drain().then_inc(prod_s[p].full, 1)
                        v.drain().then_inc(kf_s.free, 1)
                    for p in range(2):
                        v.wait_ge(corr_s[p].full, corr_s[p].turn(it))
                        v.wait_ge(w_s[p].free, w_s[p].turn(it))
                        nc.vector.memset(late[:, :, 1:8], TAKEN)
                        for c in range(DC):
                            nc.vector.max(best[:, c, :], corr[:, p, c, :])
                        v.drain()
                        nc.vector.tensor_scalar(nbest[:, p, :], best[:, :, 0], -1.0, None, ALU.mult).then_inc(nbest_ready, 1)
                        for c in range(DC):
                            nc.vector.match_replace(left[:, p, c, :], best[:, c, :], corr[:, p, c, :], TAKEN)
                        v.drain()
                        for c in range(DC):
                            nc.vector.max(ninth[:, c, :], left[:, p, c, :])
                        v.drain()
                        nc.vector.tensor_copy(late[:, :, 0], ninth[:, :, 0])
                        v.drain()
                        for c in range(DC):
                            nc.vector.match_replace(left[:, p, c, :], late[:, c, :], left[:, p, c, :], TAKEN)
                        v.drain()
                        v.wait_ge(e_ready, 2 * it + p + 1)
                        lf = left[:, p, :, :].rearrange("p c n -> p (c n)")
                        nc.vector.scalar_tensor_tensor(lf, lf, TAKEN, e[:, p, :, :].rearrange("p c n -> p (c n)"),
                                                       ALU.is_le, ALU.mult)
                        v.drain().then_inc(corr_s[p].free, 1)
                        nc.vector.tensor_reduce(wsum[:, p, :], left[:, p, :, :], AX.X, ALU.add)
                        v.drain()
                        nc.vector.reciprocal(wsum[:, p, :], wsum[:, p, :])
                        v.drain()
                        nc.vector.tensor_tensor(left[:, p, :, :], left[:, p, :, :],
                                                wsum[:, p, :].unsqueeze(2).to_broadcast([P, DC, LAGS]), ALU.mult
                                                ).then_inc(w_s[p].full, 1)
                    for p in range(2):
                        v.wait_ge(vf_s[p].full, vf_s[p].turn(it))
                        v.wait_ge(wprod_s.free, wprod_s.turn(it, p))
                        for i in range(4):
                            for j, (b, k) in enumerate(plan.of("w", p, i)):
                                t = slice(j * BANK, (j + 1) * BANK)
                                v.wait_ge(bank[b].full, bank[b].turn(it, k))
                                nc.vector.tensor_tensor(wprod[:, i, t], PS[:, b, :], vf[:, p, i, t], ALU.mult
                                                        ).then_inc(bank[b].free, 1)
                        v.drain().then_inc(wprod_s.full, 1)
                        v.drain().then_inc(vf_s[p].free, 1)
                        if more and p == 0:
                            norm.vector(v, it + 1)
                        v.wait_ge(x_tile[p].full, x_tile[p].turn(it))
                        for i, (b, k) in enumerate(plan.of("y", p)):
                            v.wait_ge(bank[b].full, bank[b].turn(it, k))
                            part = xr[:, p, i * BANK:(i + 1) * BANK]
                            nc.vector.tensor_tensor(part, part, PS[:, b, :], ALU.add).then_inc(bank[b].free, 1)
                        v.drain().then_inc(y_ready[p], 1)

                each_step(v, body)

            @block.scalar
            def _(act):
                def body(it, more):
                    def evacuate(banks, out):
                        for j, (b, k) in enumerate(banks):
                            act.wait_ge(bank[b].full, bank[b].turn(it, k))
                            nc.scalar.activation(out[:, j * BANK:(j + 1) * BANK], PS[:, b, :], ACT.Copy).then_inc(bank[b].free, 1)

                    for p in range(2):
                        act.wait_ge(kf_s.free, kf_s.turn(it, p))
                        for i in range(2):
                            evacuate(plan.of("k", p, i), kf[:, i, :])
                        act.drain().then_inc(kf_s.full, 1)

                    def exps(p):
                        act.wait_ge(nbest_ready, 2 * it + p + 1)
                        act.wait_ge(w_s[p].free, w_s[p].turn(it))
                        for c in range(DC):
                            nc.scalar.activation(e[:, p, c, :], corr[:, p, c, :], ACT.Exp, bias=nbest[:, p, c:c + 1])
                        act.drain().then_inc(e_ready, 1)

                    def spectrum(p):
                        act.wait_ge(vf_s[p].free, vf_s[p].turn(it))
                        for i in range(4):
                            evacuate(plan.of("v", p, i), vf[:, p, i, :])
                        act.drain().then_inc(vf_s[p].full, 1)

                    for p in range(2):
                        act.wait_ge(corr_s[p].free, corr_s[p].turn(it))
                        evacuate(plan.of("corr", p), corr[:, p, :, :].rearrange("p c n -> p (c n)"))
                        act.drain().then_inc(corr_s[p].full, 1)
                    spectrum(0)
                    exps(0)
                    spectrum(1)
                    exps(1)
                    for p in range(2):
                        act.wait_ge(wT_s.free, wT_s.turn(it, p))
                        evacuate(plan.of("wT", p), wT[:, :])
                        act.drain().then_inc(wT_s.full, 1)

                each_step(act, body)

            @block.tensor
            def _(pe):
                pe.wait_ge(loaded, LOADS)

                def body(it, more):
                    def transform(banks, matrices, srcs):
                        for j, (b, k) in enumerate(banks):
                            pe.wait_ge(bank[b].free, bank[b].turn(it, k))
                            for n, (m, src) in enumerate(zip(matrices, srcs)):
                                last = nc.tensor.matmul(PS[:, b, :], mats[:, m, :], src[:, j * BANK:(j + 1) * BANK],
                                                        start=(n == 0), stop=(n == len(srcs) - 1))
                            last.then_inc(bank[b].full, 1)

                    for p in range(2):
                        pe.wait_ge(kv_tile[p].full, kv_tile[p].turn(it))
                        for i in range(2):
                            transform(plan.of("k", p, i), [K1 + i], [kv[:, p, :]])
                        pe.wait_ge(norm.ready[p], it + 1)
                        for i in range(2):
                            transform(plan.of("q", p, i), [Q1 + i], [norm.xn[:, p, :]])
                        pe.drain().then_inc(norm.landed[p].free, 16)
                    for p in range(2):
                        pe.wait_ge(prod_s[p].full, prod_s[p].turn(it))
                        for j, (b, k) in enumerate(plan.of("corr", p)):
                            pe.wait_ge(bank[b].free, bank[b].turn(it, k))
                            for c in range(4 * j, 4 * j + 4):
                                for i in range(2):
                                    last = nc.tensor.matmul(PS[:, b, (c % 4) * P:(c % 4 + 1) * P],
                                                            prod[:, p, i, c * P:(c + 1) * P], mats[:, INV, :],
                                                            start=(i == 0), stop=(i == 1))
                            last.then_inc(bank[b].full, 1)
                        pe.drain().then_inc(prod_s[p].free, 1)
                    for p in range(2):
                        for i in range(4):
                            transform(plan.of("v", p, i), [VE1 + i], [kv[:, p, :]])
                        pe.drain().then_inc(kv_tile[p].free, 16)
                    for p in range(2):
                        pe.wait_ge(w_s[p].full, w_s[p].turn(it))
                        transpose_chunks(nc, pe, plan.of("wT", p), bank, it, PS,
                                         left[:, p, :, :].rearrange("p c n -> p (c n)"), ident, DC).then_inc(w_s[p].free, 1)
                        pe.wait_ge(wT_s.full, wT_s.turn(it, p))
                        for i in range(4):
                            transform(plan.of("w", p, i), [WE1 + i], [wT[:, :]])
                        pe.drain().then_inc(wT_s.free, 1)
                        pe.wait_ge(wprod_s.full, wprod_s.turn(it, p))
                        transform(plan.of("y", p), [INV_E, INV_E, INV_O, INV_O], [wprod[:, i, :] for i in range(4)])
                        pe.drain().then_inc(wprod_s.free, 1)

                each_step(pe, body)
        clear(nc, ctx)



ROUTED, R = 8, 16
ER = ROUTED * R


def routed_linear(nc, x_in, x_out, w_base, w_la, w_lb, b_base, b_router, eye):
    with ExitStack() as ctx:
        sb, sem, slots = makers(ctx, nc, "r_")
        PS = ctx.enter_context(nc.psum_tensor("r_ps", [P, 8, BANK], F32))
        wb = sb("wb", [P, DC, D])
        wa = sb("wa", [P, DC, ER + ROUTED])
        wlb = sb("wlb", [P, D])
        ident = sb("ident", [P, P])
        bb = sb("bb", [P, D])
        br = sb("br", [P, ROUTED])
        xr = sb("xr", [P, 2, D])
        xT = sb("xT", [P, 2, DC, P])
        z = sb("z", [P, 2, ROUTED])
        runs = sb("runs", [P, 4, 4 + ROUTED])
        inv_k = sb("inv_k", [P, ROUTED])
        tau = sb("tau", [P, 2, 1])
        gate = sb("gate", [P, 2, ROUTED])
        h = sb("h", [P, 2, ER])
        hT = sb("hT", [P, 2, P])
        norm = Norm(nc, sb, sem, slots, x_in)

        loaded = sem("loaded")
        made = sem("made")
        x_tile = slots("x", unit=16)
        biased = [sem(f"biased{p}") for p in range(2)]
        xT_s = slots("xT")
        h_s = slots("h")
        hT_s = slots("hT")
        y_ready = [sem(f"y_ready{p}") for p in range(2)]

        plan = Plan(8)
        for p in range(2):
            plan.add(("xT", p), 6, 7)
            plan.add(("h", p), 2 + 3 * p)
            plan.add(("y", p), 3 * p, 3 * p + 1)
            plan.add(("hT", p), 6)
        bank = [Slot(sem, f"bank{b}", plan.uses[b]) for b in range(8)]
        LOADS = 16 * 9

        with nc.Block() as block:

            @block.sync
            def _(sp):
                sp.dma_start(ident[:, :], eye).then_inc(loaded, 16)
                open_slots(sp, x_tile + norm.landed)
                norm.load(sp, 0)
                sp.dma_start(wa[:, :, :], w_la.rearrange("(c p) n -> p c n", p=P)).then_inc(loaded, 16)
                w_rows = w_base.rearrange("(c p) n -> p c n", p=P)
                for c in range(0, DC, 2):
                    sp.dma_start(wb[:, c:c + 2, :], w_rows[:, c:c + 2, :]).then_inc(loaded, 16)
                sp.dma_start(wlb[:, :], w_lb).then_inc(loaded, 16)
                sp.dma_start(bb[:, :], b_base.to_broadcast([P, D])).then_inc(loaded, 16)
                sp.dma_start(br[:, :], b_router.to_broadcast([P, ROUTED])).then_inc(loaded, 16)

                def body(it, more):
                    if more:
                        norm.load(sp, it + 1)
                    for p in range(2):
                        sp.wait_ge(x_tile[p].free, x_tile[p].turn(it))
                        sp.dma_start(xr[:, p, :], rows(x_in, it, p)).then_inc(x_tile[p].full, 16)
                    for p in range(2):
                        sp.wait_ge(y_ready[p], it + 1)
                        sp.dma_start(rows(x_out, it, p), xr[:, p, :]).then_inc(x_tile[p].free, 16)

                each_step(sp, body)
                for p in range(2):
                    sp.wait_ge(x_tile[p].free, 16 * (PAIRS + 1))

            @block.gpsimd
            def _(pool):
                pool.memset(norm.nhalf[:, :], -0.5).then_inc(made, 1)
                pool.memset(runs[:, :, :], 0.0).then_inc(made, 1)
                for k in range(ROUTED):
                    pool.memset(inv_k[:, k:k + 1], 1.0 / (k + 1)).then_inc(made, 1)
                pool.wait_ge(made, 2 + ROUTED)
                norm.pool(pool, 0)
                pool.wait_ge(loaded, LOADS)

                def body(it, more):
                    for p in range(2):
                        pool.wait_ge(x_tile[p].full, x_tile[p].turn(it))
                        pool.tensor_tensor(xr[:, p, :], xr[:, p, :], bb[:, :], ALU.add).then_inc(biased[p], 1)
                    if more:
                        norm.pool(pool, it + 1)

                each_step(pool, body)

            @block.vector
            def _(v):
                open_slots(v, bank)
                open_slots(v, xT_s + h_s + hT_s)
                v.wait_ge(made, 2 + ROUTED)
                norm.vector(v, 0)
                v.wait_ge(loaded, LOADS)

                def body(it, more):
                    for p in range(2):
                        (b, k), = plan.of("h", p)
                        v.wait_ge(bank[b].full, bank[b].turn(it, k))
                        nc.vector.tensor_tensor(z[:, p, :], PS[:, b, ER:ER + ROUTED], br[:, :], ALU.add)
                        v.drain()
                        nc.vector.max(runs[:, 0, 4:4 + ROUTED], z[:, p, :])
                        v.drain()
                        for i in range(3):
                            d = 4 - 2 ** i
                            nc.vector.tensor_tensor(runs[:, i + 1, 4:4 + ROUTED], runs[:, i, 4:4 + ROUTED],
                                                    runs[:, i, d:d + ROUTED], ALU.add)
                            v.drain()
                        nc.vector.scalar_tensor_tensor(runs[:, 0, 4:4 + ROUTED], runs[:, 3, 4:4 + ROUTED], -1.0, inv_k[:, :],
                                                       ALU.add, ALU.mult)
                        v.drain()
                        nc.vector.tensor_reduce(tau[:, p, :], runs[:, 0, 4:4 + ROUTED], AX.X, ALU.max)
                        v.drain()
                        nc.vector.tensor_scalar(gate[:, p, :], z[:, p, :], tau[:, p, :], 0.0, ALU.subtract, ALU.max)
                        v.drain()
                        v.wait_ge(h_s[p].free, h_s[p].turn(it))
                        nc.vector.tensor_tensor(h[:, p, :].rearrange("p (e r) -> p e r", r=R),
                                                PS[:, b, 0:ER].rearrange("p (e r) -> p e r", r=R),
                                                gate[:, p, :].unsqueeze(2).to_broadcast([P, ROUTED, R]), ALU.mult
                                                ).then_inc(h_s[p].full, 1)
                        v.drain().then_inc(bank[b].free, 1)
                    if more:
                        norm.vector(v, it + 1)
                    for p in range(2):
                        v.wait_ge(biased[p], it + 1)
                        for i, (b, k) in enumerate(plan.of("y", p)):
                            v.wait_ge(bank[b].full, bank[b].turn(it, k))
                            part = xr[:, p, i * BANK:(i + 1) * BANK]
                            nc.vector.tensor_tensor(part, part, PS[:, b, :], ALU.add).then_inc(bank[b].free, 1)
                        v.drain().then_inc(y_ready[p], 1)

                each_step(v, body)

            @block.scalar
            def _(act):
                def body(it, more):
                    for p in range(2):
                        act.wait_ge(xT_s[p].free, xT_s[p].turn(it))
                        copy_banks(nc, act, plan.of("xT", p), bank, it, PS, xT[:, p, :, :], 4)
                        act.drain().then_inc(xT_s[p].full, 1)
                        (b, k), = plan.of("hT", p)
                        act.wait_ge(hT_s[p].free, hT_s[p].turn(it))
                        act.wait_ge(bank[b].full, bank[b].turn(it, k))
                        nc.scalar.activation(hT[:, p, :], PS[:, b, 0:P], ACT.Copy).then_inc(bank[b].free, 1)
                        act.drain().then_inc(hT_s[p].full, 1)

                each_step(act, body)

            @block.tensor
            def _(pe):
                pe.wait_ge(loaded, LOADS)

                def body(it, more):
                    for p in range(2):
                        pe.wait_ge(norm.ready[p], it + 1)
                        transpose_chunks(nc, pe, plan.of("xT", p), bank, it, PS, norm.xn[:, p, :], ident, DC
                                         ).then_inc(norm.landed[p].free, 16)
                        pe.wait_ge(xT_s[p].full, xT_s[p].turn(it))
                        (b, k), = plan.of("h", p)
                        pe.wait_ge(bank[b].free, bank[b].turn(it, k))
                        for c in range(DC):
                            last = nc.tensor.matmul(PS[:, b, 0:ER + ROUTED], xT[:, p, c, :], wa[:, c, :],
                                                    start=(c == 0), stop=(c == DC - 1))
                        last.then_inc(bank[b].full, 1)
                        for i, (b, k) in enumerate(plan.of("y", p)):
                            pe.wait_ge(bank[b].free, bank[b].turn(it, k))
                            for c in range(DC):
                                nc.tensor.matmul(PS[:, b, :], xT[:, p, c, :], wb[:, c, i * BANK:(i + 1) * BANK],
                                                 start=(c == 0), stop=False)
                        pe.drain().then_inc(xT_s[p].free, 1)
                        pe.wait_ge(h_s[p].full, h_s[p].turn(it))
                        transpose_chunks(nc, pe, plan.of("hT", p), bank, it, PS, h[:, p, :], ident, 1).then_inc(h_s[p].free, 1)
                        pe.wait_ge(hT_s[p].full, hT_s[p].turn(it))
                        for i, (b, k) in enumerate(plan.of("y", p)):
                            nc.tensor.matmul(PS[:, b, :], hT[:, p, :], wlb[:, i * BANK:(i + 1) * BANK],
                                             start=False, stop=True).then_inc(bank[b].full, 1)
                        pe.drain().then_inc(hT_s[p].free, 1)

                each_step(pe, body)
        clear(nc, ctx)


def program(nc, d, out):
    xs = [d['x']] + [nc.dram_tensor(f'x{i}', (BATCHES * P, D), F32, kind='Internal').ap() for i in range(1, 6)] + [out]
    self_attention(nc, xs[0], xs[1], d['w_qkv'], d['w_o'], d['cos_sin'], d['causal'], d['eye'])
    window_attention(nc, xs[1], xs[2], d['ctx'], d['wx'], d['bx'], d['head_rows'], d['vrow'], d['band'], d['eye'])
    lora_mixture(nc, xs[2], xs[3], d['w_a'], d['w_b'], d['eye'])
    h = nc.dram_tensor('sparse_gate', (BATCHES * P, I), F32, kind='Internal').ap()
    u = nc.dram_tensor('up', (BATCHES * P, I), F32, kind='Internal').ap()
    with ExitStack() as ctx:
        weights = ctx.enter_context(nc.sbuf_tensor('ffn_weights', [P, DOWN_COLS], F32))
        wd_loaded = ctx.enter_context(nc.semaphore('wd_loaded'))
        sparse_gate(nc, xs[3], h, u, d['w_gate'], d['w_up'], d['w_down'], d['eye'], weights, wd_loaded)
        sparse_ffn(nc, xs[3], h, u, xs[4], d['eye'], weights, wd_loaded)
    autocorrelation(nc, xs[4], xs[5], d['ctx'], d['dft'], d['eye'])
    routed_linear(nc, xs[5], xs[6], d['w_base'], d['w_la'], d['w_lb'], d['b_base'], d['b_router'], d['eye'])



def dft_matrices():
    import numpy as np

    half = P // 2
    t = np.arange(P)

    def spectrum(size, freqs, pad):
        phase = -2.0 * np.pi * np.outer(np.arange(size), freqs) / size
        re, im = np.cos(phase), np.sin(phase)
        if pad:
            re[P - 1], im[P - 1] = re[P - 1:size - 1].sum(0), im[P - 1:size - 1].sum(0)
        return re[:P], im[:P]

    def block(size, freqs, ends, pad):
        re, im = spectrum(size, freqs, pad)
        a1, a2 = np.concatenate([re, im], 1), np.concatenate([im, -re], 1)
        re, im = spectrum(size, freqs, False)
        b1, b2 = np.concatenate([re, re], 1), np.concatenate([im, im], 1)
        if ends:
            a1[:, half] = spectrum(size, [size // 2], pad)[0][:, 0]
            b1[:, half] = spectrum(size, [size // 2], False)[0][:, 0]
            a2[:, half] = 0.0
            b2[:, half] = 0.0
        return a1, a2, b1, b2

    def inverse(size, freqs, ends):
        phase = 2.0 * np.pi * np.outer(freqs, t) / size
        out = np.concatenate([2.0 * np.cos(phase), -2.0 * np.sin(phase)], 0) / size
        if ends:
            out[0] /= 2.0
            out[half] = np.cos(np.pi * t) / size
        return out

    g = np.arange(half)
    q1, q2, k1, k2 = block(P, g, True, False)
    e1, e2, we1, we2 = block(2 * P, 2 * g, True, True)
    o1, o2, wo1, wo2 = block(2 * P, 2 * g + 1, False, True)
    mats = [q1, q2, k1, k2, e1, e2, o1, o2, we1, we2, wo1, wo2,
            inverse(P, g, True), inverse(2 * P, 2 * g, True), inverse(2 * P, 2 * g + 1, False)]
    return np.stack(mats, 1).astype(np.float32)


def layouts(inputs):
    import numpy as np

    a = {k: np.asarray(v) for k, v in inputs.items()}
    lay = {}
    wq = a["L0_attn_Wq"].reshape(2, 4, REP, HD, D).transpose(0, 2, 1, 3, 4).reshape(D, D)
    lay["w_qkv"] = np.concatenate([wq, a["L0_attn_Wk"], a["L0_attn_Wv"]], axis=0).T
    lay["w_o"] = a["L0_attn_Wo"].T
    inv = (1.0 / np.float32(10000.0) ** (np.arange(0, HD, 2, dtype=np.float32) / np.float32(HD))).astype(np.float32)
    freqs = np.outer(np.arange(P, dtype=np.float32), inv).astype(np.float32)
    cos, sin = np.cos(freqs), np.sin(freqs)
    lay["cos_sin"] = np.stack([np.concatenate([cos, cos], 1), np.concatenate([-sin, sin], 1)], 1).astype(np.float32)
    i = np.arange(P)
    lay["causal"] = np.where(i[:, None] < i[None, :], MASKED, 0.0).astype(np.float32)
    lay["eye"] = np.eye(P, dtype=np.float32)
    lay["x"] = a["x"].reshape(BATCHES * P, D)
    lay["ctx"] = a["ctx_4096"].reshape(BATCHES * P, D)
    lay["wx"] = np.stack([a["L0_xattn_W" + n].T for n in "qkvo"], 1)
    lay["bx"] = np.stack([a["L0_xattn_b" + n] for n in "qko"], 1)
    lay["head_rows"] = np.where(i[:, None] // X_HD == np.arange(X_HEADS)[None, :], X_HD ** -0.5, 0.0).astype(np.float32)
    ones = np.zeros(PADDED, np.float32)
    ones[LEFT:LEFT + D] = 1.0
    lay["vrow"] = np.concatenate([a["L0_xattn_bv"], ones])[None, :]
    past = np.arange(NK)[None, :] - i[:, None]
    lay["band"] = np.where((past >= 0) & (past < WINDOW), 0.0, MASKED).astype(np.float32)
    lay["w_a"] = np.concatenate([a["L0_ffn_A"].reshape(EXPERTS * RANK, D), a["L0_ffn_Wr"]], 0).T
    lay["w_b"] = a["L0_ffn_B"].transpose(0, 2, 1).reshape(EXPERTS * RANK, D)
    lay["w_gate"] = a["L1_attn_w_gate"].T
    lay["w_up"] = a["L1_attn_w_up"].T
    lay["w_down"] = a["L1_attn_w_down"].T
    lay["dft"] = dft_matrices()
    lay["w_base"] = a["L1_ffn_W_base"].T
    lay["w_la"] = np.concatenate([a["L1_ffn_lora_A"].transpose(1, 0, 2).reshape(D, ER), a["L1_ffn_W_router"].T], 1)
    lay["w_lb"] = a["L1_ffn_lora_B"].reshape(ER, D)
    lay["b_base"] = a["L1_ffn_b_base"][None, :]
    lay["b_router"] = a["L1_ffn_b_router"][None, :]
    return {k: np.ascontiguousarray(v) for k, v in lay.items()}


def kernel(**inputs):
    import concourse.bacc as bacc
    from concourse.bass_utils import run_bass_kernel_spmd as run

    nc = bacc.Bacc("TRN2", target_bir_lowering=False, num_devices=1, dynamic_dma_scratch_size=1024)
    lay = layouts(inputs)
    d = {k: nc.dram_tensor("in_" + k, v.shape, mybir.dt.from_np(v.dtype), kind="ExternalInput").ap() for k, v in lay.items()}
    out = nc.dram_tensor("out_x", (BATCHES * P, D), F32, kind="ExternalOutput").ap()
    program(nc, d, out)
    r = run(nc, [{"in_" + k: v for k, v in lay.items()}], core_ids=[0])
    return r.results[0]["out_x"].reshape(BATCHES, P, D)
```
